# Optimizing a Trainium2 kernel written in Bass

```python
import numpy as np
import jax
import jax.numpy as jnp

def _softmax(x, axis=-1):
    return jax.nn.softmax(x, axis=axis)

def _gelu(x):
    return jax.nn.gelu(x, approximate=True)

def _silu(x):
    return jax.nn.silu(x)

def _sigmoid(x):
    return jax.nn.sigmoid(x)

def _layernorm(x, axis=-1, eps=1e-05):
    m = jnp.mean(x, axis=axis, keepdims=True)
    v = jnp.var(x, axis=axis, keepdims=True)
    return (x - m) / jnp.sqrt(v + eps)

def _scatter_add(tgt, idx, src, axis=0):
    return tgt.at[idx].add(src)

def _segment_sum(src, seg, n):
    return jax.ops.segment_sum(src, seg, n)
kernel_name = 'mk_flamingo_gated_d2_seqx_r4_16bfaa'

def setup_inputs(seed: int=0):
    np.random.seed(seed)
    _w = jnp.asarray

    def _rec_inputs():
        import jax
        import jax.numpy as jnp
        _rk = jax.random.key(seed)
        x = 7.22e-05 + 1 * jax.random.normal(jax.random.fold_in(_rk, 1), (8, 256, 512), jnp.float32)
        _lenS = 256 - jax.random.randint(jax.random.fold_in(_rk, 7), (8,), 0, max(1, 256 // 4) + 1, jnp.int32)
        _lenS2 = 256 - jax.random.randint(jax.random.fold_in(_rk, 8), (8,), 0, max(1, 256 // 4) + 1, jnp.int32)
        _ctx_1024P = jax.random.normal(jax.random.fold_in(_rk, 11), (8, 16, 256), jnp.float32)
        _ctx_1024c = jax.random.dirichlet(jax.random.fold_in(_rk, 511), 0.3 * jnp.ones((16,), jnp.float32), (8, 256))
        _ctx_1024t = jnp.einsum('bsk,bkd->bsd', _ctx_1024c, _ctx_1024P)
        _ctx_1024t = _ctx_1024t * jax.lax.rsqrt(jnp.mean(jnp.square(_ctx_1024t)) + 1e-12) * 0.953939
        ctx_1024 = -1.39393e-06 + 0.999914 * (_ctx_1024t + 0.3 * jax.random.normal(jax.random.fold_in(_rk, 611), (8, 256, 256), jnp.float32))
        fside_BxSx2_0 = jax.random.uniform(jax.random.fold_in(_rk, 12), (8, 256, 2), jnp.float32, 0.0, 0.999707)
        _g = jax.random.normal(jax.random.fold_in(_rk, 9001), (2, 2), jnp.float32)
        _g = jnp.sign(_g) * jnp.maximum(jnp.abs(_g), 1.0) + (_g == 0) * 1.0
        g_xattn = _g[0]
        g_ffn = _g[1]
        return (x, ctx_1024, fside_BxSx2_0, g_xattn, g_ffn)
    x, ctx_1024, fside_BxSx2_0, g_xattn, g_ffn = _rec_inputs()

    def _L0_xattn_setup():
        import jax, jax.numpy as jnp
        import numpy as np
        DIM = 512
        CTX_DIM = 256
        N_HEADS = 32
        HEAD_DIM = DIM // N_HEADS
        POS_DIM = 2
        B, N, CTXN = (2, 512, 512)
        ROPE_BASE = 10000.0

        def apply_axial_rope(x, pos):
            b, n, h, d = x.shape
            p = pos.shape[-1]
            dpa = d // p
            half = dpa // 2
            freqs = ROPE_BASE ** (-jnp.arange(half, dtype=x.dtype) / half)
            ang = pos[..., :, None] * freqs
            cos = jnp.cos(ang)[:, :, None, :, :]
            sin = jnp.sin(ang)[:, :, None, :, :]
            xr = x.reshape(b, n, h, p, half, 2)
            x1, x2 = (xr[..., 0], xr[..., 1])
            out = jnp.stack([x1 * cos - x2 * sin, x1 * sin + x2 * cos], axis=-1)
            return out.reshape(b, n, h, d)
        key = jax.random.key(seed)
        ks = jax.random.split(key, 8)
        x = jax.random.normal(ks[0], (B, N, DIM), jnp.float32)
        ctx = jax.random.normal(ks[1], (B, CTXN, CTX_DIM), jnp.float32)
        pos_map = jax.random.uniform(ks[2], (B, N, POS_DIM), jnp.float32)
        ctx_pos_map = jax.random.uniform(ks[3], (B, CTXN, POS_DIM), jnp.float32)
        Wq = jax.random.normal(ks[4], (DIM, DIM), jnp.float32) / np.sqrt(DIM)
        Wkv = jax.random.normal(ks[5], (CTX_DIM, 2 * DIM), jnp.float32) / np.sqrt(CTX_DIM)
        Wout = jax.random.normal(ks[6], (DIM, DIM), jnp.float32) / np.sqrt(DIM)
        bout = jnp.zeros((DIM,), jnp.float32)
        return {'x': x, 'ctx': ctx, 'pos_map': pos_map, 'ctx_pos_map': ctx_pos_map, 'Wq': Wq, 'Wkv': Wkv, 'Wout': Wout, 'bout': bout}
    _L0_xattn_all = _L0_xattn_setup()
    _L0_xattn_in = {k: v for k, v in _L0_xattn_all.items() if k in ('Wq', 'Wkv', 'Wout', 'bout')}
    del _L0_xattn_all

    def _L0_ffn_setup():
        import jax, jax.numpy as jnp
        import numpy as np
        H = 512
        E = 16
        K = 4
        I = 352
        SH_I = 2 * I
        B, S = (1, 256)
        key = jax.random.key(seed)
        ks = jax.random.split(key, 9)
        sc_h = 1.0 / np.sqrt(H)
        sc_i = 1.0 / np.sqrt(I)
        return {'hidden_states': jax.random.normal(ks[0], (B, S, H), dtype=jnp.float32), 'w_gate': jax.random.normal(ks[1], (E, H), dtype=jnp.float32) * sc_h, 'wg': jax.random.normal(ks[2], (E, H, I), dtype=jnp.float32) * sc_h, 'wu': jax.random.normal(ks[3], (E, H, I), dtype=jnp.float32) * sc_h, 'wd': jax.random.normal(ks[4], (E, I, H), dtype=jnp.float32) * sc_i, 'sg': jax.random.normal(ks[5], (H, SH_I), dtype=jnp.float32) * sc_h, 'su': jax.random.normal(ks[6], (H, SH_I), dtype=jnp.float32) * sc_h, 'sd': jax.random.normal(ks[7], (SH_I, H), dtype=jnp.float32) * (1.0 / np.sqrt(SH_I))}
    _L0_ffn_all = _L0_ffn_setup()
    _L0_ffn_in = {k: v for k, v in _L0_ffn_all.items() if k in ('w_gate', 'wg', 'wu', 'wd', 'sg', 'su', 'sd')}
    del _L0_ffn_all

    def _L1_xattn_setup():
        import jax, jax.numpy as jnp
        import numpy as np
        B, S1, S2, DCA = (2, 512, 256, 16)
        QDIM, KDIM, H = (512, 256, 16)
        HD = QDIM // H
        SCALE = HD ** (-0.5)
        EPS = 1e-06
        DCA_WEIGHT = 1.0

        def _ln(t, w, b):
            m = jnp.mean(t, axis=-1, keepdims=True)
            v = jnp.var(t, axis=-1, keepdims=True)
            return (t - m) * jax.lax.rsqrt(v + EPS) * w + b

        def _attn(q, k, v):
            s = jnp.einsum('bhqd,bhkd->bhqk', q, k) * SCALE
            p = jax.nn.softmax(s, axis=-1)
            return jnp.einsum('bhqk,bhkd->bhqd', p, v)
        key = jax.random.key(seed)
        ks = jax.random.split(key, 8)
        w = lambda k, shape: jax.random.normal(k, shape, jnp.float32) * 0.02
        return {'x': jax.random.normal(ks[0], (B, S1, QDIM), jnp.float32), 'y': jax.random.normal(ks[1], (B, S2 + DCA, KDIM), jnp.float32), 'Wq': w(ks[2], (QDIM, QDIM)), 'bq': jnp.zeros((QDIM,), jnp.float32), 'Wk': w(ks[3], (KDIM, QDIM)), 'bk': jnp.zeros((QDIM,), jnp.float32), 'Wv': w(ks[4], (KDIM, QDIM)), 'bv': jnp.zeros((QDIM,), jnp.float32), 'Wkv_dca': w(ks[5], (KDIM, 2 * QDIM)), 'bkv_dca': jnp.zeros((2 * QDIM,), jnp.float32), 'qn_w': jnp.ones((HD,), jnp.float32), 'qn_b': jnp.zeros((HD,), jnp.float32), 'kn_w': jnp.ones((HD,), jnp.float32), 'kn_b': jnp.zeros((HD,), jnp.float32), 'kn_dca_w': jnp.ones((HD,), jnp.float32), 'kn_dca_b': jnp.zeros((HD,), jnp.float32), 'Wo': w(ks[6], (QDIM, QDIM)), 'bo': jnp.zeros((QDIM,), jnp.float32)}
    _L1_xattn_all = _L1_xattn_setup()
    _L1_xattn_in = {k: v for k, v in _L1_xattn_all.items() if k in ('Wq', 'bq', 'Wk', 'bk', 'Wv', 'bv', 'Wkv_dca', 'bkv_dca', 'qn_w', 'qn_b', 'kn_w', 'kn_b', 'kn_dca_w', 'kn_dca_b', 'Wo', 'bo')}
    del _L1_xattn_all

    def _L1_ffn_setup():
        import jax, jax.numpy as jnp
        import numpy as np
        TOP_K = 2
        key = jax.random.key(seed)
        ks = jax.random.split(key, 7)
        B, S, H = (2, 512, 512)
        E, A, NS = (8, 64, 4096)
        x = jax.random.normal(ks[0], (B, S, H), jnp.float32)
        gate_w = jax.random.normal(ks[1], (E, H), jnp.float32) * 0.01
        W = jax.random.normal(ks[2], (H, H), jnp.float32) * 0.02
        atoms = jax.random.normal(ks[3], (A, NS), jnp.float32) * 0.02
        expert_atom_weights = jax.random.normal(ks[4], (E, A), jnp.float32) * 0.1
        importance = jax.random.normal(ks[5], (E, NS), jnp.float32) * 0.1
        mask_idx = jax.random.randint(ks[6], (NS,), 0, H * H, jnp.int32)
        return dict(x=x, gate_w=gate_w, W=W, atoms=atoms, expert_atom_weights=expert_atom_weights, importance=importance, mask_idx=mask_idx)
    _L1_ffn_all = _L1_ffn_setup()
    _L1_ffn_in = {k: v for k, v in _L1_ffn_all.items() if k in ('gate_w', 'W', 'atoms', 'expert_atom_weights', 'importance', 'mask_idx')}
    del _L1_ffn_all
    return {'x': x, 'ctx_1024': ctx_1024, 'fside_BxSx2_0': fside_BxSx2_0, 'g_xattn': g_xattn, 'g_ffn': g_ffn, 'L0_xattn_Wq': _L0_xattn_in['Wq'], 'L0_xattn_Wkv': _L0_xattn_in['Wkv'], 'L0_xattn_Wout': _L0_xattn_in['Wout'], 'L0_xattn_bout': _L0_xattn_in['bout'], 'L0_ffn_w_gate': _L0_ffn_in['w_gate'], 'L0_ffn_wg': _L0_ffn_in['wg'], 'L0_ffn_wu': _L0_ffn_in['wu'], 'L0_ffn_wd': _L0_ffn_in['wd'], 'L0_ffn_sg': _L0_ffn_in['sg'], 'L0_ffn_su': _L0_ffn_in['su'], 'L0_ffn_sd': _L0_ffn_in['sd'], 'L1_xattn_Wq': _L1_xattn_in['Wq'], 'L1_xattn_bq': _L1_xattn_in['bq'], 'L1_xattn_Wk': _L1_xattn_in['Wk'], 'L1_xattn_bk': _L1_xattn_in['bk'], 'L1_xattn_Wv': _L1_xattn_in['Wv'], 'L1_xattn_bv': _L1_xattn_in['bv'], 'L1_xattn_Wkv_dca': _L1_xattn_in['Wkv_dca'], 'L1_xattn_bkv_dca': _L1_xattn_in['bkv_dca'], 'L1_xattn_qn_w': _L1_xattn_in['qn_w'], 'L1_xattn_qn_b': _L1_xattn_in['qn_b'], 'L1_xattn_kn_w': _L1_xattn_in['kn_w'], 'L1_xattn_kn_b': _L1_xattn_in['kn_b'], 'L1_xattn_kn_dca_w': _L1_xattn_in['kn_dca_w'], 'L1_xattn_kn_dca_b': _L1_xattn_in['kn_dca_b'], 'L1_xattn_Wo': _L1_xattn_in['Wo'], 'L1_xattn_bo': _L1_xattn_in['bo'], 'L1_ffn_gate_w': _L1_ffn_in['gate_w'], 'L1_ffn_W': _L1_ffn_in['W'], 'L1_ffn_atoms': _L1_ffn_in['atoms'], 'L1_ffn_expert_atom_weights': _L1_ffn_in['expert_atom_weights'], 'L1_ffn_importance': _L1_ffn_in['importance'], 'L1_ffn_mask_idx': _L1_ffn_in['mask_idx']}

def reference(x, ctx_1024, fside_BxSx2_0, g_xattn, g_ffn, L0_xattn_Wq, L0_xattn_Wkv, L0_xattn_Wout, L0_xattn_bout, L0_ffn_w_gate, L0_ffn_wg, L0_ffn_wu, L0_ffn_wd, L0_ffn_sg, L0_ffn_su, L0_ffn_sd, L1_xattn_Wq, L1_xattn_bq, L1_xattn_Wk, L1_xattn_bk, L1_xattn_Wv, L1_xattn_bv, L1_xattn_Wkv_dca, L1_xattn_bkv_dca, L1_xattn_qn_w, L1_xattn_qn_b, L1_xattn_kn_w, L1_xattn_kn_b, L1_xattn_kn_dca_w, L1_xattn_kn_dca_b, L1_xattn_Wo, L1_xattn_bo, L1_ffn_gate_w, L1_ffn_W, L1_ffn_atoms, L1_ffn_expert_atom_weights, L1_ffn_importance, L1_ffn_mask_idx):
    import jax
    import jax.numpy as jnp

    def _L0_xattn_ref(x, ctx, pos_map, ctx_pos_map, Wq, Wkv, Wout, bout):
        import jax, jax.numpy as jnp
        import numpy as np
        DIM = 512
        CTX_DIM = 256
        N_HEADS = 32
        HEAD_DIM = DIM // N_HEADS
        POS_DIM = 2
        B, N, CTXN = (2, 512, 512)
        ROPE_BASE = 10000.0

        def apply_axial_rope(x, pos):
            b, n, h, d = x.shape
            p = pos.shape[-1]
            dpa = d // p
            half = dpa // 2
            freqs = ROPE_BASE ** (-jnp.arange(half, dtype=x.dtype) / half)
            ang = pos[..., :, None] * freqs
            cos = jnp.cos(ang)[:, :, None, :, :]
            sin = jnp.sin(ang)[:, :, None, :, :]
            xr = x.reshape(b, n, h, p, half, 2)
            x1, x2 = (xr[..., 0], xr[..., 1])
            out = jnp.stack([x1 * cos - x2 * sin, x1 * sin + x2 * cos], axis=-1)
            return out.reshape(b, n, h, d)
        b, n, _ = x.shape
        ctx_n = ctx.shape[1]
        q = (x @ Wq).reshape(b, n, N_HEADS, HEAD_DIM)
        k, v = jnp.split(ctx @ Wkv, 2, axis=-1)
        k = k.reshape(b, ctx_n, N_HEADS, HEAD_DIM)
        v = v.reshape(b, ctx_n, N_HEADS, HEAD_DIM)
        q = apply_axial_rope(q, pos_map)
        k = apply_axial_rope(k, ctx_pos_map)
        scale = 1.0 / np.sqrt(HEAD_DIM).astype(np.float32)
        logits = jnp.einsum('bqhd,bkhd->bhqk', q, k) * scale
        w = jax.nn.softmax(logits, axis=-1)
        attn = jnp.einsum('bhqk,bkhd->bqhd', w, v)
        attn = attn.reshape(b, n, N_HEADS * HEAD_DIM)
        return attn @ Wout + bout

    def _L0_ffn_ref(hidden_states, w_gate, wg, wu, wd, sg, su, sd):
        import jax, jax.numpy as jnp
        import numpy as np
        H = 512
        E = 16
        K = 4
        I = 352
        SH_I = 2 * I
        B, S = (1, 256)
        b, s, h = hidden_states.shape
        x = hidden_states.reshape(-1, h)
        T = x.shape[0]
        logits = x @ w_gate.T
        probs = jax.nn.softmax(logits.astype(jnp.float32), axis=-1)
        top_w, top_i = jax.lax.top_k(probs, K)
        routing_weight = jnp.zeros((T, E), dtype=probs.dtype)
        routing_weight = routing_weight.at[jnp.arange(T)[:, None], top_i].add(top_w)
        g = jnp.einsum('th,ehi->tei', x, wg)
        u = jnp.einsum('th,ehi->tei', x, wu)
        act = jax.nn.silu(g) * u
        routed = jnp.einsum('te,tei,eih->th', routing_weight, act, wd)
        shared = jax.nn.silu(x @ sg) * (x @ su) @ sd
        out = (routed + shared).astype(hidden_states.dtype)
        return out.reshape(b, s, h)

    def _L1_xattn_ref(x, y, Wq, bq, Wk, bk, Wv, bv, Wkv_dca, bkv_dca, qn_w, qn_b, kn_w, kn_b, kn_dca_w, kn_dca_b, Wo, bo):
        import jax, jax.numpy as jnp
        import numpy as np
        B, S1, S2, DCA = (2, 512, 256, 16)
        QDIM, KDIM, H = (512, 256, 16)
        HD = QDIM // H
        SCALE = HD ** (-0.5)
        EPS = 1e-06
        DCA_WEIGHT = 1.0

        def _ln(t, w, b):
            m = jnp.mean(t, axis=-1, keepdims=True)
            v = jnp.var(t, axis=-1, keepdims=True)
            return (t - m) * jax.lax.rsqrt(v + EPS) * w + b

        def _attn(q, k, v):
            s = jnp.einsum('bhqd,bhkd->bhqk', q, k) * SCALE
            p = jax.nn.softmax(s, axis=-1)
            return jnp.einsum('bhqk,bhkd->bhqd', p, v)
        b, s1, _ = x.shape
        y_dca = y[:, -DCA:, :]
        y_main = y[:, :-DCA, :]
        kv_dca = (y_dca @ Wkv_dca + bkv_dca).reshape(b, DCA, 2, H, HD)
        k_dca = _ln(kv_dca[:, :, 0], kn_dca_w, kn_dca_b)
        v_dca = kv_dca[:, :, 1]
        s2 = y_main.shape[1]
        q = _ln((x @ Wq + bq).reshape(b, s1, H, HD), qn_w, qn_b)
        kv = jnp.concatenate([y_main @ Wk + bk, y_main @ Wv + bv], axis=-1)
        kv = kv.reshape(b, s2, H, 2 * HD)
        k = _ln(kv[..., :HD], kn_w, kn_b)
        v = kv[..., HD:]
        qT = q.transpose(0, 2, 1, 3)
        ctx = _attn(qT, k.transpose(0, 2, 1, 3), v.transpose(0, 2, 1, 3))
        ctx = ctx.transpose(0, 2, 1, 3).reshape(b, s1, QDIM)
        ctx_dca = _attn(qT, k_dca.transpose(0, 2, 1, 3), v_dca.transpose(0, 2, 1, 3))
        ctx_dca = ctx_dca.transpose(0, 2, 1, 3).reshape(b, s1, QDIM)
        ctx = ctx + DCA_WEIGHT * ctx_dca
        return ctx @ Wo + bo

    def _L1_ffn_ref(x, gate_w, W, atoms, expert_atom_weights, importance, mask_idx):
        import jax, jax.numpy as jnp
        import numpy as np
        TOP_K = 2
        B, S, H = x.shape
        xt = x.reshape(-1, H)
        logits = jnp.clip(xt @ gate_w.T, -50.0, 50.0)
        top_w, top_idx = jax.lax.top_k(logits, TOP_K)
        rw = jax.nn.softmax(top_w, axis=-1)
        deltas = jax.nn.softmax(expert_atom_weights, axis=-1) @ atoms
        weighted = deltas * jax.nn.sigmoid(importance)
        rows = mask_idx // H
        cols = mask_idx % H
        vals = jnp.einsum('tk,tks->ts', rw, weighted[top_idx])
        xg = xt[:, cols]
        contrib = jax.ops.segment_sum((xg * vals).T, rows, num_segments=H)
        out = xt @ W.T + contrib.T
        return out.reshape(B, S, H)
    x = x + jnp.tanh(g_xattn[0]) * _L0_xattn_ref(_layernorm(x, axis=-1), ctx_1024, fside_BxSx2_0, fside_BxSx2_0, L0_xattn_Wq, L0_xattn_Wkv, L0_xattn_Wout, L0_xattn_bout)
    x = x + jnp.tanh(g_ffn[0]) * _L0_ffn_ref(_layernorm(x, axis=-1), L0_ffn_w_gate, L0_ffn_wg, L0_ffn_wu, L0_ffn_wd, L0_ffn_sg, L0_ffn_su, L0_ffn_sd)
    x = x + jnp.tanh(g_xattn[1]) * _L1_xattn_ref(_layernorm(x, axis=-1), ctx_1024, L1_xattn_Wq, L1_xattn_bq, L1_xattn_Wk, L1_xattn_bk, L1_xattn_Wv, L1_xattn_bv, L1_xattn_Wkv_dca, L1_xattn_bkv_dca, L1_xattn_qn_w, L1_xattn_qn_b, L1_xattn_kn_w, L1_xattn_kn_b, L1_xattn_kn_dca_w, L1_xattn_kn_dca_b, L1_xattn_Wo, L1_xattn_bo)
    x = x + jnp.tanh(g_ffn[1]) * _L1_ffn_ref(_layernorm(x, axis=-1), L1_ffn_gate_w, L1_ffn_W, L1_ffn_atoms, L1_ffn_expert_atom_weights, L1_ffn_importance, L1_ffn_mask_idx)
    return x

_drawn_inputs = setup_inputs


def setup_inputs(seed=0):
    import zlib

    import numpy as np

    out = dict(_drawn_inputs(seed))
    spreads = {'g_ffn': (-1.0, 0.6),
     'L0_xattn_bout': (0.0, 0.1),
     'L1_xattn_bq': (0.0, 0.8),
     'L1_xattn_bk': (0.0, 0.322),
     'L1_xattn_bv': (0.0, 0.315),
     'L1_xattn_bkv_dca': (0.0, 0.1),
     'L1_xattn_qn_w': (1.0, 0.6),
     'L1_xattn_qn_b': (0.0, 0.8),
     'L1_xattn_kn_w': (1.0, 0.6),
     'L1_xattn_kn_b': (0.0, 2.0),
     'L1_xattn_kn_dca_w': (1.0, 0.6),
     'L1_xattn_kn_dca_b': (0.0, 2.0),
     'L1_xattn_bo': (0.0, 0.1)}
    factors = {'L1_ffn_gate_w': 26.819,
     'L1_ffn_atoms': 8.0,
     'L1_ffn_expert_atom_weights': 24.247,
     'L1_ffn_importance': 53.378}
    for name, (base, spread) in spreads.items():
        noise = np.random.default_rng([zlib.crc32(name.encode()), seed]).standard_normal(out[name].shape)
        drawn = base * np.exp(spread * noise) if base else spread * noise
        out[name] = jnp.asarray(drawn.astype(out[name].dtype))
    for name, factor in factors.items():
        out[name] = (out[name] * factor).astype(out[name].dtype)
    return out
```

```python
from contextlib import ExitStack

import numpy as np
import concourse.bass as bass
from concourse import mybir

F32 = mybir.dt.float32
F32R = mybir.dt.float32r
BF16 = mybir.dt.bfloat16
I32 = mybir.dt.int32
U32 = mybir.dt.uint32
ALU = mybir.AluOpType
ACT = mybir.ActivationFunctionType
AX = mybir.AxisListType

P = 128
D = 512
KD = D // P
CD = 256
KC = CD // P
B = 8
S = 256
T = B * S
NT = T // P
BT = S // P


class Count:

    def __init__(self, base=0, step=1):
        self.base, self.step, self.n = base, step, 0

    def inc(self, k=1):
        self.n += k
        return k * self.step

    @property
    def now(self):
        return self.base + self.n * self.step if self.n else self.base


class Ring:

    def __init__(self, filled, freed, items):
        assert items % len(filled) == 0
        self.filled, self.freed, self.k, self.per = filled, freed, len(filled), items // len(filled)
        self.items = items

    def until_free(self, it, j):
        assert j < self.items
        return self.freed[j % self.k], it * self.per + j // self.k + 1

    def until_filled(self, it, j):
        assert j < self.items
        return self.filled[j % self.k], it * self.per + j // self.k + 1

    def until_freed(self, it, j):
        assert j < self.items
        return self.freed[j % self.k], it * self.per + j // self.k + 2


def semaphores(nc, ctx, prefix):
    taken = []

    def clear():
        nc.clear_and_free_semaphores(taken)
        nc.all_engine_barrier()
    ctx.callback(clear)

    def sem(name):
        taken.append(nc.alloc_semaphore(prefix + name))
        return taken[-1]
    return sem


def r32(ap):
    return ap.bitcast(F32)


def rsqrt_steps(eng, sem, c, v, y, a, h):
    eng.wait_ge(sem, c.now)
    eng.tensor_scalar(a.bitcast(I32), v.bitcast(I32), 1, None, ALU.arith_shift_right).then_inc(sem, c.inc())
    eng.tensor_scalar(h, v, -0.5, None, ALU.mult).then_inc(sem, c.inc())
    eng.wait_ge(sem, c.now)
    eng.tensor_scalar(y.bitcast(I32), a.bitcast(I32), -1.0, float(0x5F3759DF), ALU.mult, ALU.add).then_inc(sem, c.inc())
    for _ in range(3):
        eng.wait_ge(sem, c.now)
        eng.tensor_tensor(a, y, y, ALU.mult).then_inc(sem, c.inc())
        eng.wait_ge(sem, c.now)
        eng.tensor_tensor(a, a, h, ALU.mult).then_inc(sem, c.inc())
        eng.wait_ge(sem, c.now)
        eng.scalar_tensor_tensor(out=y, in0=a, scalar=1.5, in1=y, op0=ALU.add, op1=ALU.mult).then_inc(sem, c.inc())


def layer_norm_scales(eng, sem, c, x, st, w, out):
    for t in range(NT):
        eng.bn_stats(st[:, t, :], x[:, t, :]).then_inc(sem, c.inc())
    eng.wait_ge(sem, c.now)
    eng.tensor_tensor(w[:, 0, :], st[:, :, 2], st[:, :, 5], ALU.add).then_inc(sem, c.inc())
    eng.tensor_tensor(w[:, 1, :], st[:, :, 1], st[:, :, 4], ALU.subtract).then_inc(sem, c.inc())
    eng.tensor_tensor(w[:, 2, :], st[:, :, 1], st[:, :, 4], ALU.add).then_inc(sem, c.inc())
    eng.wait_ge(sem, c.now)
    eng.scalar_tensor_tensor(out=w[:, 1, :], in0=w[:, 1, :], scalar=0.25, in1=w[:, 1, :],
                             op0=ALU.mult, op1=ALU.mult).then_inc(sem, c.inc())
    eng.wait_ge(sem, c.now)
    eng.scalar_tensor_tensor(out=w[:, 0, :], in0=w[:, 0, :], scalar=1.0 / D, in1=w[:, 1, :],
                             op0=ALU.mult, op1=ALU.add).then_inc(sem, c.inc())
    eng.wait_ge(sem, c.now)
    eng.tensor_scalar(w[:, 0, :], w[:, 0, :], 1e-5, None, ALU.add).then_inc(sem, c.inc())
    rsqrt_steps(eng, sem, c, w[:, 0, :], w[:, 3, :], w[:, 1, :], w[:, 4, :])
    eng.wait_ge(sem, c.now)
    eng.tensor_copy(out[:, :, 0], w[:, 3, :]).then_inc(sem, c.inc())
    eng.scalar_tensor_tensor(out=out[:, :, 1], in0=w[:, 2, :], scalar=-0.5, in1=w[:, 3, :],
                             op0=ALU.mult, op1=ALU.mult).then_inc(sem, c.inc())


class Core:
    pass


def setup(nc, core, x, g_xattn, g_ffn):
    with ExitStack() as ctx:
        graw = ctx.enter_context(nc.sbuf_tensor("graw", [P, 4], F32))
        sem = semaphores(nc, ctx, "su_")
        loaded, zeroed = sem("loaded"), sem("zeroed")
        block = ctx.enter_context(nc.Block())

        @block.sync
        def _(eng):
            eng.dma_start(graw[:, 0:2], g_xattn.partition_broadcast(P)).then_inc(loaded, 16)
            eng.dma_start(graw[:, 2:4], g_ffn.partition_broadcast(P)).then_inc(loaded, 16)
            xf = x.rearrange("b (t p) d -> p (b t) d", p=P)
            for h in range(4):
                eng.dma_start(core.X[:, 4 * h:4 * h + 4, :], xf[:, 4 * h:4 * h + 4, :]).then_inc(loaded, 16)
            eng.wait_ge(loaded, 6 * 16)

        @block.gpsimd
        def _(eng):
            eng.memset(core.ident[:, :], 0.0).then_inc(zeroed, 1)
            eng.wait_ge(zeroed, 1)
            eng.affine_select(out=core.ident[:, :], in_=core.ident[:, :], compare_op=ALU.not_equal, fill=1.0,
                              base=0, pattern=[[-1, P]], channel_multiplier=1)

        @block.scalar
        def _(eng):
            eng.wait_ge(loaded, 6 * 16)
            eng.activation(core.gates[:, :], graw[:, :], ACT.Tanh)


def split_weights(nc, name, parts):
    with ExitStack() as ctx:
        sem = semaphores(nc, ctx, name)
        loaded, hi_done, free = sem("_loaded"), sem("_hi"), sem("_free")
        n = max(a.shape[1] * a.shape[2] for a, _, _ in parts)
        raw = ctx.enter_context(nc.sbuf_tensor(name + "_raw", [P, 2, n], F32))
        block = ctx.enter_context(nc.Block())

        def views(i):
            a, hi, lo = parts[i]
            k, m = a.shape[1], a.shape[2]
            return a, hi, lo, raw[:, i % 2, 0:k * m].rearrange("p (k m) -> p k m", k=k)

        @block.sync
        def _(eng):
            for i in range(len(parts)):
                a, _, _, r = views(i)
                if i >= 2:
                    eng.wait_ge(free, i - 1)
                eng.dma_start(r, a).then_inc(loaded, 16)
                eng.wait_ge(loaded, 16 * (i + 1))

        @block.scalar
        def _(eng):
            for i in range(len(parts)):
                _, hi, _, r = views(i)
                eng.wait_ge(loaded, 16 * (i + 1))
                eng.activation(hi, r, ACT.Copy).then_inc(hi_done, 1)

        @block.vector
        def _(eng):
            for i in range(len(parts)):
                _, hi, lo, r = views(i)
                eng.wait_ge(hi_done, i + 1)
                eng.tensor_tensor(lo, r, r32(hi), ALU.subtract).then_inc(free, 1)


def rope_tables(nc, core, pos, CS):
    HALF = 4
    n = NT * 2 * HALF
    TWO_PI = 2 * np.pi
    HI = float(np.float32(6.28125))
    LO = float(np.float32(TWO_PI - 6.28125))
    MAGIC = float(1.5 * 2 ** 23)
    with ExitStack() as ctx:
        sb = lambda name, shape, dt=F32: ctx.enter_context(nc.sbuf_tensor(name, shape, dt))
        ps = sb("rt_pos", [P, NT, 2])
        ang = sb("rt_ang", [P, 2, NT, 2, HALF])
        turns = sb("rt_turns", [P, 2, NT, 2, HALF])
        sn = sb("rt_sin", [P, 2, NT, 2, HALF])
        sem = semaphores(nc, ctx, "rt_")
        loaded, vdone, sdone = sem("loaded"), sem("vdone"), sem("sdone")
        block = ctx.enter_context(nc.Block())
        c = Count()
        angles_ready = 2 * HALF // 2 + 1 + 6

        @block.sync
        def _(eng):
            eng.dma_start(ps[:, :, :], pos.rearrange("b (t p) c -> p (b t) c", p=P)).then_inc(loaded, 16)

        @block.vector
        def _(eng):
            eng.wait_ge(loaded, 16)
            for i in range(HALF):
                f = float(np.float32(10000.0) ** np.float32(-i / HALF))
                eng.tensor_scalar(ang[:, 0, :, :, i], ps[:, :, :], f, None, ALU.mult).then_inc(vdone, c.inc())
            eng.wait_ge(vdone, c.now)
            eng.tensor_scalar(ang[:, 1], ang[:, 0], float(np.pi / 2), None, ALU.add).then_inc(vdone, c.inc())
            eng.wait_ge(vdone, c.now)
            flat = lambda a: a[:, :, :, :, :].rearrange("p a t c h -> p (a t c h)")
            A, U = flat(ang), flat(turns)
            eng.tensor_scalar(U, A, float(1 / TWO_PI), None, ALU.mult).then_inc(vdone, c.inc())
            eng.wait_ge(vdone, c.now)
            eng.tensor_scalar(U, U, MAGIC, None, ALU.add).then_inc(vdone, c.inc())
            eng.wait_ge(vdone, c.now)
            eng.tensor_scalar(U, U, -MAGIC, None, ALU.add).then_inc(vdone, c.inc())
            eng.wait_ge(vdone, c.now)
            eng.scalar_tensor_tensor(out=A, in0=U, scalar=-HI, in1=A, op0=ALU.mult, op1=ALU.add).then_inc(vdone, c.inc())
            eng.wait_ge(vdone, c.now)
            eng.scalar_tensor_tensor(out=A, in0=U, scalar=-LO, in1=A, op0=ALU.mult, op1=ALU.add).then_inc(vdone, c.inc())
            eng.wait_ge(vdone, c.now)
            PI = 3.1415925
            eng.tensor_scalar(A, A, PI, -PI, ALU.min, ALU.max).then_inc(vdone, c.inc())
            assert c.now == angles_ready
            eng.wait_ge(sdone, 1)
            cs = CS[:, :, :, :].rearrange("p t c (a i) -> p t c a i", i=2)
            both = lambda k: sn[:, k].rearrange("p t c h -> p t (c h)")
            for i in range(2):
                eng.tensor_copy(cs[:, :, 0, :, i], both(1)).then_inc(vdone, c.inc())
                eng.tensor_scalar(cs[:, :, 1, :, i], both(0), -1.0 if i == 0 else 1.0, None,
                                  ALU.mult).then_inc(vdone, c.inc())

        @block.scalar
        def _(eng):
            eng.wait_ge(vdone, angles_ready)
            eng.activation(sn[:, :, :, :, :].rearrange("p a t c h -> p (a t c h)"),
                           ang[:, :, :, :, :].rearrange("p a t c h -> p (a t c h)"), ACT.Sin).then_inc(sdone, 1)


def rope_attention(nc, core, ctx_d, pos, Wq, Wkv, Wout, bout, gate):
    H, HD = 32, 16
    R = 64
    HI_HI, HI_LO, LO_HI, MAXROW = 0, HD, 2 * HD, 3 * HD
    PAIRS = H // 2
    GH = 8
    NG = H // GH
    QH = 4
    NQ = H // QH
    SCALE = 1.0 / HD ** 0.5

    with ExitStack() as ctx:
        sb = lambda name, shape, dt=F32: ctx.enter_context(nc.sbuf_tensor(name, shape, dt))
        sem = semaphores(nc, ctx, "")
        wq = [sb(f"a_wq{i}", [P, KD, D], F32R) for i in range(2)]
        wkv = [sb(f"a_wkv{i}", [P, KC, 2 * D], F32R) for i in range(2)]
        wo = [sb(f"a_wo{i}", [P, KD, D], F32R) for i in range(2)]
        CS = sb("a_cs", [P, NT, 2, 2 * 8])
        lnsc = sb("a_lnsc", [P, NT, 2])
        split_weights(nc, "a_w", [
            (Wq.rearrange("(k p) n -> p k n", p=P), wq[0][:, :, :], wq[1][:, :, :]),
            (Wkv.rearrange("(k p) n -> p k n", p=P), wkv[0][:, :, :], wkv[1][:, :, :]),
            (Wout.rearrange("(k p) n -> p k n", p=P), wo[0][:, :, :], wo[1][:, :, :])])
        rope_tables(nc, core, pos, CS)

        bo = sb("a_bo", [P, D])
        ctxb = sb("a_ctx", [P, BT, CD])
        xn = sb("a_xn", [P, BT, D])
        scb = sb("a_scb", [P, BT, 2])
        csb = sb("a_csb", [P, BT, 2, 16])
        xT = [sb(f"a_xT{i}", [P, KD, S], F32R) for i in range(2)]
        cT = [sb(f"a_cT{i}", [P, KC, S], F32R) for i in range(2)]
        rot = sb("a_rot", [P, 2, D])
        tmp = sb("a_tmp", [P, 2, D])
        aug = sb("a_aug", [P, 2, H, R])
        qT = sb("a_qT", [P, PAIRS, S], F32R)
        kT = sb("a_kT", [P, PAIRS, S], F32R)
        V = sb("a_V", [P, BT, H, 32])
        PT = sb("a_PT", [P, 4, BT, S])
        oT = sb("a_oT", [P, 2, S])
        nm = sb("a_nm", [P, H, BT])
        nms = sb("a_nms", [P, BT, 16])
        nmT = sb("a_nmT", [16, NG, S])
        rden = sb("a_rden", [P, BT, QH])
        att = sb("a_att", [P, BT, D])
        aT = [sb(f"a_aT{i}", [P, KD, S], F32R) for i in range(2)]
        y = sb("a_y", [P, D])

        W = [ctx.enter_context(nc.psum_tensor(f"a_W{i}", [P, 512], F32)) for i in range(2)]
        SM = [ctx.enter_context(nc.psum_tensor(f"a_SM{i}", [P, 512], F32)) for i in range(2)]
        ST = [ctx.enter_context(nc.psum_tensor(f"a_ST{i}", [P, 512], F32)) for i in range(2)]
        O = [ctx.enter_context(nc.psum_tensor(f"a_O{i}", [P, 512], F32)) for i in range(2)]

        loaded_bo, ones_set = sem("a_loaded_bo"), sem("a_ones_set")
        ctx_loaded, xn_ready = sem("a_ctx_loaded"), sem("a_xn_ready")
        xT_hi = sem("a_xT_hi")
        added, aug_hi, aug_lo = [[sem(f"a_{n}{w}") for w in "qk"] for n in ("added", "aug_hi", "aug_lo")]
        nms_ready = sem("a_nms_ready")
        max_rows = [sem(f"a_max_rows{g}") for g in range(NG)]
        exp_done, weighted_done = sem("a_exp_done"), sem("a_weighted_done")
        aT_hi = sem("a_aT_hi")
        vseq = sem("a_vseq")
        Wf, We = [[sem(f"a_{n}{i}") for i in range(2)] for n in ("W_filled", "W_free")]
        SMf, SMe = [[sem(f"a_{n}{i}") for i in range(2)] for n in ("SM_filled", "SM_free")]
        STf = [sem(f"a_ST_filled{i}") for i in range(2)]
        Oe = [sem(f"a_O_free{i}") for i in range(2)]

        X_TR, C_TR = [0, 1], [2, 3]
        PROJ = {(t, w): 4 + 3 * t + i for t in range(BT) for i, w in enumerate("qkv")}
        AUG_TR = {(t, w, i): 10 + 8 * t + 4 * (w == "k") + i for t in range(BT) for w in "qk" for i in range(4)}
        MAX_TR, O_TR = [26, 27, 29, 32], [28, 30, 31, 33, 34, 35, 36, 37]
        A_TR = [30 + NQ, 31 + NQ]
        OUT = [32 + NQ, 33 + NQ]
        ITEMS = 34 + NQ
        X = core.X

        def rings(it):
            return Ring(Wf, We, ITEMS), Ring(SMf, SMe, H), Ring(STf, STf, H), Ring(Oe, Oe, NQ)

        def evacuate_turned(eng, it, Wr, t, w, which):
            for i in range(4):
                j = AUG_TR[t, w, i]
                if j % 2 != which:
                    continue
                eng.wait_ge(*Wr.until_filled(it, j))
                dst = (qT if w == "q" else kT)[:, 4 * i:4 * i + 4, t * P:(t + 1) * P]
                src = W[j % 2][:, :].rearrange("p (g n) -> p g n", g=4)
                if which == 0:
                    eng.activation(dst, src, ACT.Copy).then_inc(We[j % 2], 1)
                else:
                    eng.tensor_copy(dst, src).then_inc(We[j % 2], 1)

        block = ctx.enter_context(nc.Block())

        @block.sync
        def _(eng):
            eng.dma_start(bo[:, :], bout.partition_broadcast(P)).then_inc(loaded_bo, 16)
            with eng.Fori(0, B) as b:
                Wr = rings(b)[0]
                for t in range(BT):
                    eng.dma_start(ctxb[:, t, :], ctx_d[bass.ds(b, 1), t * P:(t + 1) * P, :]
                                  .rearrange("o p c -> (o p) c")).then_inc(ctx_loaded, 16)
                for g in range(NG):
                    eng.wait_ge(*Wr.until_freed(b, MAX_TR[g]))
                    for par in range(2):
                        for j in range(2):
                            r = 4 * (2 * par + j)
                            row = R * par + MAXROW + j
                            eng.dma_start(r32(qT[row:row + 1, 4 * g:4 * g + 4, :]),
                                          nmT[r:r + 4, g, :]).then_inc(max_rows[g], 16)
            eng.wait_ge(loaded_bo, 16)

        @block.gpsimd
        def _(eng):
            eng.memset(aug[:, :, :, :], 0.0).then_inc(ones_set, 1)
            eng.memset(V[:, :, :, :], 0.0).then_inc(ones_set, 1)
            eng.wait_ge(ones_set, 2)
            eng.memset(V[:, :, :, HD:HD + 1], 1.0).then_inc(ones_set, 1)
            eng.memset(aug[:, 1, :, MAXROW:MAXROW + 2], 1.0).then_inc(ones_set, 1)
            eng.wait_ge(ones_set, 4)
            with eng.Fori(0, B) as b:
                Wr = rings(b)[0]
                for t in range(BT):
                    for a in range(2):
                        n = b * BT + t
                        eng.wait_ge(*Wr.until_freed(b, PROJ[t, "qk"[a]]))
                        eng.tensor_tensor(rot[:, a, :], rot[:, a, :], tmp[:, a, :], ALU.add).then_inc(added[a], 1)
                        lo = LO_HI if a == 0 else HI_LO
                        eng.wait_ge(aug_hi[a], (n + 1) * 2)
                        eng.tensor_tensor(aug[:, a, :, lo:lo + HD], rot[:, a, :].rearrange("p (h e) -> p h e", e=HD),
                                          aug[:, a, :, 0:HD], ALU.subtract).then_inc(aug_lo[a], 1)

        @block.vector
        def _(eng):
            st = ctx.enter_context(nc.sbuf_tensor("a_st", [P, NT, 6], F32))
            lw = ctx.enter_context(nc.sbuf_tensor("a_lnw", [P, 5, NT], F32))
            c = Count()
            layer_norm_scales(eng, vseq, c, X, st, lw, lnsc)
            eng.wait_ge(loaded_bo, 16)
            start = c.now
            PER = 2 + NG + NQ + 2
            with eng.Fori(0, B) as b:
                c = Count(b * PER + start)
                Wr, SMr, STr, Or = rings(b)
                eng.wait_ge(vseq, c.now)
                eng.tensor_copy(scb[:, :, :], lnsc[:, bass.ds(2 * b, 2), :]).then_inc(vseq, c.inc())
                eng.tensor_copy(csb[:, :, :, :].rearrange("p t c e -> p t (c e)"),
                                CS[:, bass.ds(2 * b, 2), :, :].rearrange("p t c e -> p t (c e)")).then_inc(vseq, c.inc())
                eng.wait_ge(vseq, c.now)
                for t in range(BT):
                    eng.tensor_scalar(xn[:, t, :], X[:, bass.ds(2 * b + t, 1), :].rearrange("p o d -> p (o d)"),
                                      scb[:, t, 0:1], scb[:, t, 1:2], ALU.mult, ALU.add).then_inc(xn_ready, 1)
                for t in range(BT):
                    eng.wait_ge(xT_hi, b * 4 + t + 1)
                    eng.tensor_tensor(xT[1][:, :, t * P:(t + 1) * P],
                                      W[X_TR[t] % 2][:, :].rearrange("p (k n) -> p k n", k=KD),
                                      r32(xT[0][:, :, t * P:(t + 1) * P]), ALU.subtract).then_inc(We[X_TR[t] % 2], 1)
                for t in range(BT):
                    eng.wait_ge(xT_hi, b * 4 + 2 + t + 1)
                    eng.tensor_tensor(cT[1][:, :, t * P:(t + 1) * P],
                                      W[C_TR[t] % 2][:, 0:KC * P].rearrange("p (k n) -> p k n", k=KC),
                                      r32(cT[0][:, :, t * P:(t + 1) * P]), ALU.subtract).then_inc(We[C_TR[t] % 2], 1)
                for t in range(BT):
                    for a, w in enumerate("qk"):
                        j = PROJ[t, w]
                        src = W[j % 2][:, :].rearrange("p (h a i) -> p h a i", h=H, i=2)
                        tv = tmp[:, a, :].rearrange("p (h a i) -> p h a i", h=H, i=2)
                        cosb = csb[:, t, 0, :].unsqueeze(1).to_broadcast([P, H, 16])
                        sinv = csb[:, t, 1, :].rearrange("p (a i) -> p a i", i=2)
                        eng.wait_ge(*Wr.until_filled(b, j))
                        if t:
                            eng.wait_ge(aug_lo[a], b * BT + t)
                        eng.tensor_tensor(rot[:, a, :].rearrange("p (h e) -> p h e", h=H),
                                          W[j % 2][:, :].rearrange("p (h e) -> p h e", h=H), cosb, ALU.mult)
                        eng.tensor_tensor(tv[:, :, :, 0], src[:, :, :, 1],
                                          sinv[:, :, 0].unsqueeze(1).to_broadcast([P, H, 8]), ALU.mult)
                        eng.tensor_tensor(tv[:, :, :, 1], src[:, :, :, 0],
                                          sinv[:, :, 1].unsqueeze(1).to_broadcast([P, H, 8]), ALU.mult)\
                           .then_inc(We[j % 2], 1)
                for t in range(BT):
                    for w in "qk":
                        evacuate_turned(eng, b, Wr, t, w, 1)

                def top(h):
                    eng.wait_ge(*SMr.until_filled(b, h))
                    eng.tensor_reduce(nm[:, h, :], SM[h % 2][:, :].rearrange("p (t k) -> p t k", t=BT),
                                      AX.X, ALU.max, negate=True).then_inc(SMe[h % 2], 1)
                    if h % GH == GH - 1:
                        g = h // GH
                        for i in (h - 1, h):
                            eng.wait_ge(*SMr.until_freed(b, i))
                        if g:
                            eng.wait_ge(*Wr.until_freed(b, MAX_TR[g - 1]))
                        src = nm[:, g * GH:(g + 1) * GH, :].rearrange("p (a r) t -> p t r a", r=2)
                        dst = nms[:, :, :].rearrange("p t (r j a) -> p t r j a", r=2, j=2)
                        for t in range(BT):
                            i = eng.tensor_copy(dst[:, t, :, 0, :].bitcast(F32R), src[:, t])
                        i.then_inc(vseq, c.inc())
                        eng.wait_ge(vseq, c.now)
                        for t in range(BT):
                            i = eng.tensor_tensor(dst[:, t, :, 1, :], src[:, t], dst[:, t, :, 0, :], ALU.subtract)
                        i.then_inc(nms_ready, 1)

                def normalise(q):
                    j = O_TR[q]
                    o = W[j % 2][:, 0:BT * P].rearrange("p (t h e) -> p t h e", t=BT, h=QH)
                    eng.wait_ge(*Wr.until_filled(b, j))
                    if q:
                        eng.wait_ge(*Wr.until_freed(b, O_TR[q - 1]))
                    eng.reciprocal(rden[:, :, :], o[:, :, :, HD]).then_inc(vseq, c.inc())
                    eng.wait_ge(vseq, c.now)
                    for t in range(BT):
                        i = eng.tensor_tensor(att[:, t, q * QH * HD:(q + 1) * QH * HD]
                                              .rearrange("p (h e) -> p h e", h=QH), o[:, t, :, 0:HD],
                                              rden[:, t].unsqueeze(2).to_broadcast([P, QH, HD]), ALU.mult)
                    i.then_inc(We[j % 2], 1)

                for h in range(2 * GH):
                    top(h)
                for h in range(H):
                    if h + 2 * GH < H:
                        top(h + 2 * GH)
                    if h % QH == 2 and h >= QH:
                        normalise(h // QH - 1)
                normalise(NQ - 1)
                for t in range(BT):
                    eng.wait_ge(aT_hi, b * BT + t + 1)
                    eng.tensor_tensor(aT[1][:, :, t * P:(t + 1) * P],
                                      W[A_TR[t] % 2][:, :].rearrange("p (k n) -> p k n", k=KD),
                                      r32(aT[0][:, :, t * P:(t + 1) * P]), ALU.subtract).then_inc(We[A_TR[t] % 2], 1)
                for t in range(BT):
                    j = OUT[t]
                    xx = X[:, bass.ds(2 * b + t, 1), :].rearrange("p o d -> p (o d)")
                    eng.wait_ge(*Wr.until_filled(b, j))
                    eng.wait_ge(vseq, c.now)
                    eng.tensor_tensor(y[:, :], W[j % 2][:, :], bo[:, :], ALU.add).then_inc(We[j % 2], 1)
                    eng.wait_ge(*Wr.until_freed(b, j))
                    eng.scalar_tensor_tensor(out=xx, in0=y[:, :], scalar=gate, in1=xx,
                                             op0=ALU.mult, op1=ALU.add).then_inc(vseq, c.inc())
                assert c.n == PER, (c.n, PER)

        @block.scalar
        def _(eng):
            eng.wait_ge(ones_set, 4)
            with eng.Fori(0, B) as b:
                Wr, SMr, STr, Or = rings(b)
                for t in range(BT):
                    eng.wait_ge(*Wr.until_filled(b, X_TR[t]))
                    eng.activation(xT[0][:, :, t * P:(t + 1) * P],
                                   W[X_TR[t] % 2][:, :].rearrange("p (k n) -> p k n", k=KD),
                                   ACT.Copy).then_inc(xT_hi, 1)
                for t in range(BT):
                    eng.wait_ge(*Wr.until_filled(b, C_TR[t]))
                    eng.activation(cT[0][:, :, t * P:(t + 1) * P],
                                   W[C_TR[t] % 2][:, 0:KC * P].rearrange("p (k n) -> p k n", k=KC),
                                   ACT.Copy).then_inc(xT_hi, 1)

                def rounded(t, a):
                    n = b * BT + t
                    heads = rot[:, a, :].rearrange("p (h e) -> p h e", e=HD)
                    dup = HI_LO if a == 0 else LO_HI
                    eng.wait_ge(added[a], n + 1)
                    if t:
                        eng.wait_ge(*Wr.until_filled(b, AUG_TR[t - 1, "qk"[a], 3]))
                    for at in (HI_HI, dup):
                        eng.activation(aug[:, a, :, at:at + HD].bitcast(F32R), heads, ACT.Copy).then_inc(aug_hi[a], 1)

                def values(t):
                    j = PROJ[t, "v"]
                    eng.wait_ge(*Wr.until_filled(b, j))
                    eng.activation(V[:, t, :, 0:HD], W[j % 2][:, :].rearrange("p (h e) -> p h e", h=H),
                                   ACT.Copy).then_inc(We[j % 2], 1)

                rounded(0, 0)
                rounded(0, 1)
                values(0)
                values(1)
                evacuate_turned(eng, b, Wr, 0, "q", 0)
                rounded(1, 0)
                evacuate_turned(eng, b, Wr, 0, "k", 0)
                rounded(1, 1)
                evacuate_turned(eng, b, Wr, 1, "q", 0)
                evacuate_turned(eng, b, Wr, 1, "k", 0)

                def maxima(g):
                    j = MAX_TR[g]
                    eng.wait_ge(*Wr.until_filled(b, j))
                    eng.activation(nmT[:, g, :], W[j % 2][0:16, 0:S], ACT.Copy).then_inc(We[j % 2], 1)

                def turned_outputs(q):
                    eng.wait_ge(weighted_done, b * H + (q + 1) * QH)
                    if q >= 2:
                        eng.wait_ge(*Wr.until_filled(b, O_TR[q - 2]))
                    eng.activation(oT[:, q % 2, :], O[q % 2][:, 0:S], ACT.Copy).then_inc(Oe[q % 2], 1)

                maxima(0)
                for h in range(H):
                    eng.wait_ge(*STr.until_filled(b, h))
                    if h >= 4:
                        eng.wait_ge(weighted_done, b * H + h - 3)
                    eng.activation(PT[:, h % 4, :, :].rearrange("p t s -> p (t s)"), ST[h % 2][:, :], ACT.Exp,
                                   scale=SCALE).then_inc(exp_done, 1)
                    if h % GH == 1 and h // GH + 1 < NG:
                        maxima(h // GH + 1)
                    if h % QH == 1 and h >= QH:
                        turned_outputs(h // QH - 1)
                turned_outputs(NQ - 1)
                for t in range(BT):
                    eng.wait_ge(*Wr.until_filled(b, A_TR[t]))
                    eng.activation(aT[0][:, :, t * P:(t + 1) * P],
                                   W[A_TR[t] % 2][:, :].rearrange("p (k n) -> p k n", k=KD),
                                   ACT.Copy).then_inc(aT_hi, 1)

        @block.tensor
        def _(eng):
            for s_ in We + SMe + Oe:
                eng.sem_inc(s_, 1)
            with eng.Fori(0, B) as b:
                Wr, SMr, STr, Or = rings(b)

                def turn(j, srcs):
                    eng.wait_ge(*Wr.until_free(b, j))
                    for i, s in enumerate(srcs):
                        m = eng.transpose(W[j % 2][0:s.shape[1], i * P:(i + 1) * P], s, core.ident[:, :])
                    m.then_inc(Wf[j % 2], 1)

                def product(j, tok, lhs, rhs, k, cols):
                    eng.wait_ge(*Wr.until_free(b, j))
                    n = 0
                    for x_, w_ in ((0, 0), (0, 1), (1, 0)):
                        for i in range(k):
                            m = eng.matmul(W[j % 2][:, :], lhs[x_][:, i, tok * P:(tok + 1) * P],
                                           rhs[w_][:, i, cols:cols + D], start=(n == 0), stop=(n == 3 * k - 1))
                            n += 1
                    m.then_inc(Wf[j % 2], 1)

                for t in range(BT):
                    eng.wait_ge(xn_ready, b * BT + t + 1)
                    turn(X_TR[t], [xn[:, t, k * P:(k + 1) * P] for k in range(KD)])
                eng.wait_ge(ctx_loaded, (b + 1) * 32)
                for t in range(BT):
                    turn(C_TR[t], [ctxb[:, t, k * P:(k + 1) * P] for k in range(KC)])
                for j in C_TR:
                    eng.wait_ge(*Wr.until_freed(b, j))
                for t in range(BT):
                    product(PROJ[t, "q"], t, xT, wq, KD, 0)
                    product(PROJ[t, "k"], t, cT, wkv, KC, 0)
                    product(PROJ[t, "v"], t, cT, wkv, KC, D)
                for t in range(BT):
                    for a, w in enumerate("qk"):
                        eng.wait_ge(aug_lo[a], b * BT + t + 1)
                        for i in range(4):
                            turn(AUG_TR[t, w, i],
                                 [aug[:, a, 2 * g:2 * g + 2, :].rearrange("p h r -> p (h r)")
                                  for g in range(4 * i, 4 * i + 4)])
                for i in (2, 3):
                    eng.wait_ge(*Wr.until_freed(b, AUG_TR[1, "k", i]))

                def scores_for_max(h):
                    r = R * (h % 2)
                    eng.wait_ge(*SMr.until_free(b, h))
                    for t in range(BT):
                        m = eng.matmul(SM[h % 2][:, t * S:(t + 1) * S],
                                       qT[r:r + MAXROW, h // 2, t * P:(t + 1) * P], kT[r:r + MAXROW, h // 2, :],
                                       start=True, stop=True)
                    m.then_inc(SMf[h % 2], 1)

                def turn_maxima(g):
                    eng.wait_ge(nms_ready, b * NG + g + 1)
                    turn(MAX_TR[g], [nms[:, t, :] for t in range(BT)])

                def scores(h):
                    r = R * (h % 2)
                    if h % GH == 0:
                        eng.wait_ge(max_rows[h // GH], (b + 1) * 64)
                    if h >= 2:
                        eng.wait_ge(exp_done, b * H + h - 1)
                    for t in range(BT):
                        m = eng.matmul(ST[h % 2][:, t * S:(t + 1) * S],
                                       kT[r:r + MAXROW + 2, h // 2, t * P:(t + 1) * P],
                                       qT[r:r + MAXROW + 2, h // 2, :], start=True, stop=True)
                    m.then_inc(STf[h % 2], 1)

                def weighted(h):
                    q, r = h // QH, 32 * (h % QH)
                    if h % QH == 0:
                        eng.wait_ge(*Or.until_free(b, q))
                    eng.wait_ge(exp_done, b * H + h + 1)
                    for k in range(BT):
                        m = eng.matmul(O[q % 2][r:r + 32, 0:S], V[:, k, h, :], PT[:, h % 4, k, :],
                                       start=(k == 0), stop=(k == BT - 1))
                    m.then_inc(weighted_done, 1)

                def turn_outputs(q):
                    eng.wait_ge(*Or.until_freed(b, q))
                    turn(O_TR[q], [oT[:, q % 2, t * P:(t + 1) * P] for t in range(BT)])

                for h in range(2 * GH):
                    scores_for_max(h)
                    if h == GH:
                        turn_maxima(0)
                for h in range(H):
                    scores(h)
                    if h + 2 * GH < H:
                        scores_for_max(h + 2 * GH)
                    if h % GH == 1 and h // GH + 1 < NG:
                        turn_maxima(h // GH + 1)
                    if h:
                        weighted(h - 1)
                    if h % QH == 2 and h >= QH:
                        turn_outputs(h // QH - 1)
                weighted(H - 1)
                turn_outputs(NQ - 1)
                eng.wait_ge(*Wr.until_freed(b, O_TR[NQ - 1]))
                for t in range(BT):
                    turn(A_TR[t], [att[:, t, k * P:(k + 1) * P] for k in range(KD)])
                for t in range(BT):
                    eng.wait_ge(*Wr.until_freed(b, A_TR[t]))
                for t in range(BT):
                    product(OUT[t], t, aT, wo, KD, 0)


def turned_tokens(nc, core, name, xT):
    with ExitStack() as ctx:
        sb = lambda n, shape, dt=F32: ctx.enter_context(nc.sbuf_tensor(name + n, shape, dt))
        sem = semaphores(nc, ctx, name)
        lnsc, st, lw = sb("lnsc", [P, NT, 2]), sb("st", [P, NT, 6]), sb("lw", [P, 5, NT])
        xn = sb("xn", [P, 2, D])
        bank = [ctx.enter_context(nc.psum_tensor(f"{name}bank{i}", [P, KD * P], F32)) for i in range(4)]
        vseq, xn_ready, turned, hi_done, lo_done = (sem("vseq"), sem("xn_ready"), sem("turned"), sem("hi_done"),
                                                    sem("lo_done"))
        block = ctx.enter_context(nc.Block())

        def view(t):
            return bank[t % 4][:, :].rearrange("p (k n) -> p k n", k=KD)

        def part(x, t):
            return x[:, :, t * P:(t + 1) * P]

        @block.vector
        def _(eng):
            c = Count()
            layer_norm_scales(eng, vseq, c, core.X, st, lw, lnsc)
            eng.wait_ge(vseq, c.now)

            def low(t):
                eng.wait_ge(hi_done, t + 1)
                eng.tensor_tensor(part(xT[1], t), view(t), r32(part(xT[0], t)), ALU.subtract).then_inc(lo_done, 1)

            for t in range(NT):
                if t >= 2:
                    eng.wait_ge(turned, t - 1)
                eng.tensor_scalar(xn[:, t % 2, :], core.X[:, t, :], lnsc[:, t, 0:1], lnsc[:, t, 1:2],
                                  ALU.mult, ALU.add).then_inc(xn_ready, 1)
                if t >= 2:
                    low(t - 2)
            low(NT - 2)
            low(NT - 1)

        @block.tensor
        def _(eng):
            for t in range(NT):
                eng.wait_ge(xn_ready, t + 1)
                if t >= 4:
                    eng.wait_ge(lo_done, t - 3)
                for k in range(KD):
                    m = eng.transpose(bank[t % 4][:, k * P:(k + 1) * P], xn[:, t % 2, k * P:(k + 1) * P],
                                      core.ident[:, :])
                m.then_inc(turned, 1)

        @block.scalar
        def _(eng):
            for t in range(NT):
                eng.wait_ge(turned, t + 1)
                eng.activation(part(xT[0], t), view(t), ACT.Copy).then_inc(hi_done, 1)


def turned_rows(nc, core, name, w, n, hi, lo):
    with ExitStack() as ctx:
        raw = ctx.enter_context(nc.sbuf_tensor(name + "raw", [n, D], F32))
        bank = ctx.enter_context(nc.psum_tensor(name + "bank", [P, KD * n], F32))
        sem = semaphores(nc, ctx, name)
        loaded, turned, hi_done = sem("loaded"), sem("turned"), sem("hi_done")
        block = ctx.enter_context(nc.Block())
        v = bank[:, :].rearrange("p (k n) -> p k n", k=KD)

        @block.sync
        def _(eng):
            eng.dma_start(raw[:, :], w).then_inc(loaded, 16)

        @block.tensor
        def _(eng):
            eng.wait_ge(loaded, 16)
            for k in range(KD):
                m = eng.transpose(bank[:, k * n:(k + 1) * n], raw[:, k * P:(k + 1) * P], core.ident[0:n, 0:n])
            m.then_inc(turned, 1)

        @block.scalar
        def _(eng):
            eng.wait_ge(turned, 1)
            eng.activation(hi, v, ACT.Copy).then_inc(hi_done, 1)

        @block.vector
        def _(eng):
            eng.wait_ge(hi_done, 1)
            eng.tensor_tensor(lo, v, r32(hi), ALU.subtract)


def router_logits(eng, bank, xT, gw, n, done):
    for t in range(NT):
        i = 0
        for x_, w_ in ((0, 0), (0, 1), (1, 0)):
            for k in range(KD):
                m = eng.matmul(bank[:, t * n:(t + 1) * n], xT[x_][:, k, t * P:(t + 1) * P], gw[w_][:, k, :],
                               start=(i == 0), stop=(i == 3 * KD - 1))
                i += 1
    m.then_inc(done, 1)


def chosen(eng, sem, c, p, n, top, tri, gt, eq, rank):
    a = p.unsqueeze(2).to_broadcast([P, NT, n, n])
    b = p.unsqueeze(3).to_broadcast([P, NT, n, n])
    eng.wait_ge(sem, c.now)
    eng.tensor_tensor(gt, a, b, ALU.is_gt).then_inc(sem, c.inc())
    eng.tensor_tensor(eq, a, b, ALU.is_equal).then_inc(sem, c.inc())
    eng.wait_ge(sem, c.now)
    eng.tensor_tensor(eq, eq, tri.unsqueeze(1).to_broadcast([P, NT, n, n]), ALU.mult).then_inc(sem, c.inc())
    eng.wait_ge(sem, c.now)
    eng.tensor_tensor(gt, gt, eq, ALU.add).then_inc(sem, c.inc())
    eng.wait_ge(sem, c.now)
    eng.tensor_reduce(rank, gt, AX.X, ALU.add).then_inc(sem, c.inc())


def expert_router(nc, core, xT, gw, E, K, rT):
    with ExitStack() as ctx:
        sb = lambda n, shape, dt=F32: ctx.enter_context(nc.sbuf_tensor("br_" + n, shape, dt))
        sem = semaphores(nc, ctx, "br_")
        p, rank, r = sb("p", [P, NT, E]), sb("rank", [P, NT, E]), sb("r", [P, NT, E])
        m1, s1 = sb("m1", [P, NT]), sb("s1", [P, NT])
        tri, gt, eq = sb("tri", [P, E, E]), sb("gt", [P, NT, E, E], BF16), sb("eq", [P, NT, E, E], BF16)
        rs, ones = sb("rs", [E, T]), sb("ones", [1, T])
        bank = ctx.enter_context(nc.psum_tensor("br_bank", [P, NT * E], F32))
        tb = [ctx.enter_context(nc.psum_tensor(f"br_tb{i}", [E, 4 * P], F32)) for i in range(4)]
        logits, shifted, exped, vseq, r_ready, turned, sent, consts, outs = [
            sem(n) for n in ("logits", "shifted", "exped", "vseq", "r_ready", "turned", "sent", "consts", "outs")]
        block = ctx.enter_context(nc.Block())
        bc = lambda a: a.unsqueeze(2).to_broadcast([P, NT, E])

        @block.gpsimd
        def _(eng):
            eng.memset(ones[:, :], 1.0).then_inc(consts, 1)
            eng.memset(tri[:, :, :], 1.0).then_inc(consts, 1)
            eng.wait_ge(consts, 2)
            eng.affine_select(out=tri[:, :, :], in_=tri[:, :, :], compare_op=ALU.is_gt, fill=0.0, base=0,
                              pattern=[[1, E], [-1, E]], channel_multiplier=0).then_inc(consts, 1)

        @block.tensor
        def _(eng):
            router_logits(eng, bank, xT, gw, E, logits)
            eng.wait_ge(r_ready, 1)
            for i in range(4):
                for j in range(4):
                    m = eng.transpose(tb[i][:, j * P:(j + 1) * P], r[:, 4 * i + j, :], core.ident[:, :])
                m.then_inc(turned, 1)

        @block.vector
        def _(eng):
            c = Count()
            lg = bank[:, :].rearrange("p (t e) -> p t e", t=NT)
            eng.wait_ge(logits, 1)
            eng.tensor_reduce(m1[:, :], lg, AX.X, ALU.max).then_inc(vseq, c.inc())
            eng.wait_ge(vseq, c.now)
            eng.tensor_tensor(p[:, :, :], lg, bc(m1[:, :]), ALU.subtract).then_inc(shifted, 1)
            eng.wait_ge(exped, 1)
            eng.tensor_reduce(s1[:, :], p[:, :, :], AX.X, ALU.add).then_inc(vseq, c.inc())
            eng.wait_ge(vseq, c.now)
            eng.reciprocal(m1[:, :], s1[:, :]).then_inc(vseq, c.inc())
            eng.wait_ge(vseq, c.now)
            eng.tensor_tensor(p[:, :, :], p[:, :, :], bc(m1[:, :]), ALU.mult).then_inc(vseq, c.inc())
            eng.wait_ge(consts, 3)
            chosen(eng, vseq, c, p[:, :, :], E, K, tri[:, :, :], gt[:, :, :, :], eq[:, :, :, :], rank[:, :, :])
            eng.wait_ge(vseq, c.now)
            eng.scalar_tensor_tensor(out=r[:, :, :], in0=rank[:, :, :], scalar=K - 0.5, in1=p[:, :, :],
                                     op0=ALU.is_lt, op1=ALU.mult).then_inc(r_ready, 1)

        @block.scalar
        def _(eng):
            eng.wait_ge(shifted, 1)
            eng.activation(p[:, :, :], p[:, :, :], ACT.Exp).then_inc(exped, 1)
            for i in range(4):
                eng.wait_ge(turned, i + 1)
                eng.activation(rs[:, 4 * i * P:4 * (i + 1) * P], tb[i][:, :], ACT.Copy).then_inc(sent, 1)

        @block.sync
        def _(eng):
            eng.wait_ge(consts, 1)
            eng.dma_start(rT[E:E + 1, :], ones[:, :]).then_inc(outs, 16)
            eng.wait_ge(sent, 4)
            eng.dma_start(rT[0:E, :], rs[:, :]).then_inc(outs, 16)
            eng.wait_ge(outs, 32)


def expert_ffn(nc, core, w_gate, wg, wu, wd, sg, su, sd, gate):
    E, K, I = wg.shape[0], 4, wg.shape[2]
    SI = sg.shape[1]
    TAIL = I - 2 * P
    PART = P - TAIL
    NTAIL = E * TAIL // P
    assert TAIL == 3 * PART and SI == 5 * P + P // 2
    TB = 512
    STEPS = T // TB
    LOOPED = E + NTAIL // 2 + 2
    rT = nc.dram_tensor("b_rT", [E + 1, T], F32, kind="Internal").ap()
    with ExitStack() as ctx:
        sb = lambda n, shape, dt=F32: ctx.enter_context(nc.sbuf_tensor("b_" + n, shape, dt))
        sem = semaphores(nc, ctx, "b_")
        sems = lambda n: [sem(f"{n}{c}") for c in range(2)]
        xT = [sb(f"xT{i}", [P, KD, T], F32R) for i in range(2)]
        turned_tokens(nc, core, "bt_", xT)
        with ExitStack() as c2:
            gw = [c2.enter_context(nc.sbuf_tensor(f"b_gw{i}", [P, KD, E], F32R)) for i in range(2)]
            turned_rows(nc, core, "bg_", w_gate, E, gw[0][:, :, :], gw[1][:, :, :])
            expert_router(nc, core, xT, gw, E, K, rT)

        raw = sb("raw", [P, 2, 3, KD * P])
        wh = sb("wh", [P, 2, 2, 3, KD * P], F32R)
        wl = sb("wl", [P, 2, 2, 3, KD * P], F32R)
        rb = sb("rb", [P, 2, 2, T])
        silu, act = sb("silu", [P, 2, TB]), sb("act", [P, 2, TB])
        ah, al = sb("ah", [P, 2, TB], F32R), sb("al", [P, 2, TB], F32R)
        G = [ctx.enter_context(nc.psum_tensor(f"b_G{i}", [P, TB], F32)) for i in range(2)]
        U = [ctx.enter_context(nc.psum_tensor(f"b_U{i}", [P, TB], F32)) for i in range(2)]
        Y = [ctx.enter_context(nc.psum_tensor(f"b_Y{i}", [P, D], F32)) for i in range(4)]
        raw_in, w_hi, w_lo = sems("raw_in"), sems("w_hi"), sems("w_lo")
        rb_in = [sems(f"rb_in_{s}_") for s in range(2)]
        gu_done, silu_done, up_done, act_done, a_hi, a_lo = [
            sems(n) for n in ("gu_done", "silu_done", "up_done", "act_done", "a_hi", "a_lo")]
        y_done, y_free = sem("y_done"), sem("y_free")
        NB = TB // P
        W_DMAS, R_DMAS = 6, 2
        block = ctx.enter_context(nc.Block())


        @block.sync
        def _(eng):
            for s_ in w_lo + silu_done + up_done + a_lo:
                eng.sem_inc(s_, 1)
            eng.sem_inc(y_free, NB)
            eng.sem_inc(y_done, NB)

            def chunk(p, c, gparts, dparts, rparts):
                eng.wait_ge(w_lo[c], p + 1)
                for dst_k, cols, g_, u_ in gparts:
                    for which, src in enumerate((g_, u_)):
                        dst = raw[:, c, which, :].rearrange("p (k n) -> p k n", k=KD)[:, dst_k, cols]
                        eng.dma_start(dst, src).then_inc(raw_in[c], 16)
                for rows, src in dparts:
                    eng.dma_start(raw[rows, c, 2, :], src).then_inc(raw_in[c], 16)
                assert 2 * len(gparts) + len(dparts) == W_DMAS and len(rparts) == R_DMAS

            allk, halves = slice(0, KD), (slice(0, KD // 2), slice(KD // 2, KD))
            allc = slice(0, P)

            def whole(w3, e, h, cols):
                return w3[bass.ds(e, 1)].rearrange("o (k p) n -> p (o k) n", p=P)[:, h, cols]

            def load(p, s, c, gparts, dparts, rparts, first=False):
                chunk(p, c, gparts, dparts, rparts)
                if not first:
                    eng.wait_ge(up_done[c], STEPS * (p - 1) + 1)
                for rows, row in rparts:
                    eng.dma_start(rb[rows, s, c, :], rT[row, :].rearrange("o t -> (o t)")
                                  .partition_broadcast(rows.stop - rows.start)).then_inc(rb_in[s][c], 16)

            def load_whole(p, s, e, first=False):
                for c in range(2):
                    cols = slice(c * P, (c + 1) * P)
                    hp = P // 2
                    load(p, s, c, [(h, allc, whole(wg, e, h, cols), whole(wu, e, h, cols)) for h in halves],
                         [(slice(i * hp, (i + 1) * hp),
                           wd[bass.ds(e, 1), c * P + i * hp:c * P + (i + 1) * hp, :].rearrange("o i n -> (o i) n"))
                          for i in range(2)],
                         [(slice(i * hp, (i + 1) * hp), bass.ds(e, 1)) for i in range(2)], first)

            def load_tail(p, s, n0):
                for c in range(2):
                    n = n0 + c
                    group = n // 3
                    e, f, at = n + group, group * 4 + 3, (n % 3) * PART + 2 * P
                    load(p, s, c,
                         [(allk, slice(0, TAIL), whole(wg, e, allk, slice(2 * P, I)), whole(wu, e, allk, slice(2 * P, I))),
                          (allk, slice(TAIL, P), whole(wg, f, allk, bass.ds(at, PART)),
                           whole(wu, f, allk, bass.ds(at, PART)))],
                         [(slice(0, TAIL), wd[bass.ds(e, 1), 2 * P:I, :].rearrange("o i n -> (o i) n")),
                          (slice(TAIL, P), wd[bass.ds(f, 1), bass.ds(at, PART), :].rearrange("o i n -> (o i) n"))],
                         [(slice(0, TAIL), bass.ds(e, 1)), (slice(TAIL, P), bass.ds(f, 1))])

            def load_shared(p, s, n0):
                sk = lambda a, h, c0, c1: a.rearrange("(k p) n -> p k n", p=P)[:, h, c0:c1]
                for c in range(2):
                    c0, c1 = (n0 + c) * P, min((n0 + c + 1) * P, SI)
                    w = c1 - c0
                    load(p, s, c, [(h, slice(0, w), sk(sg, h, c0, c1), sk(su, h, c0, c1)) for h in halves],
                         [(slice(i * w // 2, (i + 1) * w // 2), sd[c0 + i * w // 2:c0 + (i + 1) * w // 2, :])
                          for i in range(2)],
                         [(slice(i * w // 2, (i + 1) * w // 2), slice(E, E + 1)) for i in range(2)])

            load_whole(0, 0, 0, first=True)
            load_whole(1, 1, 1, first=True)
            with eng.Fori(1, E // 2) as it:
                for s in range(2):
                    load_whole(2 * it + s, s, 2 * it + s)
            with eng.Fori(0, NTAIL // 4) as it:
                for s in range(2):
                    load_tail(E + 2 * it + s, s, 4 * it + 2 * s)
            for i in range(3):
                load_shared(E + NTAIL // 2 + i, i % 2, 2 * i)

        def width(c, last):
            return SI % P if last and c == 1 else P

        def prepare_hi(eng, p, s, c, w=P):
            eng.wait_ge(raw_in[c], (p + 1) * 16 * W_DMAS)
            if w == P:
                eng.activation(wh[:, s, c].rearrange("p a n -> p (a n)"), raw[:, c].rearrange("p a n -> p (a n)"),
                               ACT.Copy).then_inc(w_hi[c], 1)
            else:
                for a in range(2):
                    v = lambda x: x.rearrange("p (k n) -> p k n", k=KD)[:, :, 0:w]
                    eng.activation(v(wh[:, s, c, a, :]), v(raw[:, c, a, :]), ACT.Copy)
                eng.activation(wh[0:w, s, c, 2, :], raw[0:w, c, 2, :], ACT.Copy).then_inc(w_hi[c], 1)

        def prepare_lo(eng, p, s, c, w=P):
            eng.wait_ge(w_hi[c], p + 1)
            if w == P:
                flat = lambda x: x.rearrange("p a n -> p (a n)")
                eng.tensor_tensor(flat(wl[:, s, c]), flat(raw[:, c]), flat(r32(wh[:, s, c])),
                                  ALU.subtract).then_inc(w_lo[c], 1)
            else:
                for a in range(2):
                    v = lambda x: x.rearrange("p (k n) -> p k n", k=KD)[:, :, 0:w]
                    eng.tensor_tensor(v(wl[:, s, c, a, :]), v(raw[:, c, a, :]), v(r32(wh[:, s, c, a, :])), ALU.subtract)
                eng.tensor_tensor(wl[0:w, s, c, 2, :], raw[0:w, c, 2, :], r32(wh[0:w, s, c, 2, :]),
                                  ALU.subtract).then_inc(w_lo[c], 1)

        @block.tensor
        def _(eng):
            def gate_up(n, s, i, c, w):
                eng.wait_ge(silu_done[c], n + 1)
                eng.wait_ge(up_done[c], n + 1)
                for a, bank in enumerate((G[c], U[c])):
                    j = 0
                    for w_, x_ in ((wh, 0), (wh, 1), (wl, 0)):
                        for k in range(KD):
                            m = eng.matmul(bank[0:w, :], w_[:, s, c, a, k * P:k * P + w],
                                           xT[x_][:, k, i * TB:(i + 1) * TB], start=(j == 0), stop=(j == 3 * KD - 1))
                            j += 1
                m.then_inc(gu_done[c], 1)

            def down(n, s, i, w1):
                for b in range(NB):
                    eng.wait_ge(y_free, NB * n + b + 1)
                    if b == 0:
                        eng.wait_ge(a_lo[0], n + 2)
                    t = slice(b * P, (b + 1) * P)
                    eng.matmul(Y[b][:, :], ah[:, 0, t], wh[:, s, 0, 2, :], start=True, stop=False)
                    eng.matmul(Y[b][:, :], ah[:, 0, t], wl[:, s, 0, 2, :], start=False, stop=False)
                    eng.matmul(Y[b][:, :], al[:, 0, t], wh[:, s, 0, 2, :], start=False, stop=False)
                eng.wait_ge(a_hi[1], n + 1)
                for b in range(NB):
                    t = slice(b * P, (b + 1) * P)
                    eng.matmul(Y[b][:, :], ah[0:w1, 1, t], wh[0:w1, s, 1, 2, :], start=False, stop=False)
                    eng.matmul(Y[b][:, :], ah[0:w1, 1, t], wl[0:w1, s, 1, 2, :], start=False, stop=False)
                eng.wait_ge(a_lo[1], n + 2)
                for b in range(NB):
                    t = slice(b * P, (b + 1) * P)
                    eng.matmul(Y[b][:, :], al[0:w1, 1, t], wh[0:w1, s, 1, 2, :], start=False, stop=True)\
                       .then_inc(y_done, 1)

            def pair(p, s, last=False):
                for i in range(STEPS):
                    n = STEPS * p + i
                    for c in range(2):
                        if i == 0:
                            eng.wait_ge(w_lo[c], p + 2)
                        gate_up(n, s, i, c, width(c, last))
                    down(n, s, i, width(1, last))

            with eng.Fori(0, LOOPED // 2) as it:
                for s in range(2):
                    pair(2 * it + s, s)
            pair(LOOPED, 0, last=True)

        @block.scalar
        def _(eng):
            def step(n, c, w):
                eng.wait_ge(gu_done[c], n + 1)
                eng.activation(silu[0:w, c, :], G[c][0:w, :], ACT.Silu).then_inc(silu_done[c], 1)
                eng.wait_ge(act_done[c], n + 1)
                eng.activation(ah[0:w, c, :], act[0:w, c, :], ACT.Copy).then_inc(a_hi[c], 1)

            def pair(p, s, last=False, before_last=False):
                for i in range(STEPS):
                    for c in range(2):
                        step(STEPS * p + i, c, width(c, last))
                    if i in (0, 1) and not last:
                        if i == 0:
                            eng.wait_ge(y_done, NB * STEPS * p + NB)
                        prepare_hi(eng, p + 1, 1 - s, i, width(i, before_last))

            for c in range(2):
                prepare_hi(eng, 0, 0, c)
            with eng.Fori(0, LOOPED // 2 - 1) as it:
                for s in range(2):
                    pair(2 * it + s, s)
            pair(LOOPED - 2, 0)
            pair(LOOPED - 1, 1, before_last=True)
            pair(LOOPED, 0, last=True)

        @block.gpsimd
        def _(eng):
            def pair(p, s, last=False, before_last=False):
                for i in range(STEPS):
                    n = STEPS * p + i
                    for c in range(2):
                        w = width(c, last)
                        eng.wait_ge(a_hi[c], n + 1)
                        eng.tensor_tensor(al[0:w, c, :], act[0:w, c, :], r32(ah[0:w, c, :]),
                                          ALU.subtract).then_inc(a_lo[c], 1)
                    if i in (0, 1) and not last:
                        prepare_lo(eng, p + 1, 1 - s, i, width(i, before_last))

            for c in range(2):
                prepare_lo(eng, 0, 0, c)
            with eng.Fori(0, LOOPED // 2 - 1) as it:
                for s in range(2):
                    pair(2 * it + s, s)
            pair(LOOPED - 2, 0)
            pair(LOOPED - 1, 1, before_last=True)
            pair(LOOPED, 0, last=True)

        @block.vector
        def _(eng):
            def pair(it, s, last=False):
                for i in range(STEPS):
                    n = STEPS * (2 * it + s) + i
                    for c in range(2):
                        w = width(c, last)
                        if i == 0:
                            eng.wait_ge(rb_in[s][c], (it + 1) * 16 * R_DMAS)
                        eng.wait_ge(gu_done[c], n + 1)
                        eng.wait_ge(a_lo[c], n + 1)
                        eng.tensor_tensor(act[0:w, c, :], U[c][0:w, :], rb[0:w, s, c, i * TB:(i + 1) * TB],
                                          ALU.mult).then_inc(up_done[c], 1)
                        eng.wait_ge(silu_done[c], n + 2)
                        eng.wait_ge(up_done[c], n + 2)
                        eng.tensor_tensor(act[0:w, c, :], act[0:w, c, :], silu[0:w, c, :],
                                          ALU.mult).then_inc(act_done[c], 1)
                    for b in range(NB):
                        eng.wait_ge(y_done, NB * n + b + 1 + NB)
                        x = core.X[:, i * NB + b, :]
                        eng.scalar_tensor_tensor(out=x, in0=Y[b][:, :], scalar=gate, in1=x, op0=ALU.mult,
                                                 op1=ALU.add).then_inc(y_free, 1)

            with eng.Fori(0, LOOPED // 2) as it:
                for s in range(2):
                    pair(it, s)
            pair(LOOPED // 2, 0, last=True)


def normed_attention(nc, core, ctx_d, Wq, bq, Wk, bk, Wv, bv, Wkv_dca, bkv_dca, qn_w, qn_b, kn_w, kn_b,
                     kn_dca_w, kn_dca_b, Wo, bo_d, gate):
    H, HD = 16, 32
    DCA = 16
    MAIN = S - DCA
    MT = MAIN - P
    LO_HI, MAXROW = 2 * HD, 3 * HD
    NROW = 4
    VC = 2 * HD + 2
    GH = 8
    NG = H // GH
    LEAD = 12
    QH = 2
    NQ = H // QH
    SCALE = 1.0 / HD ** 0.5

    with ExitStack() as ctx:
        sb = lambda name, shape, dt=F32: ctx.enter_context(nc.sbuf_tensor("c_" + name, shape, dt))
        sem = semaphores(nc, ctx, "c_")
        wq = [sb(f"wq{i}", [P, KD, D], F32R) for i in range(2)]
        wkv = [sb(f"wkv{i}", [P, KC, 2 * D], F32R) for i in range(2)]
        wdc = [sb(f"wdc{i}", [P, KC, 2 * D], F32R) for i in range(2)]
        wo = [sb(f"wo{i}", [P, KD, D], F32R) for i in range(2)]
        lnsc = sb("lnsc", [P, NT, 2])
        kview = lambda a: a.rearrange("(k p) n -> p k n", p=P)
        split_weights(nc, "c_w", [
            (kview(Wq), wq[0][:, :, :], wq[1][:, :, :]),
            (kview(Wk), wkv[0][:, :, 0:D], wkv[1][:, :, 0:D]),
            (kview(Wv), wkv[0][:, :, D:2 * D], wkv[1][:, :, D:2 * D]),
            (kview(Wkv_dca), wdc[0][:, :, :], wdc[1][:, :, :]),
            (kview(Wo), wo[0][:, :, :], wo[1][:, :, :])])

        bqt, bkt, bvt, bvd, bo = sb("bq", [P, D]), sb("bk", [P, BT, D]), sb("bv", [P, D]), sb("bvd", [P, D]), sb("bo", [P, D])
        lnw = sb("lnw", [P, 3, 2, HD])
        ind = sb("ind", [P, BT, NROW])
        ctxb = sb("ctx", [P, BT, CD])
        xn = sb("xn", [P, BT, D])
        att = xn
        scb = sb("scb", [P, BT, 2])
        xT = [sb(f"xT{i}", [P, KD, S], F32R) for i in range(2)]
        aT = xT
        cT = [sb(f"cT{i}", [P, KC, S], F32R) for i in range(2)]
        cD = [sb(f"cD{i}", [P, KC, P], F32R) for i in range(2)]
        cen = sb("cen", [P, 4, D])
        sq = sb("sq", [P, D])
        y = sq
        sm, ss, lw = sb("sm", [P, 4, H]), sb("ss", [P, 4 * H]), sb("lw", [P, 3, 4 * H])
        aug = sb("aug", [P, 2, H, P])
        qT = sb("qT", [P, H, S], F32R)
        kT = sb("kT", [P, H, S], F32R)
        V = sb("V", [P, BT, H, VC])
        PT = sb("PT", [P, 2, BT, S])
        oT = sb("oT", [VC, 2, QH * S])
        nm = sb("nm", [P, H, 2, BT])
        nms = sb("nms", [P, BT, NROW * GH])
        nmT = sb("nmT", [NROW * GH, NG, S])
        rden = sb("rden", [P, QH * BT, 2])
        nrm = sq[:, 0:QH * BT * 2 * HD].rearrange("p (x m e) -> p x m e", m=2, e=HD)

        W = [ctx.enter_context(nc.psum_tensor(f"c_W{i}", [P, 512], F32)) for i in range(2)]
        SM = [ctx.enter_context(nc.psum_tensor(f"c_SM{i}", [P, 512], F32)) for i in range(2)]
        ST = [ctx.enter_context(nc.psum_tensor(f"c_ST{i}", [P, 512], F32)) for i in range(2)]
        O = [ctx.enter_context(nc.psum_tensor(f"c_O{i}", [P, 512], F32)) for i in range(2)]

        tables_in, cleared, consts = sem("tables_in"), sem("cleared"), sem("consts")
        ctx_loaded, xn_ready, xT_hi = sem("ctx_loaded"), sem("xn_ready"), sem("xT_hi")
        scaled, normed, pseq = sem("scaled"), sem("normed"), sem("pseq")
        aug_hi, aug_lo = [[sem(f"{n}{w}") for w in "qk"] for n in ("aug_hi", "aug_lo")]
        nms_ready = sem("nms_ready")
        max_rows = [sem(f"max_rows{g}") for g in range(NG)]
        exp_done, weighted_done, aT_hi, vseq, att_ready = [
            sem(n) for n in ("exp_done", "weighted_done", "aT_hi", "vseq", "att_ready")]
        Wf, We = [[sem(f"{n}{i}") for i in range(2)] for n in ("W_filled", "W_free")]
        SMf, SMe = [[sem(f"{n}{i}") for i in range(2)] for n in ("SM_filled", "SM_free")]
        STf = [sem(f"ST_filled{i}") for i in range(2)]
        Oe = [sem(f"O_free{i}") for i in range(2)]

        X_TR, C_TR = [0, 1], 2
        PROJ = {(0, "q"): 3, (0, "k"): 4, (0, "v"): 5, (1, "q"): 6, (1, "k"): 7, (1, "v"): 8, (1, "d"): 9}
        AUG_TR = {(t, w, i): 10 + 8 * t + 4 * (w == "k") + i for t in range(BT) for w in "qk" for i in range(4)}
        MAX_TR, O_TR = [26, 28], [27, 29, 30, 31, 32, 33, 34, 35]
        A_TR = [36, 37]
        OUT = [38, 39]
        ITEMS = 40
        X = core.X
        NORMED = [(0, "q"), (0, "k"), (1, "q"), (1, "k")]

        def rings(it):
            return Ring(Wf, We, ITEMS), Ring(SMf, SMe, H), Ring(STf, STf, H), Ring(Oe, Oe, NQ)

        def evacuate_turned(eng, it, Wr, t, w, which):
            for i in range(4):
                j = AUG_TR[t, w, i]
                if j % 2 != which:
                    continue
                eng.wait_ge(*Wr.until_filled(it, j))
                dst = (qT if w == "q" else kT)[:, 4 * i:4 * i + 4, t * P:(t + 1) * P]
                src = W[j % 2][:, :].rearrange("p (g n) -> p g n", g=4)
                if which == 0:
                    eng.activation(dst, src, ACT.Copy).then_inc(We[j % 2], 1)
                else:
                    eng.tensor_copy(dst, src).then_inc(We[j % 2], 1)

        def context_parts():
            w = W[C_TR % 2][:, :].rearrange("p (t k n) -> p t k n", t=BT, k=KC)
            return [(lambda i: cT[i][:, :, 0:P], cT[0][:, :, 0:P], w[:, 0]),
                    (lambda i: cT[i][:, :, P:MAIN], cT[0][:, :, P:MAIN], w[:, 1, :, 0:MT]),
                    (lambda i: cD[i][:, :, MT:P], cD[0][:, :, MT:P], w[:, 1, :, MT:P])]

        if True:
            with nc.Block() as blk:
                @blk.sync
                def _(eng):
                    eng.wait_ge(cleared, 2)
                    loads = [(bqt[:, :], bq), (bo[:, :], bo_d), (bvd[MT:P, :], bkv_dca[D:2 * D]),
                             (bkt[MT:P, 1, :], bkv_dca[0:D])]
                    for half, b_ in enumerate((bk, bv)):
                        v = b_.rearrange("(h s e) -> s h e", s=2, e=HD)
                        cols = slice(half * D // 2, (half + 1) * D // 2)
                        fold = lambda a: a.rearrange("p (h e) -> p h e", e=HD)
                        loads += [(fold(bkt[:, 0, cols]), v[0]), (fold(bkt[0:MT, 1, cols]), v[0]),
                                  (fold(bvt[:, cols]), v[1])]
                    for i, (a, b_) in enumerate(((qn_w, qn_b), (kn_w, kn_b))):
                        loads += [(lnw[:, i, 0, :], a), (lnw[:, i, 1, :], b_)]
                    loads += [(lnw[0:MT, 2, 0, :], kn_w), (lnw[0:MT, 2, 1, :], kn_b),
                              (lnw[MT:P, 2, 0, :], kn_dca_w), (lnw[MT:P, 2, 1, :], kn_dca_b)]
                    for dst, src in loads:
                        eng.dma_start(dst, src.partition_broadcast(dst.shape[0])).then_inc(tables_in, 16)
                    eng.wait_ge(tables_in, 16 * len(loads))

                @blk.gpsimd
                def _(eng):
                    eng.memset(bvd[:, :], 0.0).then_inc(cleared, 1)
                    eng.memset(aug[:, :, :, :], 0.0).then_inc(cleared, 1)
                    eng.memset(ind[:, :, 0:2], 1.0).then_inc(consts, 1)
                    eng.memset(ind[:, :, 2:4], 0.0).then_inc(consts, 1)
                    eng.wait_ge(consts, 2)
                    eng.affine_select(out=ind[:, 1, 0:2], in_=ind[:, 1, 0:2], compare_op=ALU.is_ge, fill=0.0,
                                      base=MT - 1, pattern=[[0, 2]], channel_multiplier=-1).then_inc(consts, 1)
                    eng.affine_select(out=ind[:, 1, 2:4], in_=ind[:, 1, 2:4], compare_op=ALU.is_ge, fill=1.0,
                                      base=MT - 1, pattern=[[0, 2]], channel_multiplier=-1).then_inc(consts, 1)

                @blk.vector
                def _(eng):
                    for i in range(2):
                        eng.memset(r32(cT[i][:, :, :]), 0.0)
                        eng.memset(r32(cD[i][:, :, :]), 0.0)
                    eng.memset(V[:, :, :, :], 0.0).then_inc(vseq, 1)
                    eng.wait_ge(vseq, 1)
                    eng.wait_ge(consts, 4)
                    for t in range(BT):
                        i = eng.tensor_copy(V[:, t, :, 2 * HD:VC],
                                            ind[:, t, 0:NROW:2].unsqueeze(1).to_broadcast([P, H, 2]))
                    i.then_inc(vseq, 1)

        block = ctx.enter_context(nc.Block())

        @block.sync
        def _(eng):
            with eng.Fori(0, B) as b:
                Wr = rings(b)[0]
                for t in range(BT):
                    eng.dma_start(ctxb[:, t, :], ctx_d[bass.ds(b, 1), t * P:(t + 1) * P, :]
                                  .rearrange("o p c -> (o p) c")).then_inc(ctx_loaded, 16)
                for g in range(NG):
                    eng.wait_ge(*Wr.until_freed(b, MAX_TR[g]))
                    for r in range(NROW):
                        eng.dma_start(r32(qT[MAXROW + r:MAXROW + r + 1, GH * g:GH * (g + 1), :]),
                                      nmT[r * GH:(r + 1) * GH, g, :]).then_inc(max_rows[g], 16)

        @block.gpsimd
        def _(eng):
            with eng.Fori(0, B) as b:
                Wr = rings(b)[0]
                c = Count(b * 4)
                for n, (t, w) in enumerate(NORMED):
                    a = "qk".index(w)
                    i = 0 if w == "q" else 1 + t
                    d = cen[:, n, :].rearrange("p (h e) -> p h e", h=H)
                    bc = lambda v: v.unsqueeze(1).to_broadcast([P, H, HD])
                    eng.wait_ge(scaled, b * 4 + n + 1)
                    eng.tensor_tensor(d, d, bc(lnw[:, i, 0, :]), ALU.mult).then_inc(pseq, c.inc())
                    eng.wait_ge(pseq, c.now)
                    eng.tensor_tensor(d, d, bc(lnw[:, i, 1, :]), ALU.add).then_inc(normed, 1)
                    lo = LO_HI if a == 0 else HD
                    eng.wait_ge(aug_hi[a], (b * BT + t + 1) * 2)
                    if w == "k":
                        flags = ind[:, t, :].unsqueeze(1).to_broadcast([P, H, NROW])
                        eng.tensor_tensor(aug[:, 1, :, MAXROW:MAXROW + NROW], flags, flags, ALU.mult)
                    eng.tensor_tensor(aug[:, a, :, lo:lo + HD], d, aug[:, a, :, 0:HD],
                                      ALU.subtract).then_inc(aug_lo[a], 1)

        @block.vector
        def _(eng):
            st = PT[:, 0, 0, 0:6 * NT].rearrange("p (t s) -> p t s", s=6)
            llw = PT[:, 0, 1, 0:5 * NT].rearrange("p (s t) -> p s t", t=NT)
            c = Count(2)
            layer_norm_scales(eng, vseq, c, X, st, llw, lnsc)
            start = c.now
            PER = 1 + 4 * 5 + 1 + 12 + NG + NQ * 2 - 1 + 2
            with eng.Fori(0, B) as b:
                c = Count(b * PER + start)
                Wr, SMr, STr, Or = rings(b)
                eng.wait_ge(vseq, c.now)
                eng.tensor_copy(scb[:, :, :], lnsc[:, bass.ds(2 * b, 2), :]).then_inc(vseq, c.inc())
                eng.wait_ge(vseq, c.now)
                for t in range(BT):
                    eng.tensor_scalar(xn[:, t, :], X[:, bass.ds(2 * b + t, 1), :].rearrange("p o d -> p (o d)"),
                                      scb[:, t, 0:1], scb[:, t, 1:2], ALU.mult, ALU.add).then_inc(xn_ready, 1)
                for t in range(BT):
                    eng.wait_ge(xT_hi, b * 3 + t + 1)
                    eng.tensor_tensor(xT[1][:, :, t * P:(t + 1) * P],
                                      W[X_TR[t] % 2][:, :].rearrange("p (k n) -> p k n", k=KD),
                                      r32(xT[0][:, :, t * P:(t + 1) * P]), ALU.subtract).then_inc(We[X_TR[t] % 2], 1)
                eng.wait_ge(xT_hi, b * 3 + 3)
                for dst, hi, src in context_parts():
                    i = eng.tensor_tensor(dst(1), src, r32(hi), ALU.subtract)
                i.then_inc(We[C_TR % 2], 1)

                def values(t, w):
                    j = PROJ[t, w]
                    eng.wait_ge(*Wr.until_filled(b, j))
                    r0, r1 = (0, P if t == 0 else MT) if w == "v" else (P - 32, P)
                    at = 0 if w == "v" else HD
                    table = bvt if w == "v" else bvd
                    hv = lambda a: a.rearrange("p (h e) -> p h e", h=H)
                    eng.tensor_tensor(V[r0:r1, t, :, at:at + HD], hv(W[j % 2][r0:r1, :]), hv(table[r0:r1, :]),
                                      ALU.add).then_inc(We[j % 2], 1)

                for n, (t, w) in enumerate(NORMED):
                    j = PROJ[t, w]
                    d = cen[:, n, :]
                    dh = d.rearrange("p (h e) -> p h e", h=H)
                    eng.wait_ge(*Wr.until_filled(b, j))
                    eng.tensor_tensor(d, W[j % 2][:, :], bqt[:, :] if w == "q" else bkt[:, t, :],
                                      ALU.add).then_inc(We[j % 2], 1)
                    eng.wait_ge(*Wr.until_freed(b, j))
                    eng.tensor_reduce(sm[:, n, :], dh, AX.X, ALU.add).then_inc(vseq, c.inc())
                    eng.wait_ge(vseq, c.now)
                    eng.tensor_scalar(sm[:, n, :], sm[:, n, :], 1.0 / HD, None, ALU.mult).then_inc(vseq, c.inc())
                    eng.wait_ge(vseq, c.now)
                    eng.tensor_tensor(dh, dh, sm[:, n, :].unsqueeze(2).to_broadcast([P, H, HD]),
                                      ALU.subtract).then_inc(vseq, c.inc())
                    eng.wait_ge(vseq, c.now)
                    eng.tensor_tensor(sq[:, :], d, d, ALU.mult).then_inc(vseq, c.inc())
                    eng.wait_ge(vseq, c.now)
                    eng.tensor_reduce(ss[:, n * H:(n + 1) * H], sq[:, :].rearrange("p (h e) -> p h e", h=H),
                                      AX.X, ALU.add).then_inc(vseq, c.inc())
                    if w == "k":
                        values(t, "v")
                        if t == 1:
                            values(1, "d")
                eng.wait_ge(vseq, c.now)
                eng.tensor_scalar(ss[:, :], ss[:, :], 1.0 / HD, 1e-6, ALU.mult, ALU.add).then_inc(vseq, c.inc())
                rsqrt_steps(eng, vseq, c, ss[:, :], lw[:, 0, :], lw[:, 1, :], lw[:, 2, :])
                eng.wait_ge(vseq, c.now)
                for n in range(4):
                    dh = cen[:, n, :].rearrange("p (h e) -> p h e", h=H)
                    eng.tensor_tensor(dh, dh, lw[:, 0, n * H:(n + 1) * H].unsqueeze(2).to_broadcast([P, H, HD]),
                                      ALU.mult).then_inc(scaled, 1)
                for t in range(BT):
                    for w in "qk":
                        evacuate_turned(eng, b, Wr, t, w, 1)

                def top(h):
                    eng.wait_ge(*SMr.until_filled(b, h))
                    v = SM[h % 2][:, :].rearrange("p (t k) -> p t k", t=BT)
                    eng.tensor_reduce(nm[:, h, 0, :], v[:, :, 0:MAIN], AX.X, ALU.max, negate=True)
                    eng.tensor_reduce(nm[:, h, 1, :], v[:, :, MAIN:S], AX.X, ALU.max,
                                      negate=True).then_inc(SMe[h % 2], 1)
                    if h % GH == GH - 1:
                        g = h // GH
                        for i in (h - 1, h):
                            eng.wait_ge(*SMr.until_freed(b, i))
                        if g:
                            eng.wait_ge(*Wr.until_freed(b, MAX_TR[g - 1]))
                        src = nm[:, g * GH:(g + 1) * GH, :, :].rearrange("p a m t -> p t m a")
                        dst = nms[:, :, :].rearrange("p t (m j a) -> p t m j a", m=2, j=2)
                        for t in range(BT):
                            i = eng.tensor_copy(dst[:, t, :, 0, :].bitcast(F32R), src[:, t])
                        i.then_inc(vseq, c.inc())
                        eng.wait_ge(vseq, c.now)
                        for t in range(BT):
                            i = eng.tensor_tensor(dst[:, t, :, 1, :], src[:, t], dst[:, t, :, 0, :], ALU.subtract)
                        i.then_inc(nms_ready, 1)

                def normalise(q):
                    j = O_TR[q]
                    o = W[j % 2][:, 0:QH * BT * VC].rearrange("p (x e) -> p x e", e=VC)
                    eng.wait_ge(*Wr.until_filled(b, j))
                    eng.wait_ge(vseq, c.now)
                    if q:
                        eng.wait_ge(*Wr.until_freed(b, O_TR[q - 1]))
                    eng.reciprocal(rden[:, :, :], o[:, :, 2 * HD:VC]).then_inc(vseq, c.inc())
                    eng.wait_ge(vseq, c.now)
                    eng.tensor_tensor(nrm[:, :, :, :], o[:, :, 0:2 * HD].rearrange("p x (m e) -> p x m e", m=2),
                                      rden[:, :, :].unsqueeze(3).to_broadcast([P, QH * BT, 2, HD]),
                                      ALU.mult).then_inc(We[j % 2], 1)
                    eng.wait_ge(*Wr.until_freed(b, j))
                    dst = att[:, :, q * QH * HD:(q + 1) * QH * HD].rearrange("p t (h e) -> p h t e", h=QH)
                    nv = nrm[:, :, :, :].rearrange("p (h t) m e -> p h t m e", h=QH)
                    i = eng.tensor_tensor(dst, nv[:, :, :, 0, :], nv[:, :, :, 1, :], ALU.add)
                    if q == NQ - 1:
                        i.then_inc(att_ready, 1)
                    else:
                        i.then_inc(vseq, c.inc())

                for h in range(LEAD):
                    top(h)
                for h in range(H):
                    if h + LEAD < H:
                        top(h + LEAD)
                    if h % 2 == 1 and h >= 3:
                        normalise((h - 3) // 2)
                normalise(NQ - 1)
                for t in range(BT):
                    eng.wait_ge(aT_hi, b * BT + t + 1)
                    eng.tensor_tensor(aT[1][:, :, t * P:(t + 1) * P],
                                      W[A_TR[t] % 2][:, :].rearrange("p (k n) -> p k n", k=KD),
                                      r32(aT[0][:, :, t * P:(t + 1) * P]), ALU.subtract).then_inc(We[A_TR[t] % 2], 1)
                for t in range(BT):
                    j = OUT[t]
                    xx = X[:, bass.ds(2 * b + t, 1), :].rearrange("p o d -> p (o d)")
                    eng.wait_ge(*Wr.until_filled(b, j))
                    eng.wait_ge(vseq, c.now)
                    eng.tensor_tensor(y[:, :], W[j % 2][:, :], bo[:, :], ALU.add).then_inc(We[j % 2], 1)
                    eng.wait_ge(*Wr.until_freed(b, j))
                    eng.scalar_tensor_tensor(out=xx, in0=y[:, :], scalar=gate, in1=xx,
                                             op0=ALU.mult, op1=ALU.add).then_inc(vseq, c.inc())
                assert c.n == PER, (c.n, PER)

        @block.scalar
        def _(eng):
            with eng.Fori(0, B) as b:
                Wr, SMr, STr, Or = rings(b)
                for t in range(BT):
                    eng.wait_ge(*Wr.until_filled(b, X_TR[t]))
                    eng.activation(xT[0][:, :, t * P:(t + 1) * P],
                                   W[X_TR[t] % 2][:, :].rearrange("p (k n) -> p k n", k=KD),
                                   ACT.Copy).then_inc(xT_hi, 1)
                eng.wait_ge(*Wr.until_filled(b, C_TR))
                for dst, _, src in context_parts():
                    i = eng.activation(dst(0), src, ACT.Copy)
                i.then_inc(xT_hi, 1)

                def rounded(n):
                    t, w = NORMED[n]
                    a = "qk".index(w)
                    heads = cen[:, n, :].rearrange("p (h e) -> p h e", e=HD)
                    eng.wait_ge(normed, b * 4 + n + 1)
                    if t:
                        eng.wait_ge(*Wr.until_filled(b, AUG_TR[t - 1, w, 3]))
                    for at in (0, HD if a == 0 else LO_HI):
                        eng.activation(aug[:, a, :, at:at + HD].bitcast(F32R), heads, ACT.Copy).then_inc(aug_hi[a], 1)

                rounded(0)
                rounded(1)
                evacuate_turned(eng, b, Wr, 0, "q", 0)
                rounded(2)
                evacuate_turned(eng, b, Wr, 0, "k", 0)
                rounded(3)
                evacuate_turned(eng, b, Wr, 1, "q", 0)
                evacuate_turned(eng, b, Wr, 1, "k", 0)

                def maxima(g):
                    j = MAX_TR[g]
                    eng.wait_ge(*Wr.until_filled(b, j))
                    eng.activation(nmT[:, g, :], W[j % 2][0:NROW * GH, 0:S], ACT.Copy).then_inc(We[j % 2], 1)

                def turned_outputs(q):
                    eng.wait_ge(weighted_done, b * H + (q + 1) * QH)
                    if q >= 2:
                        eng.wait_ge(*Wr.until_filled(b, O_TR[q - 2]))
                    eng.activation(oT[:, q % 2, :], O[q % 2][0:VC, :], ACT.Copy).then_inc(Oe[q % 2], 1)

                maxima(0)
                for h in range(H):
                    eng.wait_ge(*STr.until_filled(b, h))
                    if h >= 2:
                        eng.wait_ge(weighted_done, b * H + h - 1)
                    eng.activation(PT[:, h % 2, :, :].rearrange("p t s -> p (t s)"), ST[h % 2][:, :], ACT.Exp,
                                   scale=SCALE).then_inc(exp_done, 1)
                    if h == 5:
                        maxima(1)
                    if h % 2 == 0 and h >= 2:
                        turned_outputs((h - 2) // 2)
                turned_outputs(NQ - 1)
                for t in range(BT):
                    eng.wait_ge(*Wr.until_filled(b, A_TR[t]))
                    eng.activation(aT[0][:, :, t * P:(t + 1) * P],
                                   W[A_TR[t] % 2][:, :].rearrange("p (k n) -> p k n", k=KD),
                                   ACT.Copy).then_inc(aT_hi, 1)

        @block.tensor
        def _(eng):
            for s_ in We + SMe + Oe:
                eng.sem_inc(s_, 1)
            with eng.Fori(0, B) as b:
                Wr, SMr, STr, Or = rings(b)

                def turn(j, srcs):
                    eng.wait_ge(*Wr.until_free(b, j))
                    at = 0
                    for s in srcs:
                        k = s.shape[0]
                        m = eng.transpose(W[j % 2][0:s.shape[1], at:at + k], s, core.ident[0:k, 0:k])
                        at += k
                    m.then_inc(Wf[j % 2], 1)

                def product(j, terms):
                    eng.wait_ge(*Wr.until_free(b, j))
                    total, n = 3 * sum(k for _, _, k in terms), 0
                    for lhs, rhs, k in terms:
                        for x_, w_ in ((0, 0), (0, 1), (1, 0)):
                            for i in range(k):
                                m = eng.matmul(W[j % 2][:, :], lhs(x_, i), rhs(w_, i), start=(n == 0),
                                               stop=(n == total - 1))
                                n += 1
                    m.then_inc(Wf[j % 2], 1)

                tok = lambda a, t: (lambda x_, i: a[x_][:, i, t * P:(t + 1) * P])
                cols = lambda w, c0: (lambda w_, i: w[w_][:, i, c0:c0 + D])
                heads = lambda s: (lambda w_, i: wkv[w_][:, i, :].rearrange("p (h s e) -> p s h e", s=2, e=HD)[:, s])
                for t in range(BT):
                    eng.wait_ge(xn_ready, b * BT + t + 1)
                    turn(X_TR[t], [xn[:, t, k * P:(k + 1) * P] for k in range(KD)])
                eng.wait_ge(ctx_loaded, (b + 1) * 32)
                turn(C_TR, [ctxb[:, t, k * P:(k + 1) * P] for t in range(BT) for k in range(KC)])
                eng.wait_ge(*Wr.until_freed(b, C_TR))
                eng.wait_ge(*Wr.until_freed(b, X_TR[1]))
                product(PROJ[0, "q"], [(tok(xT, 0), cols(wq, 0), KD)])
                product(PROJ[0, "k"], [(tok(cT, 0), heads(0), KC)])
                product(PROJ[0, "v"], [(tok(cT, 0), heads(1), KC)])
                product(PROJ[1, "q"], [(tok(xT, 1), cols(wq, 0), KD)])
                product(PROJ[1, "k"], [(tok(cT, 1), heads(0), KC), (tok(cD, 0), cols(wdc, 0), KC)])
                product(PROJ[1, "v"], [(tok(cT, 1), heads(1), KC)])
                product(PROJ[1, "d"], [(tok(cD, 0), cols(wdc, D), KC)])
                for t in range(BT):
                    for a, w in enumerate("qk"):
                        eng.wait_ge(aug_lo[a], b * BT + t + 1)
                        for i in range(4):
                            turn(AUG_TR[t, w, i], [aug[:, a, h, :] for h in range(4 * i, 4 * i + 4)])
                for i in (2, 3):
                    eng.wait_ge(*Wr.until_freed(b, AUG_TR[1, "k", i]))

                def scores_for_max(h):
                    eng.wait_ge(*SMr.until_free(b, h))
                    for t in range(BT):
                        m = eng.matmul(SM[h % 2][:, t * S:(t + 1) * S], qT[0:MAXROW, h, t * P:(t + 1) * P],
                                       kT[0:MAXROW, h, :], start=True, stop=True)
                    m.then_inc(SMf[h % 2], 1)

                def turn_maxima(g):
                    eng.wait_ge(nms_ready, b * NG + g + 1)
                    turn(MAX_TR[g], [nms[:, t, :] for t in range(BT)])

                def scores(h):
                    if h % GH == 0:
                        eng.wait_ge(max_rows[h // GH], (b + 1) * 16 * NROW)
                    if h >= 2:
                        eng.wait_ge(exp_done, b * H + h - 1)
                    for t in range(BT):
                        m = eng.matmul(ST[h % 2][:, t * S:(t + 1) * S], kT[0:MAXROW + NROW, h, t * P:(t + 1) * P],
                                       qT[0:MAXROW + NROW, h, :], start=True, stop=True)
                    m.then_inc(STf[h % 2], 1)

                def weighted(h):
                    q = h // QH
                    if h % QH == 0:
                        eng.wait_ge(*Or.until_free(b, q))
                    eng.wait_ge(exp_done, b * H + h + 1)
                    for k in range(BT):
                        m = eng.matmul(O[q % 2][0:VC, (h % QH) * S:(h % QH + 1) * S], V[:, k, h, :], PT[:, h % 2, k, :],
                                       start=(k == 0), stop=(k == BT - 1))
                    m.then_inc(weighted_done, 1)

                def turn_outputs(q):
                    eng.wait_ge(*Or.until_freed(b, q))
                    turn_small(O_TR[q], [oT[:, q % 2, i * P:(i + 1) * P] for i in range(QH * BT)])

                def turn_small(j, srcs):
                    eng.wait_ge(*Wr.until_free(b, j))
                    for i, s in enumerate(srcs):
                        m = eng.transpose(W[j % 2][:, i * VC:(i + 1) * VC], s, core.ident[0:VC, 0:VC])
                    m.then_inc(Wf[j % 2], 1)

                for h in range(LEAD):
                    scores_for_max(h)
                    if h == GH + 1:
                        turn_maxima(0)
                for h in range(H):
                    scores(h)
                    if h + LEAD < H:
                        scores_for_max(h + LEAD)
                    if h:
                        weighted(h - 1)
                    if h == 5:
                        turn_maxima(1)
                    if h % 2 == 1 and h >= 3:
                        turn_outputs((h - 3) // 2)
                weighted(H - 1)
                turn_outputs(NQ - 1)
                eng.wait_ge(att_ready, b + 1)
                for t in range(BT):
                    turn(A_TR[t], [att[:, t, k * P:(k + 1) * P] for k in range(KD)])
                for t in range(BT):
                    eng.wait_ge(*Wr.until_freed(b, A_TR[t]))
                for t in range(BT):
                    product(OUT[t], [(tok(aT, t), cols(wo, 0), KD)])


def scatter_tables(nc, core, atoms, eaw, importance, mask_idx, table):
    E, A = eaw.shape
    NS = mask_idx.shape[0]
    C = NS // P
    H = D
    NP = 3
    HALF = C // 2
    with ExitStack() as ctx:
        sb = lambda n, shape, dt=F32: ctx.enter_context(nc.sbuf_tensor("st_" + n, shape, dt))
        sem = semaphores(nc, ctx, "st_")
        zeros = sb("zeros", [P, 4096])
        row_i, row_f = sb("row_i", [P, NS], I32), sb("row_f", [P, C, P])
        idx_i, idx_f = sb("idx_i", [P, C], I32), sb("idx_f", [P, C])
        at_col, at_row, addr, dump, addr_u = (sb("at_col", [P, C], I32), sb("at_row", [P, C], I32), sb("addr", [P, C]),
                                              sb("dump", [P, C]), sb("addr_u", [P, C], U32))
        dump_i = sb("dump_i", [P, C], I32)
        eq = sb("eq", [P, 2, C, P], BF16)
        before, eqm = sb("before", [P, P], BF16), sb("eqm", [P, 2, P], BF16)
        ea, at_ = sb("ea", [E, A]), sb("atoms", [A, NS])
        imp = sb("imp", [E, NS])
        m1, s1 = sb("m1", [E, 1]), sb("s1", [E, 1])
        eaT = sb("eaT", [A, E])
        sig = sb("sig", [P, C * E])
        w, rest = sb("w", [P, C * E]), sb("rest", [P, C * E])
        parts = sb("parts", [P, C, NP * E + 1], BF16)
        total = sb("total", [P, C, E])
        flag = sb("flag", [P, C])
        tb = ctx.enter_context(nc.psum_tensor("st_tb", [A, E], F32))
        delta = ctx.enter_context(nc.psum_tensor("st_delta", [P, C * E], F32))
        sigT = ctx.enter_context(nc.psum_tensor("st_sigT", [P, C * E], F32))
        acc = [ctx.enter_context(nc.psum_tensor(f"st_acc{i}", [P, HALF * (NP * E + 1)], F32)) for i in range(2)]
        loaded, idx_in, imp_in, atoms_in, zeroed, scattered = [
            sem(n) for n in ("loaded", "idx_in", "imp_in", "atoms_in", "zeroed", "scattered")]
        consts, vseq, aseq, eq_ready, eq_used, parts_ready, pe_small, summed, rows_ready, acc_zero = [
            sem(n) for n in ("consts", "vseq", "aseq", "eq_ready", "eq_used", "parts_ready", "pe_small", "summed",
                             "rows_ready", "acc_zero")]
        block = ctx.enter_context(nc.Block())
        ZD = H * H * E // (P * 4096)

        @block.sync
        def _(eng):
            eng.dma_start(ea[:, :], eaw).then_inc(loaded, 16)
            eng.dma_start(idx_i[:, :], mask_idx.rearrange("(p c) -> p c", p=P)).then_inc(idx_in, 16)
            eng.dma_start(row_i[:, :], mask_idx.partition_broadcast(P)).then_inc(idx_in, 16)
            eng.dma_start(imp[:, :], importance).then_inc(imp_in, 16)
            eng.dma_start(at_[:, :], atoms).then_inc(atoms_in, 16)
            eng.wait_ge(consts, 1)
            flat = table[0:H * H, :].rearrange("(p q r) e -> p q (r e)", p=P, q=ZD)
            for q in range(ZD):
                eng.dma_start(flat[:, q, :], zeros[:, :]).then_inc(zeroed, 16)
            eng.wait_ge(zeroed, 16 * ZD)

        @block.gpsimd
        def _(eng):
            eng.memset(zeros[:, :], 0.0).then_inc(consts, 1)
            eng.memset(before[:, :], 1.0).then_inc(consts, 1)
            eng.wait_ge(consts, 2)
            eng.affine_select(out=before[:, :], in_=before[:, :], compare_op=ALU.is_gt, fill=0.0, base=0,
                              pattern=[[1, P]], channel_multiplier=-1).then_inc(consts, 1)
            eng.iota(dump_i[:, :], pattern=[[1, C]], base=H * H, channel_multiplier=C).then_inc(consts, 1)
            eng.wait_ge(zeroed, 16 * ZD)
            eng.wait_ge(rows_ready, 1)
            for c in range(C):
                eng.indirect_dma_start(out=table, out_offset=bass.IndirectOffsetOnAxis(ap=addr_u[:, c:c + 1], axis=0),
                                       in_=total[:, c, :], in_offset=None).then_inc(scattered, 16)
            eng.wait_ge(scattered, 16 * C)

        @block.scalar
        def _(eng):
            eng.wait_ge(vseq, 1)
            eng.activation(ea[:, :], ea[:, :], ACT.Exp, bias=m1[:, 0:1], accum_out=s1[:, 0:1]).then_inc(aseq, 1)
            eng.wait_ge(imp_in, 16)
            eng.activation(imp[:, :], imp[:, :], ACT.Sigmoid).then_inc(aseq, 1)
            eng.wait_ge(pe_small, 1)
            eng.activation(eaT[:, :], tb[:, :], ACT.Copy).then_inc(aseq, 1)
            eng.wait_ge(pe_small, 2)
            eng.activation(sig[:, :], sigT[:, :], ACT.Copy).then_inc(aseq, 1)

        @block.vector
        def _(eng):
            c = Count()
            eng.wait_ge(loaded, 16)
            eng.tensor_reduce(m1[:, :], ea[:, :], AX.X, ALU.max, negate=True).then_inc(vseq, c.inc())
            eng.wait_ge(aseq, 1)
            eng.reciprocal(m1[:, :], s1[:, :]).then_inc(vseq, c.inc())
            eng.wait_ge(vseq, c.now)
            eng.tensor_scalar(ea[:, :], ea[:, :], m1[:, 0:1], None, ALU.mult).then_inc(vseq, c.inc())
            for i in range(2):
                eng.memset(acc[i][:, :], 0.0).then_inc(acc_zero, 1)
            eng.wait_ge(idx_in, 32)
            eng.tensor_copy(idx_f[:, :], idx_i[:, :]).then_inc(vseq, c.inc())
            eng.tensor_copy(row_f[:, :, :], row_i[:, :].rearrange("p (q c) -> p c q", c=C)).then_inc(vseq, c.inc())
            eng.tensor_scalar(at_col[:, :], idx_i[:, :], H - 1, 9, ALU.bitwise_and,
                              ALU.logical_shift_left).then_inc(vseq, c.inc())
            eng.tensor_scalar(at_row[:, :], idx_i[:, :], 9, None, ALU.logical_shift_right).then_inc(vseq, c.inc())
            eng.wait_ge(vseq, c.now)
            eng.tensor_tensor(addr[:, :], at_col[:, :], at_row[:, :], ALU.add).then_inc(vseq, c.inc())
            eng.wait_ge(consts, 4)
            eng.tensor_copy(dump[:, :], dump_i[:, :]).then_inc(vseq, c.inc())
            eng.wait_ge(vseq, c.now)
            eng.tensor_tensor(dump[:, :], dump[:, :], addr[:, :], ALU.subtract).then_inc(vseq, c.inc())
            eng.wait_ge(aseq, 4)
            eng.wait_ge(pe_small, 3)
            eng.tensor_tensor(w[:, :], delta[:, :], sig[:, :], ALU.mult).then_inc(vseq, c.inc())
            eng.memset(parts[:, :, NP * E:NP * E + 1], 1.0).then_inc(vseq, c.inc())
            cur = w
            for i in range(NP):
                pv = parts[:, :, i * E:(i + 1) * E]
                cv = cur[:, :].rearrange("p (c e) -> p c e", e=E)
                eng.wait_ge(vseq, c.now)
                eng.tensor_copy(pv, cv).then_inc(vseq, c.inc())
                if i < NP - 1:
                    eng.wait_ge(vseq, c.now)
                    eng.tensor_tensor(rest[:, :].rearrange("p (c e) -> p c e", e=E), cv, pv,
                                      ALU.subtract).then_inc(vseq, c.inc())
                    cur = rest
            eng.wait_ge(vseq, c.now)
            for a in range(C):
                if a >= 2:
                    eng.wait_ge(eq_used, a - 1)
                eng.tensor_scalar(eq[:, a % 2].rearrange("p c q -> p (c q)"),
                                  row_f[:, :, :].rearrange("p c q -> p (c q)"), idx_f[:, a:a + 1], None,
                                  ALU.is_equal).then_inc(vseq, c.inc())
                eng.wait_ge(vseq, c.now)
                eng.tensor_tensor(eqm[:, a % 2, :], eq[:, a % 2, a, :], before[:, :], ALU.mult).then_inc(eq_ready, 1)
            eng.wait_ge(summed, 1)
            for i in range(2):
                av = acc[i][:, :].rearrange("p (c m) -> p c m", m=NP * E + 1)
                tv = total[:, i * HALF:(i + 1) * HALF, :]
                eng.tensor_copy(tv, av[:, :, 0:E]).then_inc(vseq, c.inc())
                for q in (1, 2):
                    eng.wait_ge(vseq, c.now)
                    eng.tensor_tensor(tv, tv, av[:, :, q * E:(q + 1) * E], ALU.add).then_inc(vseq, c.inc())
                eng.tensor_scalar(flag[:, i * HALF:(i + 1) * HALF], av[:, :, NP * E], 0.5, None,
                                  ALU.is_gt).then_inc(vseq, c.inc())
            eng.wait_ge(vseq, c.now)
            eng.tensor_tensor(dump[:, :], dump[:, :], flag[:, :], ALU.mult).then_inc(vseq, c.inc())
            eng.wait_ge(vseq, c.now)
            eng.tensor_tensor(addr_u[:, :], addr[:, :], dump[:, :], ALU.add).then_inc(rows_ready, 1)

        @block.tensor
        def _(eng):
            eng.wait_ge(vseq, 3)
            eng.transpose(tb[:, :], ea[:, :], core.ident[0:E, 0:E]).then_inc(pe_small, 1)
            eng.wait_ge(aseq, 2)
            for c in range(C):
                m = eng.transpose(sigT[:, c * E:(c + 1) * E], imp[:, c::C], core.ident[0:E, 0:E])
            m.then_inc(pe_small, 1)
            eng.wait_ge(atoms_in, 16)
            eng.wait_ge(aseq, 3)
            for c in range(C):
                m = eng.matmul(delta[:, c * E:(c + 1) * E], at_[:, c::C], eaT[:, :], start=True, stop=True)
            m.then_inc(pe_small, 1)
            eng.wait_ge(acc_zero, 2)
            N = NP * E + 1
            for a in range(C):
                eng.wait_ge(eq_ready, a + 1)
                for b in range(C):
                    n = N if a < b else N - 1
                    o = acc[b // HALF][:, (b % HALF) * N:(b % HALF) * N + n]
                    m = eng.matmul(o, eq[:, a % 2, b, :], parts[:, a, 0:n], start=False, stop=(a == C - 1),
                                   skip_group_check=True)
                b = a
                m = eng.matmul(acc[b // HALF][:, (b % HALF) * N + N - 1:(b % HALF) * N + N], eqm[:, a % 2, :],
                               parts[:, a, N - 1:N], start=False, stop=(a == C - 1), skip_group_check=True)
                m.then_inc(eq_used if a < C - 1 else summed, 1)


def masked_router(nc, core, xT, gw, E, gt):
    with ExitStack() as ctx:
        sb = lambda n, shape, dt=F32: ctx.enter_context(nc.sbuf_tensor("dr_" + n, shape, dt))
        sem = semaphores(nc, ctx, "dr_")
        p, rank, ex = sb("p", [P, NT, E]), sb("rank", [P, NT, E]), sb("ex", [P, NT, E])
        m1, s1 = sb("m1", [P, NT]), sb("s1", [P, NT])
        tri, g1, eq = sb("tri", [P, E, E]), sb("g1", [P, NT, E, E], BF16), sb("eq", [P, NT, E, E], BF16)
        bank = ctx.enter_context(nc.psum_tensor("dr_bank", [P, NT * E], F32))
        logits, shifted, exped, vseq, consts = [sem(n) for n in ("logits", "shifted", "exped", "vseq", "consts")]
        block = ctx.enter_context(nc.Block())
        bc = lambda a: a.unsqueeze(2).to_broadcast([P, NT, E])

        @block.gpsimd
        def _(eng):
            eng.memset(tri[:, :, :], 1.0).then_inc(consts, 1)
            eng.wait_ge(consts, 1)
            eng.affine_select(out=tri[:, :, :], in_=tri[:, :, :], compare_op=ALU.is_gt, fill=0.0, base=0,
                              pattern=[[1, E], [-1, E]], channel_multiplier=0).then_inc(consts, 1)

        @block.tensor
        def _(eng):
            router_logits(eng, bank, xT, gw, E, logits)

        @block.scalar
        def _(eng):
            eng.wait_ge(shifted, 1)
            eng.activation(ex[:, :, :], ex[:, :, :], ACT.Exp).then_inc(exped, 1)

        @block.vector
        def _(eng):
            c = Count()
            eng.wait_ge(logits, 1)
            eng.tensor_scalar(p[:, :, :], bank[:, :].rearrange("p (t e) -> p t e", t=NT), 50.0, -50.0,
                              ALU.min, ALU.max).then_inc(vseq, c.inc())
            eng.wait_ge(vseq, c.now)
            eng.tensor_reduce(m1[:, :], p[:, :, :], AX.X, ALU.max).then_inc(vseq, c.inc())
            eng.wait_ge(vseq, c.now)
            eng.tensor_tensor(ex[:, :, :], p[:, :, :], bc(m1[:, :]), ALU.subtract).then_inc(shifted, 1)
            eng.wait_ge(consts, 2)
            chosen(eng, vseq, c, p[:, :, :], E, 2, tri[:, :, :], g1[:, :, :, :], eq[:, :, :, :], rank[:, :, :])
            eng.wait_ge(exped, 1)
            eng.wait_ge(vseq, c.now)
            eng.scalar_tensor_tensor(out=p[:, :, :], in0=rank[:, :, :], scalar=1.5, in1=ex[:, :, :],
                                     op0=ALU.is_lt, op1=ALU.mult).then_inc(vseq, c.inc())
            eng.wait_ge(vseq, c.now)
            eng.tensor_reduce(s1[:, :], p[:, :, :], AX.X, ALU.add).then_inc(vseq, c.inc())
            eng.wait_ge(vseq, c.now)
            eng.reciprocal(m1[:, :], s1[:, :]).then_inc(vseq, c.inc())
            eng.wait_ge(vseq, c.now)
            eng.tensor_scalar(m1[:, :], m1[:, :], core.gates[:, 3:4], None, ALU.mult).then_inc(vseq, c.inc())
            eng.wait_ge(vseq, c.now)
            eng.tensor_tensor(gt[:, :, :], p[:, :, :], bc(m1[:, :]), ALU.mult)


def masked_ffn(nc, core, gate_w, W, table, out):
    E = gate_w.shape[0]
    with ExitStack() as ctx:
        sb = lambda n, shape, dt=F32: ctx.enter_context(nc.sbuf_tensor("d_" + n, shape, dt))
        sem = semaphores(nc, ctx, "d_")
        xT = [sb(f"xT{i}", [P, KD, T], F32R) for i in range(2)]
        gt = sb("gt", [P, NT, E])
        turned_tokens(nc, core, "dt_", xT)
        with ExitStack() as c2:
            gw = [c2.enter_context(nc.sbuf_tensor(f"d_gw{i}", [P, KD, E], F32R)) for i in range(2)]
            turned_rows(nc, core, "dg_", gate_w, E, gw[0][:, :, :], gw[1][:, :, :])
            masked_router(nc, core, xT, gw, E, gt)
        WT = sb("WT", [P, KD, D])
        with ExitStack() as c2:
            Wraw = c2.enter_context(nc.sbuf_tensor("d_Wraw", [P, KD, D], F32))
            wb = [c2.enter_context(nc.psum_tensor(f"d_wb{i}", [P, D], F32)) for i in range(KD)]
            sem2 = semaphores(nc, c2, "dw_")
            w_in, w_turned = sem2("in"), sem2("turned")
            block = c2.enter_context(nc.Block())

            @block.sync
            def _(eng):
                eng.dma_start(Wraw[:, :, :], W.rearrange("(r p) c -> p r c", p=P)).then_inc(w_in, 16)

            @block.tensor
            def _(eng):
                eng.wait_ge(w_in, 16)
                for k in range(KD):
                    for r in range(KD):
                        m = eng.transpose(wb[k][:, r * P:(r + 1) * P], Wraw[:, r, k * P:(k + 1) * P], core.ident[:, :])
                    m.then_inc(w_turned, 1)

            @block.scalar
            def _(eng):
                for k in range(KD):
                    eng.wait_ge(w_turned, k + 1)
                    eng.activation(WT[:, k, :], wb[k][:, :], ACT.Copy)

        M = sb("M", [P, KD, D, E])
        mh = [sb(f"mh{i}", [P, KD, D], F32R) for i in range(2)]
        ml = [sb(f"ml{i}", [P, KD, D], F32R) for i in range(2)]
        gb = sb("gb", [P, 2, NT])
        NBANK = 8
        Y = [ctx.enter_context(nc.psum_tensor(f"d_Y{i}", [P, D], F32)) for i in range(NBANK)]
        M_in = [sem(f"M_in{k}") for k in range(KD)]
        stored = sem("stored")
        summed, m_hi, m_lo, y_done, y_free, g_ready = [
            sem(n) for n in ("summed", "m_hi", "m_lo", "y_done", "y_free", "g_ready")]
        block = ctx.enter_context(nc.Block())
        of = out.rearrange("b (t p) d -> p (b t) d", p=P)

        @block.sync
        def _(eng):
            for k in range(KD):
                eng.dma_start(M[:, k].rearrange("p r e -> p (r e)"),
                              table[k * P * D:(k + 1) * P * D, :].rearrange("(p r) e -> p (r e)", p=P))\
                   .then_inc(M_in[k], 16)
            for q in range(4):
                eng.wait_ge(y_free, NBANK + NT * (E - 1) + 4 * (q + 1))
                eng.dma_start(of[:, 4 * q:4 * q + 4, :], core.X[:, 4 * q:4 * q + 4, :]).then_inc(stored, 16)
            eng.wait_ge(stored, 64)

        @block.vector
        def _(eng):
            eng.sem_inc(y_free, NBANK)

            def prepare(e, s, first):
                mv = M[:, :, :, bass.ds(e, 1)].rearrange("p k r o -> p k (r o)")
                if not first:
                    eng.wait_ge(m_lo, e)
                eng.tensor_tensor(mv, mv, WT[:, :, :], ALU.add).then_inc(summed, 1)
                if not first:
                    eng.wait_ge(y_free, NBANK + NT * (e - 1))
                eng.tensor_copy(gb[:, s, :], gt[:, :, bass.ds(e, 1)].rearrange("p t o -> p (t o)")).then_inc(g_ready, 1)
                eng.wait_ge(m_hi, e + 1)
                eng.tensor_tensor(ml[s][:, :, :], mv, r32(mh[s][:, :, :]), ALU.subtract).then_inc(m_lo, 1)

            def add(e, s, t):
                eng.wait_ge(y_done, NT * e + t + 1)
                eng.scalar_tensor_tensor(out=core.X[:, t, :], in0=Y[t % NBANK][:, :], scalar=gb[:, s, t:t + 1],
                                         in1=core.X[:, t, :], op0=ALU.mult, op1=ALU.add).then_inc(y_free, 1)

            def expert(e, s, last=False):
                eng.wait_ge(g_ready, e + 1)
                for t in range(NT):
                    add(e, s, t)
                    if t == 3 and not last:
                        prepare(e + 1, 1 - s, False)

            for k in range(KD):
                eng.wait_ge(M_in[k], 16)
            prepare(0, 0, True)
            with eng.Fori(0, E // 2 - 1) as it:
                for s in range(2):
                    expert(2 * it + s, s)
            expert(E - 2, 0)
            expert(E - 1, 1, last=True)

        @block.scalar
        def _(eng):
            def high(e, s):
                eng.wait_ge(summed, e + 1)
                mv = M[:, :, :, bass.ds(e, 1)].rearrange("p k r o -> p k (r o)")
                if not isinstance(e, int):
                    eng.wait_ge(y_done, NT * (e - 1))
                elif e >= 2:
                    eng.wait_ge(y_done, NT * (e - 1))
                eng.activation(mh[s][:, :, :], mv, ACT.Copy).then_inc(m_hi, 1)

            high(0, 0)
            high(1, 1)
            with eng.Fori(1, E // 2) as it:
                for s in range(2):
                    high(2 * it + s, s)

        @block.tensor
        def _(eng):
            def expert(e, s):
                eng.wait_ge(m_lo, e + 1)
                for t in range(NT):
                    eng.wait_ge(y_free, NT * e + t + 1)
                    i = 0
                    for x_, w_ in ((0, mh[s]), (0, ml[s]), (1, mh[s])):
                        for k in range(KD):
                            m = eng.matmul(Y[t % NBANK][:, :], xT[x_][:, k, t * P:(t + 1) * P], w_[:, k, :],
                                           start=(i == 0), stop=(i == 3 * KD - 1))
                            i += 1
                    m.then_inc(y_done, 1)

            with eng.Fori(0, E // 2) as it:
                for s in range(2):
                    expert(2 * it + s, s)


def program(nc, x, ctx_1024, fside_BxSx2_0, g_xattn, g_ffn, *args):
    attn0, ffn0, attn1, ffn1, out = args[0:4], args[4:11], args[11:27], args[27:33], args[33]
    gate_w, W, atoms, atom_weights, importance, mask_idx = ffn1
    core = Core()
    table = nc.dram_tensor("table", [D * D + mask_idx.shape[0], atom_weights.shape[0]], F32, kind="Internal").ap()
    with ExitStack() as ctx:
        core.X = ctx.enter_context(nc.sbuf_tensor("X", [P, NT, D], F32))
        core.ident = ctx.enter_context(nc.sbuf_tensor("ident", [P, P], F32))
        core.gates = ctx.enter_context(nc.sbuf_tensor("gates", [P, 4], F32))
        setup(nc, core, x, g_xattn, g_ffn)
        scatter_tables(nc, core, atoms, atom_weights, importance, mask_idx, table)
        rope_attention(nc, core, ctx_1024, fside_BxSx2_0, *attn0, core.gates[:, 0:1])
        expert_ffn(nc, core, *ffn0, core.gates[:, 2:3])
        normed_attention(nc, core, ctx_1024, *attn1, core.gates[:, 1:2])
        masked_ffn(nc, core, gate_w, W, table, out)


_INS = ["x", "ctx_1024", "fside_BxSx2_0", "g_xattn", "g_ffn"] \
    + ["L0_xattn_" + n for n in ("Wq", "Wkv", "Wout", "bout")] \
    + ["L0_ffn_" + n for n in ("w_gate", "wg", "wu", "wd", "sg", "su", "sd")] \
    + ["L1_xattn_" + n for n in ("Wq", "bq", "Wk", "bk", "Wv", "bv", "Wkv_dca", "bkv_dca", "qn_w", "qn_b", "kn_w", "kn_b",
                                 "kn_dca_w", "kn_dca_b", "Wo", "bo")] \
    + ["L1_ffn_" + n for n in ("gate_w", "W", "atoms", "expert_atom_weights", "importance", "mask_idx")]


def kernel(**inputs):
    import concourse.bacc as _bacc
    from concourse.bass_utils import run_bass_kernel_spmd as _run

    nc = _bacc.Bacc("TRN2", target_bir_lowering=False, num_devices=1)
    arrays, args = {}, []
    for name in _INS:
        a = np.ascontiguousarray(inputs[name])
        arrays[f"in_{name}"] = a
        args.append(nc.dram_tensor(f"in_{name}", a.shape, mybir.dt.from_np(a.dtype), kind="ExternalInput").ap())
    out = nc.dram_tensor("out", (B, S, D), F32, kind="ExternalOutput").ap()
    program(nc, *args, out)
    r = _run(nc, [arrays], core_ids=[0])
    return r.results[0]["out"]
```

```python
from contextlib import ExitStack

import numpy as np
import concourse.bass as bass
from concourse import mybir

F32 = mybir.dt.float32
F32R = mybir.dt.float32r
BF16 = mybir.dt.bfloat16
I32 = mybir.dt.int32
U32 = mybir.dt.uint32
ALU = mybir.AluOpType
ACT = mybir.ActivationFunctionType
AX = mybir.AxisListType

P = 128
D = 512
KD = D // P
CD = 256
KC = CD // P
B = 8
S = 256
T = B * S
NT = T // P
BT = S // P


class Count:

    def __init__(self, base=0, step=1):
        self.base, self.step, self.n = base, step, 0

    def inc(self, k=1):
        self.n += k
        return k * self.step

    @property
    def now(self):
        return self.base + self.n * self.step if self.n else self.base


class Ring:

    def __init__(self, filled, freed, items, before=0):
        assert items % len(filled) == 0 and before % len(filled) == 0
        self.before = before // len(filled)
        self.filled, self.freed, self.k, self.per = filled, freed, len(filled), items // len(filled)
        self.items = items

    def until_free(self, it, j):
        return self.freed[j % self.k], it * self.per + self.before + j // self.k + 1

    def until_filled(self, it, j):
        return self.filled[j % self.k], it * self.per + self.before + j // self.k + 1

    def until_freed(self, it, j):
        return self.freed[j % self.k], it * self.per + self.before + j // self.k + 2


def semaphores(nc, ctx, prefix):
    taken = []

    def clear():
        nc.clear_and_free_semaphores(taken)
        nc.all_engine_barrier()
    ctx.callback(clear)

    def sem(name):
        taken.append(nc.alloc_semaphore(prefix + name))
        return taken[-1]
    return sem


def r32(ap):
    return ap.bitcast(F32)


def rsqrt_steps(eng, sem, c, v, y, a, h):
    eng.wait_ge(sem, c.now)
    eng.tensor_scalar(a.bitcast(I32), v.bitcast(I32), 1, None, ALU.arith_shift_right).then_inc(sem, c.inc())
    eng.tensor_scalar(h, v, -0.5, None, ALU.mult).then_inc(sem, c.inc())
    eng.wait_ge(sem, c.now)
    eng.tensor_scalar(y.bitcast(I32), a.bitcast(I32), -1.0, float(0x5F3759DF), ALU.mult, ALU.add).then_inc(sem, c.inc())
    for _ in range(3):
        eng.wait_ge(sem, c.now)
        eng.tensor_tensor(a, y, y, ALU.mult).then_inc(sem, c.inc())
        eng.wait_ge(sem, c.now)
        eng.tensor_tensor(a, a, h, ALU.mult).then_inc(sem, c.inc())
        eng.wait_ge(sem, c.now)
        eng.scalar_tensor_tensor(out=y, in0=a, scalar=1.5, in1=y, op0=ALU.add, op1=ALU.mult).then_inc(sem, c.inc())


def layer_norm_scales(eng, sem, c, x, st, w, out):
    for t in range(NT):
        eng.bn_stats(st[:, t, :], x[:, t, :]).then_inc(sem, c.inc())
    eng.wait_ge(sem, c.now)
    eng.tensor_tensor(w[:, 0, :], st[:, :, 2], st[:, :, 5], ALU.add).then_inc(sem, c.inc())
    eng.tensor_tensor(w[:, 1, :], st[:, :, 1], st[:, :, 4], ALU.subtract).then_inc(sem, c.inc())
    eng.tensor_tensor(w[:, 2, :], st[:, :, 1], st[:, :, 4], ALU.add).then_inc(sem, c.inc())
    eng.wait_ge(sem, c.now)
    eng.scalar_tensor_tensor(out=w[:, 1, :], in0=w[:, 1, :], scalar=0.25, in1=w[:, 1, :],
                             op0=ALU.mult, op1=ALU.mult).then_inc(sem, c.inc())
    eng.wait_ge(sem, c.now)
    eng.scalar_tensor_tensor(out=w[:, 0, :], in0=w[:, 0, :], scalar=1.0 / D, in1=w[:, 1, :],
                             op0=ALU.mult, op1=ALU.add).then_inc(sem, c.inc())
    eng.wait_ge(sem, c.now)
    eng.tensor_scalar(w[:, 0, :], w[:, 0, :], 1e-5, None, ALU.add).then_inc(sem, c.inc())
    rsqrt_steps(eng, sem, c, w[:, 0, :], w[:, 3, :], w[:, 1, :], w[:, 4, :])
    eng.wait_ge(sem, c.now)
    eng.tensor_copy(out[:, :, 0], w[:, 3, :]).then_inc(sem, c.inc())
    eng.scalar_tensor_tensor(out=out[:, :, 1], in0=w[:, 2, :], scalar=-0.5, in1=w[:, 3, :],
                             op0=ALU.mult, op1=ALU.mult).then_inc(sem, c.inc())


class Core:
    pass


def setup(nc, core, g_xattn, g_ffn):
    with ExitStack() as ctx:
        graw = ctx.enter_context(nc.sbuf_tensor("graw", [P, 4], F32))
        sem = semaphores(nc, ctx, "su_")
        loaded, zeroed = sem("loaded"), sem("zeroed")
        block = ctx.enter_context(nc.Block())

        @block.sync
        def _(eng):
            eng.dma_start(graw[:, 0:2], g_xattn.partition_broadcast(P)).then_inc(loaded, 16)
            eng.dma_start(graw[:, 2:4], g_ffn.partition_broadcast(P)).then_inc(loaded, 16)
            eng.wait_ge(loaded, 2 * 16)

        @block.gpsimd
        def _(eng):
            eng.memset(core.ident[:, :], 0.0).then_inc(zeroed, 1)
            eng.wait_ge(zeroed, 1)
            eng.affine_select(out=core.ident[:, :], in_=core.ident[:, :], compare_op=ALU.not_equal, fill=1.0,
                              base=0, pattern=[[-1, P]], channel_multiplier=1)

        @block.scalar
        def _(eng):
            eng.wait_ge(loaded, 2 * 16)
            eng.activation(core.gates[:, :], graw[:, :], ACT.Tanh)


def split_weights(nc, name, parts, raw, sync, vector, gpsimd, scalar=None):
    with ExitStack() as ctx:
        sem = semaphores(nc, ctx, name)
        loaded, hi_done, free = [sem(f"_loaded{i}") for i in range(2)], sem("_hi"), sem("_free")
        block = ctx.enter_context(nc.Block())

        def views(i):
            a, hi, lo = parts[i]
            k, m = a.shape[1], a.shape[2]
            return a, hi, lo, raw[:, i % 2, 0:k * m].rearrange("p (k m) -> p k m", k=k)

        @block.sync
        def _(eng):
            for i in range(len(parts)):
                a, _, _, r = views(i)
                if i == 2:
                    sync(eng)
                if i >= 2:
                    eng.wait_ge(free, i - 1)
                eng.dma_start(r, a).then_inc(loaded[i % 2], 16)

        @block.scalar
        def _(eng):
            for i in range(len(parts)):
                _, hi, _, r = views(i)
                eng.wait_ge(loaded[i % 2], 16 * (i // 2 + 1))
                eng.activation(hi, r, ACT.Copy).then_inc(hi_done, 1)
            if scalar:
                scalar(eng)

        @block.gpsimd
        def _(eng):
            gpsimd[0](eng)
            for i in range(len(parts)):
                _, hi, lo, r = views(i)
                eng.wait_ge(hi_done, i + 1)
                eng.tensor_tensor(lo, r, r32(hi), ALU.subtract).then_inc(free, 1)
            eng.wait_ge(free, len(parts))
            gpsimd[1](eng)

        @block.vector
        def _(eng):
            vector(eng)


def rope_tables(nc, ctx, pos, CS, scales):
    HALF = 4
    n = NT * 2 * HALF
    TWO_PI = 2 * np.pi
    HI = float(np.float32(6.28125))
    LO = float(np.float32(TWO_PI - 6.28125))
    MAGIC = float(1.5 * 2 ** 23)
    sb = lambda name, shape, dt=F32: ctx.enter_context(nc.sbuf_tensor(name, shape, dt))
    ps = sb("rt_pos", [P, NT, 2])
    ang = sb("rt_ang", [P, 2, NT, 2, HALF])
    turns = sb("rt_turns", [P, 2, NT, 2, HALF])
    sn = sb("rt_sin", [P, 2, NT, 2, HALF])
    sem = semaphores(nc, ctx, "rt_")
    loaded, vdone, sdone = sem("loaded"), sem("vdone"), sem("sdone")
    c = Count()
    angles_ready = 2 * HALF // 2 + 1 + 6

    def load(eng):
        eng.dma_start(ps[:, :, :], pos.rearrange("b (t p) c -> p (b t) c", p=P)).then_inc(loaded, 16)

    def angles(eng):
        scales(eng)
        eng.wait_ge(loaded, 16)
        for i in range(HALF):
            f = float(np.float32(10000.0) ** np.float32(-i / HALF))
            eng.tensor_scalar(ang[:, 0, :, :, i], ps[:, :, :], f, None, ALU.mult).then_inc(vdone, c.inc())
        eng.wait_ge(vdone, c.now)
        eng.tensor_scalar(ang[:, 1], ang[:, 0], float(np.pi / 2), None, ALU.add).then_inc(vdone, c.inc())
        eng.wait_ge(vdone, c.now)
        flat = lambda a: a[:, :, :, :, :].rearrange("p a t c h -> p (a t c h)")
        A, U = flat(ang), flat(turns)
        eng.tensor_scalar(U, A, float(1 / TWO_PI), None, ALU.mult).then_inc(vdone, c.inc())
        eng.wait_ge(vdone, c.now)
        eng.tensor_scalar(U, U, MAGIC, None, ALU.add).then_inc(vdone, c.inc())
        eng.wait_ge(vdone, c.now)
        eng.tensor_scalar(U, U, -MAGIC, None, ALU.add).then_inc(vdone, c.inc())
        eng.wait_ge(vdone, c.now)
        eng.scalar_tensor_tensor(out=A, in0=U, scalar=-HI, in1=A, op0=ALU.mult, op1=ALU.add).then_inc(vdone, c.inc())
        eng.wait_ge(vdone, c.now)
        eng.scalar_tensor_tensor(out=A, in0=U, scalar=-LO, in1=A, op0=ALU.mult, op1=ALU.add).then_inc(vdone, c.inc())
        eng.wait_ge(vdone, c.now)
        PI = 3.1415925
        eng.tensor_scalar(A, A, PI, -PI, ALU.min, ALU.max).then_inc(vdone, c.inc())
        assert c.now == angles_ready
        eng.wait_ge(sdone, 1)
        cs = CS[:, :, :, :].rearrange("p t c (a i) -> p t c a i", i=2)
        both = lambda k: sn[:, k].rearrange("p t c h -> p t (c h)")
        for i in range(2):
            eng.tensor_copy(cs[:, :, 0, :, i], both(1)).then_inc(vdone, c.inc())
            eng.tensor_scalar(cs[:, :, 1, :, i], both(0), -1.0 if i == 0 else 1.0, None,
                              ALU.mult).then_inc(vdone, c.inc())

    def sines(eng):
        eng.wait_ge(vdone, angles_ready)
        eng.activation(sn[:, :, :, :, :].rearrange("p a t c h -> p (a t c h)"),
                       ang[:, :, :, :, :].rearrange("p a t c h -> p (a t c h)"), ACT.Sin).then_inc(sdone, 1)

    return load, angles, sines


def rope_attention(nc, core, ctx_d, pos, Wq, Wkv, Wout, bout, gate, then_gpsimd):
    H, HD = 32, 16
    R = 64
    HI_HI, HI_LO, LO_HI, MAXROW = 0, HD, 2 * HD, 3 * HD
    PAIRS = H // 2
    GH = 8
    NG = H // GH
    QH = 4
    NQ = H // QH
    SCALE = 1.0 / HD ** 0.5

    with ExitStack() as ctx:
        sb = lambda name, shape, dt=F32: ctx.enter_context(nc.sbuf_tensor(name, shape, dt))
        sem = semaphores(nc, ctx, "")
        wq = [sb(f"a_wq{i}", [P, KD, D], F32R) for i in range(2)]
        wkv = [sb(f"a_wkv{i}", [P, KC, 2 * D], F32R) for i in range(2)]
        wo = [sb(f"a_wo{i}", [P, KD, D], F32R) for i in range(2)]
        CS = sb("a_cs", [P, NT, 2, 2 * 8])
        lnsc = sb("a_lnsc", [P, NT, 2])
        bo = sb("a_bo", [P, D])
        ctxb = sb("a_ctx", [P, BT, CD])
        xn = sb("a_xn", [P, BT, D])
        scb = sb("a_scb", [P, BT, 2])
        csb = sb("a_csb", [P, BT, 2, 16])
        xT = [sb(f"a_xT{i}", [P, KD, S], F32R) for i in range(2)]
        cT = [sb(f"a_cT{i}", [P, KC, S], F32R) for i in range(2)]
        rot = sb("a_rot", [P, 2, D])
        tmp = sb("a_tmp", [P, 2, D])
        aug = sb("a_aug", [P, 2, H, R])
        qT = sb("a_qT", [P, PAIRS, S], F32R)
        kT = sb("a_kT", [P, PAIRS, S], F32R)
        V = sb("a_V", [P, BT, H, 32])
        PT = sb("a_PT", [P, 4, BT, S])
        oT = sb("a_oT", [P, 2, S])
        nm = sb("a_nm", [P, H, BT])
        nms = sb("a_nms", [P, BT, 16])
        nmT = sb("a_nmT", [16, NG, S])
        rden = sb("a_rden", [P, BT, QH])
        att = sb("a_att", [P, BT, D])
        aT = [sb(f"a_aT{i}", [P, KD, S], F32R) for i in range(2)]
        y = sb("a_y", [P, D])

        W = [ctx.enter_context(nc.psum_tensor(f"a_W{i}", [P, 512], F32)) for i in range(2)]
        SM = [ctx.enter_context(nc.psum_tensor(f"a_SM{i}", [P, 512], F32)) for i in range(2)]
        ST = [ctx.enter_context(nc.psum_tensor(f"a_ST{i}", [P, 512], F32)) for i in range(2)]
        O = [ctx.enter_context(nc.psum_tensor(f"a_O{i}", [P, 512], F32)) for i in range(2)]

        loaded_bo, ones_set = sem("a_loaded_bo"), sem("a_ones_set")
        ctx_loaded, xn_ready = sem("a_ctx_loaded"), sem("a_xn_ready")
        xT_hi = sem("a_xT_hi")
        added, aug_hi, aug_lo = [[sem(f"a_{n}{w}") for w in "qk"] for n in ("added", "aug_hi", "aug_lo")]
        nms_ready = sem("a_nms_ready")
        max_rows = [sem(f"a_max_rows{g}") for g in range(NG)]
        exp_done, weighted_done = sem("a_exp_done"), sem("a_weighted_done")
        aT_hi = sem("a_aT_hi")
        vseq = sem("a_vseq")
        Wf, We = [[sem(f"a_{n}{i}") for i in range(2)] for n in ("W_filled", "W_free")]
        SMf, SMe = [[sem(f"a_{n}{i}") for i in range(2)] for n in ("SM_filled", "SM_free")]
        STf = [sem(f"a_ST_filled{i}") for i in range(2)]
        Oe = [sem(f"a_O_free{i}") for i in range(2)]

        PROJ = {(0, "v"): 0, (1, "q"): 1, (1, "k"): 2, (1, "v"): 3}
        AUG_TR = {(t, w, i): 4 + 8 * t + 4 * (w == "k") + i for t in range(BT) for w in "qk" for i in range(4)}
        MAX_TR, O_TR = [20, 21, 23, 28], [22, 24, 25, 29, 32, 35, 36, 37]
        NEXT = {"c": (26, 27), "x": (30, 31), "qk": (33, 34)}
        FIRST = {"c": (0, 1), "x": (2, 3), "qk": (4, 5)}
        EARLY = 6
        A_TR, OUT = [38, 39], [40, 41]
        ITEMS = 42
        C_HEAD, X_HEAD, QK_HEAD = 15, 19, 24
        X = core.X

        def rings(it):
            return Ring(Wf, We, ITEMS, EARLY), Ring(SMf, SMe, H), Ring(STf, STf, H), Ring(Oe, Oe, NQ)

        def late(j, last):
            return j - 2 * sum(j > NEXT[n][0] for n in NEXT) if last else j

        def every_batch(eng, step):
            with eng.Fori(0, B - 1) as b:
                step(b, False)
            step(B - 1, True)

        first_ring = Ring(Wf, We, EARLY)

        def evacuate_turned(eng, it, Wr, t, w, which):
            for i in range(4):
                j = AUG_TR[t, w, i]
                if j % 2 != which:
                    continue
                eng.wait_ge(*Wr.until_filled(it, j))
                dst = (qT if w == "q" else kT)[:, 4 * i:4 * i + 4, t * P:(t + 1) * P]
                src = W[j % 2][:, :].rearrange("p (g n) -> p g n", g=4)
                if which == 0:
                    eng.activation(dst, src, ACT.Copy).then_inc(We[j % 2], 1)
                else:
                    eng.tensor_copy(dst, src).then_inc(We[j % 2], 1)

        before_loop = Count()

        def scales(eng):
            st = PT[:, 0, 0, 0:6 * NT].rearrange("p (t s) -> p t s", s=6)
            lw = PT[:, 0, 1, 0:5 * NT].rearrange("p (s t) -> p s t", t=NT)
            layer_norm_scales(eng, vseq, before_loop, X, st, lw, lnsc)

        with ExitStack() as c2:
            load_positions, angles, sines = rope_tables(nc, c2, pos, CS, scales)
            split_weights(nc, "a_w", [
                (Wq.rearrange("(k p) n -> p k n", p=P), wq[0][:, :, :], wq[1][:, :, :]),
                (Wkv.rearrange("(k p) n -> p k n", p=P), wkv[0][:, :, :], wkv[1][:, :, :]),
                (Wout.rearrange("(k p) n -> p k n", p=P), wo[0][:, :, :], wo[1][:, :, :])],
                aug[:, :, :, :].rearrange("p a h r -> p a (h r)"),
                load_positions, angles, (lambda eng: None, lambda eng: None), sines)

        block = ctx.enter_context(nc.Block())

        @block.sync
        def _(eng):
            eng.dma_start(bo[:, :], bout.partition_broadcast(P)).then_inc(loaded_bo, 16)

            def context(b):
                src = ctx_d[b:b + 1] if isinstance(b, int) else ctx_d[bass.ds(b, 1)]
                for t in range(BT):
                    eng.dma_start(ctxb[:, t, :], src[:, t * P:(t + 1) * P, :]
                                  .rearrange("o p c -> (o p) c")).then_inc(ctx_loaded, 16)

            def step(b, last):
                Wr = rings(b)[0]
                for g in range(NG):
                    eng.wait_ge(*Wr.until_freed(b, late(MAX_TR[g], last)))
                    for par in range(2):
                        for j in range(2):
                            r = 4 * (2 * par + j)
                            row = R * par + MAXROW + j
                            eng.dma_start(r32(qT[row:row + 1, 4 * g:4 * g + 4, :]),
                                          nmT[r:r + 4, g, :]).then_inc(max_rows[g], 16)
                    if g == 0 and not last:
                        context(b + 1)

            context(0)
            every_batch(eng, step)
            eng.wait_ge(loaded_bo, 16)

        @block.gpsimd
        def _(eng):
            eng.memset(aug[:, :, :, :], 0.0).then_inc(ones_set, 1)
            eng.memset(V[:, :, :, :], 0.0).then_inc(ones_set, 1)
            eng.wait_ge(ones_set, 2)
            eng.memset(V[:, :, :, HD:HD + 1], 1.0).then_inc(ones_set, 1)
            eng.memset(aug[:, 1, :, MAXROW:MAXROW + 2], 1.0).then_inc(ones_set, 1)
            eng.wait_ge(ones_set, 4)

            def turned_pairs(n, a, written):
                lo = LO_HI if a == 0 else HI_LO
                eng.wait_ge(*written)
                eng.tensor_tensor(rot[:, a, :], rot[:, a, :], tmp[:, a, :], ALU.add).then_inc(added[a], 1)
                eng.wait_ge(aug_hi[a], (n + 1) * 2)
                eng.tensor_tensor(aug[:, a, :, lo:lo + HD], rot[:, a, :].rearrange("p (h e) -> p h e", e=HD),
                                  aug[:, a, :, 0:HD], ALU.subtract).then_inc(aug_lo[a], 1)

            def step(b, last):
                Wr = rings(b)[0]
                for a, w in enumerate("qk"):
                    turned_pairs(b * BT + 1, a, Wr.until_freed(b, PROJ[1, w]))
                if not last:
                    for a in range(2):
                        turned_pairs((b + 1) * BT, a, Wr.until_freed(b, NEXT["qk"][a]))

            for a in range(2):
                turned_pairs(0, a, first_ring.until_freed(0, FIRST["qk"][a]))
            every_batch(eng, step)
            then_gpsimd(eng)

        @block.vector
        def _(eng):
            c = before_loop
            eng.wait_ge(loaded_bo, 16)

            def tokens(c, b):
                eng.wait_ge(vseq, c.now)
                eng.tensor_copy(scb[:, :, :], lnsc[:, bass.ds(2 * b, 2), :]).then_inc(vseq, c.inc())
                eng.tensor_copy(csb[:, :, :, :].rearrange("p t c e -> p t (c e)"),
                                CS[:, bass.ds(2 * b, 2), :, :].rearrange("p t c e -> p t (c e)")).then_inc(vseq, c.inc())
                eng.wait_ge(vseq, c.now)
                for t in range(BT):
                    eng.tensor_scalar(xn[:, t, :], X[:, bass.ds(2 * b + t, 1), :].rearrange("p o d -> p (o d)"),
                                      scb[:, t, 0:1], scb[:, t, 1:2], ALU.mult, ALU.add).then_inc(xn_ready, 1)

            def low_parts(b, items, hi, lo, k, before):
                for t in range(BT):
                    bank = W[items[t] % 2]
                    eng.wait_ge(xT_hi, b * 4 + before + t + 1)
                    eng.tensor_tensor(lo[:, :, t * P:(t + 1) * P],
                                      bank[:, 0:k * P].rearrange("p (k n) -> p k n", k=k),
                                      r32(hi[:, :, t * P:(t + 1) * P]), ALU.subtract).then_inc(We[items[t] % 2], 1)

            def rotate(b, Wr, it, j, t, a):
                src = W[j % 2][:, :].rearrange("p (h a i) -> p h a i", h=H, i=2)
                tv = tmp[:, a, :].rearrange("p (h a i) -> p h a i", h=H, i=2)
                cosb = csb[:, t, 0, :].unsqueeze(1).to_broadcast([P, H, 16])
                sinv = csb[:, t, 1, :].rearrange("p (a i) -> p a i", i=2)
                eng.wait_ge(*Wr.until_filled(it, j))
                if t:
                    eng.wait_ge(aug_lo[a], b * BT + t)
                eng.tensor_tensor(rot[:, a, :].rearrange("p (h e) -> p h e", h=H),
                                  W[j % 2][:, :].rearrange("p (h e) -> p h e", h=H), cosb, ALU.mult)
                eng.tensor_tensor(tv[:, :, :, 0], src[:, :, :, 1],
                                  sinv[:, :, 0].unsqueeze(1).to_broadcast([P, H, 8]), ALU.mult)
                eng.tensor_tensor(tv[:, :, :, 1], src[:, :, :, 0],
                                  sinv[:, :, 1].unsqueeze(1).to_broadcast([P, H, 8]), ALU.mult).then_inc(We[j % 2], 1)

            tokens(c, 0)
            low_parts(0, FIRST["c"], cT[0], cT[1], KC, 0)
            low_parts(0, FIRST["x"], xT[0], xT[1], KD, BT)
            for a in range(2):
                rotate(0, first_ring, 0, FIRST["qk"][a], 0, a)
            start = c.now
            PER = 2 + NG + NQ + 2

            def step(b, last):
                c = Count(b * PER + start)
                Wr, SMr, STr, Or = rings(b)
                for a, w in enumerate("qk"):
                    rotate(b, Wr, b, PROJ[1, w], 1, a)
                for t in range(BT):
                    for w in "qk":
                        evacuate_turned(eng, b, Wr, t, w, 1)

                def top(h):
                    eng.wait_ge(*SMr.until_filled(b, h))
                    eng.tensor_reduce(nm[:, h, :], SM[h % 2][:, :].rearrange("p (t k) -> p t k", t=BT),
                                      AX.X, ALU.max, negate=True).then_inc(SMe[h % 2], 1)
                    if h % GH == GH - 1:
                        g = h // GH
                        for i in (h - 1, h):
                            eng.wait_ge(*SMr.until_freed(b, i))
                        if g:
                            eng.wait_ge(*Wr.until_freed(b, late(MAX_TR[g - 1], last)))
                        src = nm[:, g * GH:(g + 1) * GH, :].rearrange("p (a r) t -> p t r a", r=2)
                        dst = nms[:, :, :].rearrange("p t (r j a) -> p t r j a", r=2, j=2)
                        for t in range(BT):
                            i = eng.tensor_copy(dst[:, t, :, 0, :].bitcast(F32R), src[:, t])
                        i.then_inc(vseq, c.inc())
                        eng.wait_ge(vseq, c.now)
                        for t in range(BT):
                            i = eng.tensor_tensor(dst[:, t, :, 1, :], src[:, t], dst[:, t, :, 0, :], ALU.subtract)
                        i.then_inc(nms_ready, 1)

                def normalise(q):
                    j = late(O_TR[q], last)
                    o = W[j % 2][:, 0:BT * P].rearrange("p (t h e) -> p t h e", t=BT, h=QH)
                    eng.wait_ge(*Wr.until_filled(b, j))
                    if q:
                        eng.wait_ge(*Wr.until_freed(b, late(O_TR[q - 1], last)))
                    eng.reciprocal(rden[:, :, :], o[:, :, :, HD]).then_inc(vseq, c.inc())
                    eng.wait_ge(vseq, c.now)
                    for t in range(BT):
                        i = eng.tensor_tensor(att[:, t, q * QH * HD:(q + 1) * QH * HD]
                                              .rearrange("p (h e) -> p h e", h=QH), o[:, t, :, 0:HD],
                                              rden[:, t].unsqueeze(2).to_broadcast([P, QH, HD]), ALU.mult)
                    i.then_inc(We[j % 2], 1)

                for h in range(2 * GH):
                    top(h)
                for h in range(H):
                    if h + 2 * GH < H:
                        top(h + 2 * GH)
                    if not last and h == C_HEAD - 2:
                        tokens(c, b + 1)
                    if not last and h == C_HEAD + 1:
                        low_parts(b + 1, NEXT["c"], cT[0], cT[1], KC, 0)
                    if h % QH == 2 and h >= QH:
                        normalise(h // QH - 1)
                    if not last and h == X_HEAD:
                        low_parts(b + 1, NEXT["x"], xT[0], xT[1], KD, BT)
                    if not last and h == QK_HEAD:
                        for a in range(2):
                            rotate(b + 1, Wr, b, NEXT["qk"][a], 0, a)
                normalise(NQ - 1)
                for t in range(BT):
                    eng.wait_ge(aT_hi, b * BT + t + 1)
                    eng.tensor_tensor(aT[1][:, :, t * P:(t + 1) * P],
                                      W[late(A_TR[t], last) % 2][:, :].rearrange("p (k n) -> p k n", k=KD),
                                      r32(aT[0][:, :, t * P:(t + 1) * P]),
                                      ALU.subtract).then_inc(We[late(A_TR[t], last) % 2], 1)
                for t in range(BT):
                    j = late(OUT[t], last)
                    xx = X[:, bass.ds(2 * b + t, 1), :].rearrange("p o d -> p (o d)")
                    eng.wait_ge(*Wr.until_filled(b, j))
                    eng.wait_ge(vseq, c.now)
                    eng.tensor_tensor(y[:, :], W[j % 2][:, :], bo[:, :], ALU.add).then_inc(We[j % 2], 1)
                    eng.wait_ge(*Wr.until_freed(b, j))
                    eng.scalar_tensor_tensor(out=xx, in0=y[:, :], scalar=gate, in1=xx,
                                             op0=ALU.mult, op1=ALU.add).then_inc(vseq, c.inc())
                assert c.n == PER - 2 * last

            every_batch(eng, step)

        @block.scalar
        def _(eng):
            eng.wait_ge(ones_set, 4)

            def high_parts(Wr, it, items, hi, k):
                for t in range(BT):
                    eng.wait_ge(*Wr.until_filled(it, items[t]))
                    eng.activation(hi[:, :, t * P:(t + 1) * P],
                                   W[items[t] % 2][:, 0:k * P].rearrange("p (k n) -> p k n", k=k),
                                   ACT.Copy).then_inc(xT_hi, 1)

            def rounded(n, a):
                heads = rot[:, a, :].rearrange("p (h e) -> p h e", e=HD)
                dup = HI_LO if a == 0 else LO_HI
                eng.wait_ge(added[a], n + 1)
                for at in (HI_HI, dup):
                    eng.activation(aug[:, a, :, at:at + HD].bitcast(F32R), heads, ACT.Copy).then_inc(aug_hi[a], 1)

            high_parts(first_ring, 0, FIRST["c"], cT[0], KC)
            high_parts(first_ring, 0, FIRST["x"], xT[0], KD)
            for a in range(2):
                rounded(0, a)

            def step(b, last):
                Wr, SMr, STr, Or = rings(b)

                def values(t):
                    j = PROJ[t, "v"]
                    eng.wait_ge(*Wr.until_filled(b, j))
                    eng.activation(V[:, t, :, 0:HD], W[j % 2][:, :].rearrange("p (h e) -> p h e", h=H),
                                   ACT.Copy).then_inc(We[j % 2], 1)

                values(0)
                values(1)
                for a, w in enumerate("qk"):
                    evacuate_turned(eng, b, Wr, 0, w, 0)
                    eng.wait_ge(*Wr.until_filled(b, AUG_TR[0, w, 3]))
                    rounded(b * BT + 1, a)
                evacuate_turned(eng, b, Wr, 1, "q", 0)
                evacuate_turned(eng, b, Wr, 1, "k", 0)

                def maxima(g):
                    j = late(MAX_TR[g], last)
                    eng.wait_ge(*Wr.until_filled(b, j))
                    eng.activation(nmT[:, g, :], W[j % 2][0:16, 0:S], ACT.Copy).then_inc(We[j % 2], 1)

                def turned_outputs(q):
                    eng.wait_ge(weighted_done, b * H + (q + 1) * QH)
                    if q >= 2:
                        eng.wait_ge(*Wr.until_filled(b, late(O_TR[q - 2], last)))
                    eng.activation(oT[:, q % 2, :], O[q % 2][:, 0:S], ACT.Copy).then_inc(Oe[q % 2], 1)

                maxima(0)
                for h in range(H):
                    eng.wait_ge(*STr.until_filled(b, h))
                    if h >= 4:
                        eng.wait_ge(weighted_done, b * H + h - 3)
                    eng.activation(PT[:, h % 4, :, :].rearrange("p t s -> p (t s)"), ST[h % 2][:, :], ACT.Exp,
                                   scale=SCALE).then_inc(exp_done, 1)
                    if h % GH == 1 and h // GH + 1 < NG:
                        maxima(h // GH + 1)
                    if h % QH == 1 and h >= QH:
                        turned_outputs(h // QH - 1)
                    if not last and h == C_HEAD + 1:
                        high_parts(Wr, b, NEXT["c"], cT[0], KC)
                    if not last and h == X_HEAD + 1:
                        high_parts(Wr, b, NEXT["x"], xT[0], KD)
                    if not last and h in (QK_HEAD + 3, QK_HEAD + 5):
                        rounded((b + 1) * BT, (h - QK_HEAD - 3) // 2)
                turned_outputs(NQ - 1)
                for t in range(BT):
                    eng.wait_ge(*Wr.until_filled(b, late(A_TR[t], last)))
                    eng.activation(aT[0][:, :, t * P:(t + 1) * P],
                                   W[late(A_TR[t], last) % 2][:, :].rearrange("p (k n) -> p k n", k=KD),
                                   ACT.Copy).then_inc(aT_hi, 1)

            every_batch(eng, step)

        @block.tensor
        def _(eng):
            for s_ in We + SMe + Oe:
                eng.sem_inc(s_, 1)

            def turn(Wr, it, j, srcs):
                eng.wait_ge(*Wr.until_free(it, j))
                for i, s in enumerate(srcs):
                    m = eng.transpose(W[j % 2][0:s.shape[1], i * P:(i + 1) * P], s, core.ident[:, :])
                m.then_inc(Wf[j % 2], 1)

            def product(Wr, it, j, tok, lhs, rhs, k, cols):
                eng.wait_ge(*Wr.until_free(it, j))
                n = 0
                for x_, w_ in ((0, 0), (0, 1), (1, 0)):
                    for i in range(k):
                        m = eng.matmul(W[j % 2][:, :], lhs[x_][:, i, tok * P:(tok + 1) * P],
                                       rhs[w_][:, i, cols:cols + D], start=(n == 0), stop=(n == 3 * k - 1))
                        n += 1
                m.then_inc(Wf[j % 2], 1)

            def turn_context(Wr, it, items, b):
                eng.wait_ge(ctx_loaded, (b + 1) * 32)
                for t in range(BT):
                    turn(Wr, it, items[t], [ctxb[:, t, k * P:(k + 1) * P] for k in range(KC)])

            def turn_tokens(Wr, it, items, b):
                for t in range(BT):
                    eng.wait_ge(xn_ready, b * BT + t + 1)
                    turn(Wr, it, items[t], [xn[:, t, k * P:(k + 1) * P] for k in range(KD)])

            def first_projections(Wr, it, n):
                for j in n["x"]:
                    eng.wait_ge(*Wr.until_freed(it, j))
                product(Wr, it, n["qk"][0], 0, xT, wq, KD, 0)
                product(Wr, it, n["qk"][1], 0, cT, wkv, KC, 0)

            turn_context(first_ring, 0, FIRST["c"], 0)
            turn_tokens(first_ring, 0, FIRST["x"], 0)
            first_projections(first_ring, 0, FIRST)

            def step(b, last):
                Wr, SMr, STr, Or = rings(b)

                product(Wr, b, PROJ[0, "v"], 0, cT, wkv, KC, D)
                product(Wr, b, PROJ[1, "q"], 1, xT, wq, KD, 0)
                product(Wr, b, PROJ[1, "k"], 1, cT, wkv, KC, 0)
                product(Wr, b, PROJ[1, "v"], 1, cT, wkv, KC, D)
                for t in range(BT):
                    for a, w in enumerate("qk"):
                        eng.wait_ge(aug_lo[a], b * BT + t + 1)
                        for i in range(4):
                            turn(Wr, b, AUG_TR[t, w, i],
                                 [aug[:, a, 2 * g:2 * g + 2, :].rearrange("p h r -> p (h r)")
                                  for g in range(4 * i, 4 * i + 4)])
                for i in (2, 3):
                    eng.wait_ge(*Wr.until_freed(b, AUG_TR[1, "k", i]))

                def scores_for_max(h):
                    r = R * (h % 2)
                    eng.wait_ge(*SMr.until_free(b, h))
                    for t in range(BT):
                        m = eng.matmul(SM[h % 2][:, t * S:(t + 1) * S],
                                       qT[r:r + MAXROW, h // 2, t * P:(t + 1) * P], kT[r:r + MAXROW, h // 2, :],
                                       start=True, stop=True)
                    m.then_inc(SMf[h % 2], 1)

                def turn_maxima(g):
                    eng.wait_ge(nms_ready, b * NG + g + 1)
                    turn(Wr, b, late(MAX_TR[g], last), [nms[:, t, :] for t in range(BT)])

                def scores(h):
                    r = R * (h % 2)
                    if h % GH == 0:
                        eng.wait_ge(max_rows[h // GH], (b + 1) * 64)
                    if h >= 2:
                        eng.wait_ge(exp_done, b * H + h - 1)
                    for t in range(BT):
                        m = eng.matmul(ST[h % 2][:, t * S:(t + 1) * S],
                                       kT[r:r + MAXROW + 2, h // 2, t * P:(t + 1) * P],
                                       qT[r:r + MAXROW + 2, h // 2, :], start=True, stop=True)
                    m.then_inc(STf[h % 2], 1)

                def weighted(h):
                    q, r = h // QH, 32 * (h % QH)
                    if h % QH == 0:
                        eng.wait_ge(*Or.until_free(b, q))
                    eng.wait_ge(exp_done, b * H + h + 1)
                    for k in range(BT):
                        m = eng.matmul(O[q % 2][r:r + 32, 0:S], V[:, k, h, :], PT[:, h % 4, k, :],
                                       start=(k == 0), stop=(k == BT - 1))
                    m.then_inc(weighted_done, 1)

                def turn_outputs(q):
                    eng.wait_ge(*Or.until_freed(b, q))
                    turn(Wr, b, late(O_TR[q], last), [oT[:, q % 2, t * P:(t + 1) * P] for t in range(BT)])

                for h in range(2 * GH):
                    scores_for_max(h)
                    if h == GH:
                        turn_maxima(0)
                for h in range(H):
                    scores(h)
                    if h + 2 * GH < H:
                        scores_for_max(h + 2 * GH)
                    if h % GH == 1 and h // GH + 1 < NG:
                        turn_maxima(h // GH + 1)
                    if h:
                        weighted(h - 1)
                    if h % QH == 2 and h >= QH:
                        turn_outputs(h // QH - 1)
                    if not last and h == C_HEAD:
                        turn_context(Wr, b, NEXT["c"], b + 1)
                    if not last and h == X_HEAD:
                        turn_tokens(Wr, b, NEXT["x"], b + 1)
                    if not last and h == QK_HEAD:
                        first_projections(Wr, b, NEXT)
                weighted(H - 1)
                turn_outputs(NQ - 1)
                eng.wait_ge(*Wr.until_freed(b, late(O_TR[NQ - 1], last)))
                for t in range(BT):
                    turn(Wr, b, late(A_TR[t], last), [att[:, t, k * P:(k + 1) * P] for k in range(KD)])
                for t in range(BT):
                    eng.wait_ge(*Wr.until_freed(b, late(A_TR[t], last)))
                for t in range(BT):
                    product(Wr, b, late(OUT[t], last), t, aT, wo, KD, 0)

            every_batch(eng, step)


def turned_tokens(nc, core, name, xT, w, n, logits, then_load=None):
    QT = T // 4
    TQ = QT // P
    with ExitStack() as ctx:
        sb = lambda n_, shape, dt=F32: ctx.enter_context(nc.sbuf_tensor(name + n_, shape, dt))
        sem = semaphores(nc, ctx, name)
        lnsc, st, lw = sb("lnsc", [P, NT, 2]), sb("st", [P, NT, 6]), sb("lw", [P, 5, NT])
        xn = sb("xn", [P, 2, D])
        raw, lt = sb("raw", [n, D]), sb("lt", [n, T])
        gw = [sb(f"gw{i}", [P, KD, P], F32R) for i in range(2)]
        bank = [ctx.enter_context(nc.psum_tensor(f"{name}bank{i}", [P, KD * P], F32)) for i in range(4)]
        LG = [ctx.enter_context(nc.psum_tensor(f"{name}LG{i}", [P, QT], F32)) for i in range(4)]
        vseq, xn_ready, turned, hi_done, lo_done = (sem("vseq"), sem("xn_ready"), sem("turned"), sem("hi_done"),
                                                    sem("lo_done"))
        raw_in, cleared, w_turned, w_hi, w_lo, lg_done, lt_ready, turned_back = [
            sem(s) for s in ("raw_in", "cleared", "w_turned", "w_hi", "w_lo", "lg_done", "lt_ready", "turned_back")]
        block = ctx.enter_context(nc.Block())
        turned_w = LG[0][:, 0:KD * n].rearrange("p (k n) -> p k n", k=KD)

        def view(t):
            return bank[t % 4][:, :].rearrange("p (k n) -> p k n", k=KD)

        def part(x, t):
            return x[:, :, t * P:(t + 1) * P]

        @block.sync
        def _(eng):
            eng.dma_start(raw[:, :], w).then_inc(raw_in, 16)
            if then_load:
                then_load(eng)

        @block.gpsimd
        def _(eng):
            for i in range(2):
                eng.memset(r32(gw[i][:, :, :]), 0.0).then_inc(cleared, 1)

        @block.vector
        def _(eng):
            c = Count()
            layer_norm_scales(eng, vseq, c, core.X, st, lw, lnsc)
            eng.wait_ge(vseq, c.now)

            def low(t):
                eng.wait_ge(hi_done, t + 1)
                eng.tensor_tensor(part(xT[1], t), view(t), r32(part(xT[0], t)), ALU.subtract).then_inc(lo_done, 1)

            for t in range(NT):
                if t >= 2:
                    eng.wait_ge(turned, t - 1)
                eng.tensor_scalar(xn[:, t % 2, :], core.X[:, t, :], lnsc[:, t, 0:1], lnsc[:, t, 1:2],
                                  ALU.mult, ALU.add).then_inc(xn_ready, 1)
                if t == 1:
                    eng.wait_ge(w_hi, 1)
                    eng.tensor_tensor(gw[1][:, :, 0:n], turned_w, r32(gw[0][:, :, 0:n]), ALU.subtract).then_inc(w_lo, 1)
                if t >= 2:
                    low(t - 2)
            low(NT - 2)
            low(NT - 1)

        @block.tensor
        def _(eng):
            def products(q):
                eng.wait_ge(w_lo, 1)
                eng.wait_ge(lo_done, TQ * (q + 1))
                i = 0
                for w_, x_ in ((0, 0), (0, 1), (1, 0)):
                    for k in range(KD):
                        m = eng.matmul(LG[q][:, :], gw[w_][:, k, :], xT[x_][:, k, q * QT:(q + 1) * QT],
                                       start=(i == 0), stop=(i == 3 * KD - 1))
                        i += 1
                m.then_inc(lg_done, 1)

            eng.wait_ge(raw_in, 16)
            for k in range(KD):
                m = eng.transpose(LG[0][:, k * n:(k + 1) * n], raw[:, k * P:(k + 1) * P], core.ident[0:n, 0:n])
            m.then_inc(w_turned, 1)
            for t in range(NT):
                eng.wait_ge(xn_ready, t + 1)
                if t >= 4:
                    eng.wait_ge(lo_done, t - 3)
                for k in range(KD):
                    m = eng.transpose(bank[t % 4][:, k * P:(k + 1) * P], xn[:, t % 2, k * P:(k + 1) * P],
                                      core.ident[:, :])
                m.then_inc(turned, 1)
                if t >= TQ + 2 and t % TQ == 2:
                    products(t // TQ - 1)
            products(3)
            for t in range(NT):
                if t % TQ == 0:
                    eng.wait_ge(lt_ready, t // TQ + 1)
                m = eng.transpose(bank[0][:, t * n:(t + 1) * n], lt[:, t * P:(t + 1) * P], core.ident[0:n, 0:n])
            m.then_inc(turned_back, 1)

        @block.scalar
        def _(eng):
            def on_chip(q):
                eng.wait_ge(lg_done, q + 1)
                eng.activation(lt[:, q * QT:(q + 1) * QT], LG[q][0:n, :], ACT.Copy).then_inc(lt_ready, 1)

            eng.wait_ge(cleared, 2)
            eng.wait_ge(w_turned, 1)
            eng.activation(gw[0][:, :, 0:n], turned_w, ACT.Copy).then_inc(w_hi, 1)
            for t in range(NT):
                eng.wait_ge(turned, t + 1)
                eng.activation(part(xT[0], t), view(t), ACT.Copy).then_inc(hi_done, 1)
                if t >= 2 * TQ and t % TQ == 0:
                    on_chip(t // TQ - 2)
            on_chip(2)
            on_chip(3)
            eng.wait_ge(turned_back, 1)
            eng.activation(logits, bank[0][:, 0:NT * n].rearrange("p (t n) -> p t n", t=NT), ACT.Copy)


def chosen(eng, sem, c, p, n, tri, gt, eq, rank):
    a = p.unsqueeze(2).to_broadcast([P, NT, n, n])
    b = p.unsqueeze(3).to_broadcast([P, NT, n, n])
    eng.wait_ge(sem, c.now)
    eng.tensor_tensor(gt, a, b, ALU.is_gt).then_inc(sem, c.inc())
    eng.tensor_tensor(eq, a, b, ALU.is_equal).then_inc(sem, c.inc())
    eng.wait_ge(sem, c.now)
    eng.tensor_tensor(eq, eq, tri.unsqueeze(1).to_broadcast([P, NT, n, n]), ALU.mult).then_inc(sem, c.inc())
    eng.wait_ge(sem, c.now)
    eng.tensor_tensor(gt, gt, eq, ALU.add).then_inc(sem, c.inc())
    eng.wait_ge(sem, c.now)
    eng.tensor_reduce(rank, gt, AX.X, ALU.add).then_inc(sem, c.inc())


def expert_router(nc, core, lg, E, K, rT):
    with ExitStack() as ctx:
        sb = lambda n, shape, dt=F32: ctx.enter_context(nc.sbuf_tensor("br_" + n, shape, dt))
        sem = semaphores(nc, ctx, "br_")
        p, rank, r = sb("p", [P, NT, E]), sb("rank", [P, NT, E]), sb("r", [P, NT, E])
        m1, s1 = sb("m1", [P, NT]), sb("s1", [P, NT])
        tri, gt, eq = sb("tri", [P, E, E]), sb("gt", [P, NT, E, E], BF16), sb("eq", [P, NT, E, E], BF16)
        rs, ones = sb("rs", [E, T]), sb("ones", [1, T])
        tb = [ctx.enter_context(nc.psum_tensor(f"br_tb{i}", [E, 4 * P], F32)) for i in range(4)]
        shifted, exped, vseq, r_ready, turned, sent, consts, outs = [
            sem(n) for n in ("shifted", "exped", "vseq", "r_ready", "turned", "sent", "consts", "outs")]
        block = ctx.enter_context(nc.Block())
        bc = lambda a: a.unsqueeze(2).to_broadcast([P, NT, E])

        @block.gpsimd
        def _(eng):
            eng.memset(ones[:, :], 1.0).then_inc(consts, 1)
            eng.memset(tri[:, :, :], 1.0).then_inc(consts, 1)
            eng.wait_ge(consts, 2)
            eng.affine_select(out=tri[:, :, :], in_=tri[:, :, :], compare_op=ALU.is_gt, fill=0.0, base=0,
                              pattern=[[1, E], [-1, E]], channel_multiplier=0).then_inc(consts, 1)

        @block.tensor
        def _(eng):
            eng.wait_ge(r_ready, 1)
            for i in range(4):
                for j in range(4):
                    m = eng.transpose(tb[i][:, j * P:(j + 1) * P], r[:, 4 * i + j, :], core.ident[:, :])
                m.then_inc(turned, 1)

        @block.vector
        def _(eng):
            c = Count()
            eng.tensor_reduce(m1[:, :], lg, AX.X, ALU.max).then_inc(vseq, c.inc())
            eng.wait_ge(vseq, c.now)
            eng.tensor_tensor(p[:, :, :], lg, bc(m1[:, :]), ALU.subtract).then_inc(shifted, 1)
            eng.wait_ge(exped, 1)
            eng.tensor_reduce(s1[:, :], p[:, :, :], AX.X, ALU.add).then_inc(vseq, c.inc())
            eng.wait_ge(vseq, c.now)
            eng.reciprocal(m1[:, :], s1[:, :]).then_inc(vseq, c.inc())
            eng.wait_ge(vseq, c.now)
            eng.tensor_tensor(p[:, :, :], p[:, :, :], bc(m1[:, :]), ALU.mult).then_inc(vseq, c.inc())
            eng.wait_ge(consts, 3)
            chosen(eng, vseq, c, p[:, :, :], E, tri[:, :, :], gt[:, :, :, :], eq[:, :, :, :], rank[:, :, :])
            eng.wait_ge(vseq, c.now)
            eng.scalar_tensor_tensor(out=r[:, :, :], in0=rank[:, :, :], scalar=K - 0.5, in1=p[:, :, :],
                                     op0=ALU.is_lt, op1=ALU.mult).then_inc(r_ready, 1)

        @block.scalar
        def _(eng):
            eng.wait_ge(shifted, 1)
            eng.activation(p[:, :, :], p[:, :, :], ACT.Exp).then_inc(exped, 1)
            for i in range(4):
                eng.wait_ge(turned, i + 1)
                eng.activation(rs[:, 4 * i * P:4 * (i + 1) * P], tb[i][:, :], ACT.Copy).then_inc(sent, 1)

        @block.sync
        def _(eng):
            eng.wait_ge(consts, 1)
            eng.dma_start(rT[E:E + 1, :], ones[:, :]).then_inc(outs, 16)
            eng.wait_ge(sent, 4)
            eng.dma_start(rT[0:E, :], rs[:, :]).then_inc(outs, 16)
            eng.wait_ge(outs, 32)


def expert_ffn(nc, core, w_gate, wg, wu, wd, sg, su, sd, gate):
    E, K, I = wg.shape[0], 4, wg.shape[2]
    SI = sg.shape[1]
    TAIL = I - 2 * P
    PART = P - TAIL
    NTAIL = E * TAIL // P
    assert TAIL == 3 * PART and SI == 5 * P + P // 2
    TB = 512
    STEPS = T // TB
    LOOPED = E + NTAIL // 2 + 2
    rT = nc.dram_tensor("b_rT", [E + 1, T], F32, kind="Internal").ap()
    with ExitStack() as ctx:
        sb = lambda n, shape, dt=F32: ctx.enter_context(nc.sbuf_tensor("b_" + n, shape, dt))
        sem = semaphores(nc, ctx, "b_")
        sems = lambda n: [sem(f"{n}{c}") for c in range(2)]
        xT = [sb(f"xT{i}", [P, KD, T], F32R) for i in range(2)]
        with nc.sbuf_tensor("b_logits", [P, NT, E], F32) as logits:
            turned_tokens(nc, core, "bt_", xT, w_gate, E, logits[:, :, :])
            expert_router(nc, core, logits[:, :, :], E, K, rT)

        raw = sb("raw", [P, 2, 3, KD * P])
        wh = sb("wh", [P, 2, 2, 3, KD * P], F32R)
        wl = sb("wl", [P, 2, 2, 3, KD * P], F32R)
        rb = sb("rb", [P, 2, 2, T])
        silu, act = sb("silu", [P, 2, TB]), sb("act", [P, 2, TB])
        ah, al = sb("ah", [P, 2, TB], F32R), sb("al", [P, 2, TB], F32R)
        G = [ctx.enter_context(nc.psum_tensor(f"b_G{i}", [P, TB], F32)) for i in range(2)]
        U = [ctx.enter_context(nc.psum_tensor(f"b_U{i}", [P, TB], F32)) for i in range(2)]
        Y = [ctx.enter_context(nc.psum_tensor(f"b_Y{i}", [P, D], F32)) for i in range(4)]
        raw_in, w_hi, w_lo = sems("raw_in"), sems("w_hi"), sems("w_lo")
        rb_in = [sems(f"rb_in_{s}_") for s in range(2)]
        gu_done, silu_done, up_done, act_done, a_hi, a_lo = [
            sems(n) for n in ("gu_done", "silu_done", "up_done", "act_done", "a_hi", "a_lo")]
        y_done, y_free = sem("y_done"), sem("y_free")
        NB = TB // P
        W_DMAS, R_DMAS = 6, 2
        block = ctx.enter_context(nc.Block())


        @block.sync
        def _(eng):
            for s_ in w_lo + silu_done + up_done + a_lo:
                eng.sem_inc(s_, 1)
            eng.sem_inc(y_free, NB)
            eng.sem_inc(y_done, NB)

            def chunk(p, c, gparts, dparts, rparts):
                eng.wait_ge(w_lo[c], p + 1)
                for dst_k, cols, g_, u_ in gparts:
                    for which, src in enumerate((g_, u_)):
                        dst = raw[:, c, which, :].rearrange("p (k n) -> p k n", k=KD)[:, dst_k, cols]
                        eng.dma_start(dst, src).then_inc(raw_in[c], 16)
                for rows, src in dparts:
                    eng.dma_start(raw[rows, c, 2, :], src).then_inc(raw_in[c], 16)
                assert 2 * len(gparts) + len(dparts) == W_DMAS and len(rparts) == R_DMAS

            allk, halves = slice(0, KD), (slice(0, KD // 2), slice(KD // 2, KD))
            allc = slice(0, P)

            def whole(w3, e, h, cols):
                return w3[bass.ds(e, 1)].rearrange("o (k p) n -> p (o k) n", p=P)[:, h, cols]

            def load(p, s, c, gparts, dparts, rparts, first=False):
                chunk(p, c, gparts, dparts, rparts)
                if not first:
                    eng.wait_ge(up_done[c], STEPS * (p - 1) + 1)
                for rows, row in rparts:
                    eng.dma_start(rb[rows, s, c, :], rT[row, :].rearrange("o t -> (o t)")
                                  .partition_broadcast(rows.stop - rows.start)).then_inc(rb_in[s][c], 16)

            def load_whole(p, s, e, first=False):
                for c in range(2):
                    cols = slice(c * P, (c + 1) * P)
                    hp = P // 2
                    load(p, s, c, [(h, allc, whole(wg, e, h, cols), whole(wu, e, h, cols)) for h in halves],
                         [(slice(i * hp, (i + 1) * hp),
                           wd[bass.ds(e, 1), c * P + i * hp:c * P + (i + 1) * hp, :].rearrange("o i n -> (o i) n"))
                          for i in range(2)],
                         [(slice(i * hp, (i + 1) * hp), bass.ds(e, 1)) for i in range(2)], first)

            def load_tail(p, s, n0):
                for c in range(2):
                    n = n0 + c
                    group = n // 3
                    e, f, at = n + group, group * 4 + 3, (n % 3) * PART + 2 * P
                    load(p, s, c,
                         [(allk, slice(0, TAIL), whole(wg, e, allk, slice(2 * P, I)), whole(wu, e, allk, slice(2 * P, I))),
                          (allk, slice(TAIL, P), whole(wg, f, allk, bass.ds(at, PART)),
                           whole(wu, f, allk, bass.ds(at, PART)))],
                         [(slice(0, TAIL), wd[bass.ds(e, 1), 2 * P:I, :].rearrange("o i n -> (o i) n")),
                          (slice(TAIL, P), wd[bass.ds(f, 1), bass.ds(at, PART), :].rearrange("o i n -> (o i) n"))],
                         [(slice(0, TAIL), bass.ds(e, 1)), (slice(TAIL, P), bass.ds(f, 1))])

            def load_shared(p, s, n0):
                sk = lambda a, h, c0, c1: a.rearrange("(k p) n -> p k n", p=P)[:, h, c0:c1]
                for c in range(2):
                    c0, c1 = (n0 + c) * P, min((n0 + c + 1) * P, SI)
                    w = c1 - c0
                    load(p, s, c, [(h, slice(0, w), sk(sg, h, c0, c1), sk(su, h, c0, c1)) for h in halves],
                         [(slice(i * w // 2, (i + 1) * w // 2), sd[c0 + i * w // 2:c0 + (i + 1) * w // 2, :])
                          for i in range(2)],
                         [(slice(i * w // 2, (i + 1) * w // 2), slice(E, E + 1)) for i in range(2)])

            load_whole(0, 0, 0, first=True)
            load_whole(1, 1, 1, first=True)
            with eng.Fori(1, E // 2) as it:
                for s in range(2):
                    load_whole(2 * it + s, s, 2 * it + s)
            with eng.Fori(0, NTAIL // 4) as it:
                for s in range(2):
                    load_tail(E + 2 * it + s, s, 4 * it + 2 * s)
            for i in range(3):
                load_shared(E + NTAIL // 2 + i, i % 2, 2 * i)

        def width(c, last):
            return SI % P if last and c == 1 else P

        def prepare_hi(eng, p, s, c, w=P):
            eng.wait_ge(raw_in[c], (p + 1) * 16 * W_DMAS)
            if w == P:
                eng.activation(wh[:, s, c].rearrange("p a n -> p (a n)"), raw[:, c].rearrange("p a n -> p (a n)"),
                               ACT.Copy).then_inc(w_hi[c], 1)
            else:
                for a in range(2):
                    v = lambda x: x.rearrange("p (k n) -> p k n", k=KD)[:, :, 0:w]
                    eng.activation(v(wh[:, s, c, a, :]), v(raw[:, c, a, :]), ACT.Copy)
                eng.activation(wh[0:w, s, c, 2, :], raw[0:w, c, 2, :], ACT.Copy).then_inc(w_hi[c], 1)

        def prepare_lo(eng, p, s, c, w=P):
            eng.wait_ge(w_hi[c], p + 1)
            if w == P:
                flat = lambda x: x.rearrange("p a n -> p (a n)")
                eng.tensor_tensor(flat(wl[:, s, c]), flat(raw[:, c]), flat(r32(wh[:, s, c])),
                                  ALU.subtract).then_inc(w_lo[c], 1)
            else:
                for a in range(2):
                    v = lambda x: x.rearrange("p (k n) -> p k n", k=KD)[:, :, 0:w]
                    eng.tensor_tensor(v(wl[:, s, c, a, :]), v(raw[:, c, a, :]), v(r32(wh[:, s, c, a, :])), ALU.subtract)
                eng.tensor_tensor(wl[0:w, s, c, 2, :], raw[0:w, c, 2, :], r32(wh[0:w, s, c, 2, :]),
                                  ALU.subtract).then_inc(w_lo[c], 1)

        @block.tensor
        def _(eng):
            def gate_up(n, s, i, c, w):
                eng.wait_ge(silu_done[c], n + 1)
                eng.wait_ge(up_done[c], n + 1)
                for a, bank in enumerate((G[c], U[c])):
                    j = 0
                    for w_, x_ in ((wh, 0), (wh, 1), (wl, 0)):
                        for k in range(KD):
                            m = eng.matmul(bank[0:w, :], w_[:, s, c, a, k * P:k * P + w],
                                           xT[x_][:, k, i * TB:(i + 1) * TB], start=(j == 0), stop=(j == 3 * KD - 1))
                            j += 1
                m.then_inc(gu_done[c], 1)

            def down(n, s, i, w1):
                for b in range(NB):
                    eng.wait_ge(y_free, NB * n + b + 1)
                    if b == 0:
                        eng.wait_ge(a_lo[0], n + 2)
                    t = slice(b * P, (b + 1) * P)
                    eng.matmul(Y[b][:, :], ah[:, 0, t], wh[:, s, 0, 2, :], start=True, stop=False)
                    eng.matmul(Y[b][:, :], ah[:, 0, t], wl[:, s, 0, 2, :], start=False, stop=False)
                    eng.matmul(Y[b][:, :], al[:, 0, t], wh[:, s, 0, 2, :], start=False, stop=False)
                eng.wait_ge(a_hi[1], n + 1)
                for b in range(NB):
                    t = slice(b * P, (b + 1) * P)
                    eng.matmul(Y[b][:, :], ah[0:w1, 1, t], wh[0:w1, s, 1, 2, :], start=False, stop=False)
                    eng.matmul(Y[b][:, :], ah[0:w1, 1, t], wl[0:w1, s, 1, 2, :], start=False, stop=False)
                eng.wait_ge(a_lo[1], n + 2)
                for b in range(NB):
                    t = slice(b * P, (b + 1) * P)
                    eng.matmul(Y[b][:, :], al[0:w1, 1, t], wh[0:w1, s, 1, 2, :], start=False, stop=True)\
                       .then_inc(y_done, 1)

            def pair(p, s, last=False):
                for i in range(STEPS):
                    n = STEPS * p + i
                    for c in range(2):
                        if i == 0:
                            eng.wait_ge(w_lo[c], p + 2)
                        gate_up(n, s, i, c, width(c, last))
                    down(n, s, i, width(1, last))

            with eng.Fori(0, LOOPED // 2) as it:
                for s in range(2):
                    pair(2 * it + s, s)
            pair(LOOPED, 0, last=True)

        @block.scalar
        def _(eng):
            def step(n, c, w):
                eng.wait_ge(gu_done[c], n + 1)
                eng.activation(silu[0:w, c, :], G[c][0:w, :], ACT.Silu).then_inc(silu_done[c], 1)
                eng.wait_ge(act_done[c], n + 1)
                eng.activation(ah[0:w, c, :], act[0:w, c, :], ACT.Copy).then_inc(a_hi[c], 1)

            def pair(p, s, last=False, before_last=False):
                for i in range(STEPS):
                    for c in range(2):
                        step(STEPS * p + i, c, width(c, last))
                    if i in (0, 1) and not last:
                        if i == 0:
                            eng.wait_ge(y_done, NB * STEPS * p + NB)
                        prepare_hi(eng, p + 1, 1 - s, i, width(i, before_last))

            for c in range(2):
                prepare_hi(eng, 0, 0, c)
            with eng.Fori(0, LOOPED // 2 - 1) as it:
                for s in range(2):
                    pair(2 * it + s, s)
            pair(LOOPED - 2, 0)
            pair(LOOPED - 1, 1, before_last=True)
            pair(LOOPED, 0, last=True)

        @block.gpsimd
        def _(eng):
            def pair(p, s, last=False, before_last=False):
                for i in range(STEPS):
                    n = STEPS * p + i
                    for c in range(2):
                        w = width(c, last)
                        eng.wait_ge(a_hi[c], n + 1)
                        eng.tensor_tensor(al[0:w, c, :], act[0:w, c, :], r32(ah[0:w, c, :]),
                                          ALU.subtract).then_inc(a_lo[c], 1)
                    if i in (0, 1) and not last:
                        prepare_lo(eng, p + 1, 1 - s, i, width(i, before_last))

            for c in range(2):
                prepare_lo(eng, 0, 0, c)
            with eng.Fori(0, LOOPED // 2 - 1) as it:
                for s in range(2):
                    pair(2 * it + s, s)
            pair(LOOPED - 2, 0)
            pair(LOOPED - 1, 1, before_last=True)
            pair(LOOPED, 0, last=True)

        @block.vector
        def _(eng):
            def pair(it, s, last=False):
                for i in range(STEPS):
                    n = STEPS * (2 * it + s) + i
                    for c in range(2):
                        w = width(c, last)
                        if i == 0:
                            eng.wait_ge(rb_in[s][c], (it + 1) * 16 * R_DMAS)
                        eng.wait_ge(gu_done[c], n + 1)
                        eng.wait_ge(a_lo[c], n + 1)
                        eng.tensor_tensor(act[0:w, c, :], U[c][0:w, :], rb[0:w, s, c, i * TB:(i + 1) * TB],
                                          ALU.mult).then_inc(up_done[c], 1)
                        eng.wait_ge(silu_done[c], n + 2)
                        eng.wait_ge(up_done[c], n + 2)
                        eng.tensor_tensor(act[0:w, c, :], act[0:w, c, :], silu[0:w, c, :],
                                          ALU.mult).then_inc(act_done[c], 1)
                    for b in range(NB):
                        eng.wait_ge(y_done, NB * n + b + 1 + NB)
                        x = core.X[:, i * NB + b, :]
                        eng.scalar_tensor_tensor(out=x, in0=Y[b][:, :], scalar=gate, in1=x, op0=ALU.mult,
                                                 op1=ALU.add).then_inc(y_free, 1)

            with eng.Fori(0, LOOPED // 2) as it:
                for s in range(2):
                    pair(it, s)
            pair(LOOPED // 2, 0, last=True)


def normed_attention(nc, core, ctx_d, Wq, bq, Wk, bk, Wv, bv, Wkv_dca, bkv_dca, qn_w, qn_b, kn_w, kn_b,
                     kn_dca_w, kn_dca_b, Wo, bo_d, gate):
    H, HD = 16, 32
    DCA = 16
    MAIN = S - DCA
    MT = MAIN - P
    LO_HI, MAXROW = 2 * HD, 3 * HD
    NROW = 4
    VC = 2 * HD + 2
    GH = 8
    NG = H // GH
    LEAD = 12
    QH = 2
    NQ = H // QH
    SCALE = 1.0 / HD ** 0.5

    with ExitStack() as ctx:
        sb = lambda name, shape, dt=F32: ctx.enter_context(nc.sbuf_tensor("c_" + name, shape, dt))
        sem = semaphores(nc, ctx, "c_")
        wq = [sb(f"wq{i}", [P, KD, D], F32R) for i in range(2)]
        wkv = [sb(f"wkv{i}", [P, KC, 2 * D], F32R) for i in range(2)]
        wdc = [sb(f"wdc{i}", [P, KC, 2 * D], F32R) for i in range(2)]
        wo = [sb(f"wo{i}", [P, KD, D], F32R) for i in range(2)]
        lnsc = sb("lnsc", [P, NT, 2])

        bqt, bkt, bvt, bvd = sb("bq", [P, D]), sb("bk", [P, BT, D]), sb("bv", [P, D]), sb("bvd", [P, D])
        bo = sb("bo", [P, D])
        lnw = sb("lnw", [P, 3, 2, HD])
        ind = sb("ind", [P, BT, NROW])
        ctxb = sb("ctx", [P, BT, CD])
        xn = sb("xn", [P, BT, D])
        att = xn
        scb = sb("scb", [P, BT, 2])
        xT = [sb(f"xT{i}", [P, KD, S], F32R) for i in range(2)]
        aT = xT
        cT = [sb(f"cT{i}", [P, KC, S], F32R) for i in range(2)]
        cD = [sb(f"cD{i}", [P, KC, P], F32R) for i in range(2)]
        cen = sb("cen", [P, 4, D])
        sq = sb("sq", [P, D])
        y = sq
        sm, ss, lw = sb("sm", [P, 4, H]), sb("ss", [P, 4 * H]), sb("lw", [P, 3, 4 * H])
        aug = sb("aug", [P, 2, H, P])
        qT = sb("qT", [P, H, S], F32R)
        kT = sb("kT", [P, H, S], F32R)
        V = sb("V", [P, BT, H, VC])
        PT = sb("PT", [P, 2, BT, S])
        oT = sb("oT", [VC, 2, QH * S])
        nm = sb("nm", [P, H, 2, BT])
        nms = sb("nms", [P, BT, NROW * GH])
        nmT = sb("nmT", [NROW * GH, NG, S])
        rden = sb("rden", [P, QH * BT, 2])
        nrm = sq[:, 0:QH * BT * 2 * HD].rearrange("p (x m e) -> p x m e", m=2, e=HD)

        W = [ctx.enter_context(nc.psum_tensor(f"c_W{i}", [P, 512], F32)) for i in range(2)]
        SM = [ctx.enter_context(nc.psum_tensor(f"c_SM{i}", [P, 512], F32)) for i in range(2)]
        ST = [ctx.enter_context(nc.psum_tensor(f"c_ST{i}", [P, 512], F32)) for i in range(2)]
        O = [ctx.enter_context(nc.psum_tensor(f"c_O{i}", [P, 512], F32)) for i in range(2)]

        tables_in, cleared, consts = sem("tables_in"), sem("cleared"), sem("consts")
        ctx_loaded, xn_ready, xT_hi = sem("ctx_loaded"), sem("xn_ready"), sem("xT_hi")
        scaled, normed, pseq = sem("scaled"), sem("normed"), sem("pseq")
        normed_q0 = sem("normed_q0")
        aug_hi, aug_lo = [[sem(f"{n}{w}") for w in "qk"] for n in ("aug_hi", "aug_lo")]
        nms_ready = sem("nms_ready")
        max_rows = [sem(f"max_rows{g}") for g in range(NG)]
        exp_done, weighted_done, aT_hi, vseq, att_ready = [
            sem(n) for n in ("exp_done", "weighted_done", "aT_hi", "vseq", "att_ready")]
        Wf, We = [[sem(f"{n}{i}") for i in range(2)] for n in ("W_filled", "W_free")]
        SMf, SMe = [[sem(f"{n}{i}") for i in range(2)] for n in ("SM_filled", "SM_free")]
        STf = [sem(f"ST_filled{i}") for i in range(2)]
        Oe = [sem(f"O_free{i}") for i in range(2)]

        FIRST_C, FIRST_K = 0, (1, 2)
        EARLY = 3
        X_TR = [3, 4]
        PROJ = {(0, "q"): 5, (0, "v"): 6, (1, "q"): 7, (1, "v"): 8, (1, "d"): 9}
        AUG_TR = {(t, w, i): 10 + 8 * t + 4 * (w == "q") + i for t in range(BT) for w in "kq" for i in range(4)}
        MAX_TR, O_TR = [26, 28], [27, 29, 31, 33, 35, 36, 37, 38]
        NEXT_C, NEXT_K = 30, (32, 34)
        A_TR = [39, 40]
        OUT = [41, 42]
        ITEMS = 40
        C_HEAD, K_HEAD = 6, (8, 10)
        X = core.X
        NORMED = [(0, "k"), (1, "k"), (0, "q"), (1, "q")]

        def rings(it):
            return Ring(Wf, We, ITEMS), Ring(SMf, SMe, H), Ring(STf, STf, H), Ring(Oe, Oe, NQ)

        def weighted_norm(eng, n, which):
            t, w = NORMED[n]
            i = 0 if w == "q" else 1 + t
            d = cen[:, n, :].rearrange("p (h e) -> p h e", h=H)
            return eng.tensor_tensor(d, d, lnw[:, i, which, :].unsqueeze(1).to_broadcast([P, H, HD]),
                                     (ALU.mult, ALU.add)[which])

        def leave_low(eng, b, n):
            t, w = NORMED[n]
            a = "qk".index(w)
            lo = LO_HI if a == 0 else HD
            eng.wait_ge(aug_hi[a], (b * BT + t + 1) * 2)
            if w == "k":
                flags = ind[:, t, :].unsqueeze(1).to_broadcast([P, H, NROW])
                eng.tensor_tensor(aug[:, 1, :, MAXROW:MAXROW + NROW], flags, flags, ALU.mult)
            eng.tensor_tensor(aug[:, a, :, lo:lo + HD], cen[:, n, :].rearrange("p (h e) -> p h e", h=H),
                              aug[:, a, :, 0:HD], ALU.subtract).then_inc(aug_lo[a], 1)

        def late(j, last):
            return j - sum(j > n for n in (NEXT_C,) + NEXT_K) if last else j

        def every_batch(eng, step):
            with eng.Fori(0, B - 1) as b:
                step(b, False)
            step(B - 1, True)

        first_ring = Ring(Wf, We, ITEMS)

        def evacuate_turned(eng, it, Wr, t, w, which):
            for i in range(4):
                j = AUG_TR[t, w, i]
                if j % 2 != which:
                    continue
                eng.wait_ge(*Wr.until_filled(it, j))
                dst = (qT if w == "q" else kT)[:, 4 * i:4 * i + 4, t * P:(t + 1) * P]
                src = W[j % 2][:, :].rearrange("p (g n) -> p g n", g=4)
                if which == 0:
                    eng.activation(dst, src, ACT.Copy).then_inc(We[j % 2], 1)
                else:
                    eng.tensor_copy(dst, src).then_inc(We[j % 2], 1)

        assert FIRST_C % 2 == NEXT_C % 2 == 0

        def context_parts():
            w = W[0][:, :].rearrange("p (t k n) -> p t k n", t=BT, k=KC)
            return [(lambda i: cT[i][:, :, 0:P], cT[0][:, :, 0:P], w[:, 0]),
                    (lambda i: cT[i][:, :, P:MAIN], cT[0][:, :, P:MAIN], w[:, 1, :, 0:MT]),
                    (lambda i: cD[i][:, :, MT:P], cD[0][:, :, MT:P], w[:, 1, :, MT:P])]

        before_loop = Count()
        def load_tables(eng):
            eng.wait_ge(cleared, 1)
            loads = [(bqt[:, :], bq), (bo[:, :], bo_d), (bvd[MT:P, :], bkv_dca[D:2 * D]),
                     (bkt[MT:P, 1, :], bkv_dca[0:D])]
            for half, b_ in enumerate((bk, bv)):
                v = b_.rearrange("(h s e) -> s h e", s=2, e=HD)
                cols = slice(half * D // 2, (half + 1) * D // 2)
                fold = lambda a: a.rearrange("p (h e) -> p h e", e=HD)
                loads += [(fold(bkt[:, 0, cols]), v[0]), (fold(bkt[0:MT, 1, cols]), v[0]),
                          (fold(bvt[:, cols]), v[1])]
            for i, (a, b_) in enumerate(((qn_w, qn_b), (kn_w, kn_b))):
                loads += [(lnw[:, i, 0, :], a), (lnw[:, i, 1, :], b_)]
            loads += [(lnw[0:MT, 2, 0, :], kn_w), (lnw[0:MT, 2, 1, :], kn_b),
                      (lnw[MT:P, 2, 0, :], kn_dca_w), (lnw[MT:P, 2, 1, :], kn_dca_b)]
            for dst, src in loads:
                eng.dma_start(dst, src.partition_broadcast(dst.shape[0])).then_inc(tables_in, 16)
            eng.wait_ge(tables_in, 16 * len(loads))

        def indicators(eng):
            eng.memset(bvd[:, :], 0.0).then_inc(cleared, 1)
            eng.memset(ind[:, :, 0:2], 1.0).then_inc(consts, 1)
            eng.memset(ind[:, :, 2:4], 0.0).then_inc(consts, 1)
            eng.wait_ge(consts, 2)
            eng.affine_select(out=ind[:, 1, 0:2], in_=ind[:, 1, 0:2], compare_op=ALU.is_ge, fill=0.0,
                              base=MT - 1, pattern=[[0, 2]], channel_multiplier=-1).then_inc(consts, 1)
            eng.affine_select(out=ind[:, 1, 2:4], in_=ind[:, 1, 2:4], compare_op=ALU.is_ge, fill=1.0,
                              base=MT - 1, pattern=[[0, 2]], channel_multiplier=-1).then_inc(consts, 1)

        def zero_aug(eng):
            eng.memset(aug[:, :, :, :], 0.0)

        def scales_and_zeros(eng):
            c = before_loop
            st = PT[:, 0, 0, 0:6 * NT].rearrange("p (t s) -> p t s", s=6)
            llw = PT[:, 0, 1, 0:5 * NT].rearrange("p (s t) -> p s t", t=NT)
            layer_norm_scales(eng, vseq, c, X, st, llw, lnsc)
            for i in range(2):
                eng.memset(r32(cT[i][:, :, :]), 0.0)
                eng.memset(r32(cD[i][:, :, :]), 0.0)
            eng.memset(V[:, :, :, :], 0.0).then_inc(vseq, c.inc())
            eng.wait_ge(vseq, c.now)
            eng.wait_ge(consts, 4)
            for t in range(BT):
                i = eng.tensor_copy(V[:, t, :, 2 * HD:VC],
                                    ind[:, t, 0:NROW:2].unsqueeze(1).to_broadcast([P, H, 2]))
            i.then_inc(vseq, c.inc())

        kview = lambda a: a.rearrange("(k p) n -> p k n", p=P)
        split_weights(nc, "c_w", [
            (kview(Wq), wq[0][:, :, :], wq[1][:, :, :]),
            (kview(Wk), wkv[0][:, :, 0:D], wkv[1][:, :, 0:D]),
            (kview(Wv), wkv[0][:, :, D:2 * D], wkv[1][:, :, D:2 * D]),
            (kview(Wkv_dca), wdc[0][:, :, :], wdc[1][:, :, :]),
            (kview(Wo), wo[0][:, :, :], wo[1][:, :, :])],
            aug[:, :, :, :].rearrange("p a h r -> p a (h r)"),
            load_tables, scales_and_zeros, (indicators, zero_aug))

        block = ctx.enter_context(nc.Block())

        @block.sync
        def _(eng):
            def context(b):
                src = ctx_d[b:b + 1] if isinstance(b, int) else ctx_d[bass.ds(b, 1)]
                for t in range(BT):
                    eng.dma_start(ctxb[:, t, :], src[:, t * P:(t + 1) * P, :]
                                  .rearrange("o p c -> (o p) c")).then_inc(ctx_loaded, 16)

            def step(b, last):
                Wr = rings(b)[0]
                for g in range(NG):
                    eng.wait_ge(*Wr.until_freed(b, late(MAX_TR[g], last)))
                    for r in range(NROW):
                        eng.dma_start(r32(qT[MAXROW + r:MAXROW + r + 1, GH * g:GH * (g + 1), :]),
                                      nmT[r * GH:(r + 1) * GH, g, :]).then_inc(max_rows[g], 16)
                    if g == 0 and not last:
                        context(b + 1)

            context(0)
            every_batch(eng, step)

        @block.gpsimd
        def _(eng):
            def weigh(b, n):
                eng.wait_ge(scaled, b * 4 + n + 1)
                weighted_norm(eng, n, 0).then_inc(pseq, 1)
                eng.wait_ge(pseq, b * 3 + min(n, 2) + 1)
                weighted_norm(eng, n, 1).then_inc(normed, 1)
                if n == 0:
                    leave_low(eng, b, n)

            def step(b, last):
                weigh(b, 3)
                if not last:
                    for n in (0, 1):
                        weigh(b + 1, n)

            for n in (0, 1):
                weigh(0, n)
            every_batch(eng, step)

        @block.vector
        def _(eng):
            def low_context(b):
                eng.wait_ge(xT_hi, b * 3 + 1)
                for dst, hi, src in context_parts():
                    i = eng.tensor_tensor(dst(1), src, r32(hi), ALU.subtract)
                i.then_inc(We[0], 1)

            def deviations(c, Wr, it, j, n):
                t, w = NORMED[n]
                d = cen[:, n, :]
                dh = d.rearrange("p (h e) -> p h e", h=H)
                eng.wait_ge(*Wr.until_filled(it, j))
                eng.tensor_tensor(d, W[j % 2][:, :], bqt[:, :] if w == "q" else bkt[:, t, :],
                                  ALU.add).then_inc(We[j % 2], 1)
                eng.wait_ge(*Wr.until_freed(it, j))
                eng.tensor_reduce(sm[:, n, :], dh, AX.X, ALU.add).then_inc(vseq, c.inc())
                eng.wait_ge(vseq, c.now)
                eng.tensor_scalar(sm[:, n, :], sm[:, n, :], 1.0 / HD, None, ALU.mult).then_inc(vseq, c.inc())
                eng.wait_ge(vseq, c.now)
                eng.tensor_tensor(dh, dh, sm[:, n, :].unsqueeze(2).to_broadcast([P, H, HD]),
                                  ALU.subtract).then_inc(vseq, c.inc())
                eng.wait_ge(vseq, c.now)
                eng.tensor_tensor(sq[:, :], d, d, ALU.mult).then_inc(vseq, c.inc())
                eng.wait_ge(vseq, c.now)
                eng.tensor_reduce(ss[:, n * H:(n + 1) * H], sq[:, :].rearrange("p (h e) -> p h e", h=H),
                                  AX.X, ALU.add).then_inc(vseq, c.inc())

            def over_spread(c, tiles):
                part = slice(tiles[0] * H, (tiles[1] + 1) * H)
                eng.wait_ge(vseq, c.now)
                eng.tensor_scalar(ss[:, part], ss[:, part], 1.0 / HD, 1e-6, ALU.mult, ALU.add).then_inc(vseq, c.inc())
                rsqrt_steps(eng, vseq, c, ss[:, part], lw[:, 0, part], lw[:, 1, part], lw[:, 2, part])
                eng.wait_ge(vseq, c.now)
                for n in tiles:
                    dh = cen[:, n, :].rearrange("p (h e) -> p h e", h=H)
                    eng.tensor_tensor(dh, dh, lw[:, 0, n * H:(n + 1) * H].unsqueeze(2).to_broadcast([P, H, HD]),
                                      ALU.mult).then_inc(scaled, 1)

            low_context(0)
            for n in (0, 1):
                deviations(before_loop, first_ring, 0, FIRST_K[n], n)
            over_spread(before_loop, (0, 1))
            start = before_loop.now
            KEYS = 2 * 5 + 13
            PER = 2 + 2 * KEYS + NG + NQ * 2 - 1 + 2

            def step(b, last):
                c = Count(b * PER + start)
                Wr, SMr, STr, Or = rings(b)
                eng.wait_ge(vseq, c.now)
                eng.tensor_copy(scb[:, :, :], lnsc[:, bass.ds(2 * b, 2), :]).then_inc(vseq, c.inc())
                eng.wait_ge(vseq, c.now)
                for t in range(BT):
                    eng.tensor_scalar(xn[:, t, :], X[:, bass.ds(2 * b + t, 1), :].rearrange("p o d -> p (o d)"),
                                      scb[:, t, 0:1], scb[:, t, 1:2], ALU.mult, ALU.add).then_inc(xn_ready, 1)
                for t in range(BT):
                    eng.wait_ge(xT_hi, b * 3 + t + 2)
                    eng.tensor_tensor(xT[1][:, :, t * P:(t + 1) * P],
                                      W[X_TR[t] % 2][:, :].rearrange("p (k n) -> p k n", k=KD),
                                      r32(xT[0][:, :, t * P:(t + 1) * P]), ALU.subtract).then_inc(We[X_TR[t] % 2], 1)

                def values(t, w):
                    j = PROJ[t, w]
                    eng.wait_ge(*Wr.until_filled(b, j))
                    r0, r1 = (0, P if t == 0 else MT) if w == "v" else (P - 32, P)
                    at = 0 if w == "v" else HD
                    table = bvt if w == "v" else bvd
                    hv = lambda a: a.rearrange("p (h e) -> p h e", h=H)
                    eng.tensor_tensor(V[r0:r1, t, :, at:at + HD], hv(W[j % 2][r0:r1, :]), hv(table[r0:r1, :]),
                                      ALU.add).then_inc(We[j % 2], 1)

                deviations(c, Wr, b, PROJ[0, "q"], 2)
                values(0, "v")
                deviations(c, Wr, b, PROJ[1, "q"], 3)
                values(1, "v")
                values(1, "d")
                evacuate_turned(eng, b, Wr, 0, "k", 1)
                over_spread(c, (2, 3))
                eng.wait_ge(scaled, b * 4 + 3)
                weighted_norm(eng, 2, 0).then_inc(vseq, c.inc())
                eng.wait_ge(vseq, c.now)
                weighted_norm(eng, 2, 1).then_inc(normed_q0, 1)
                leave_low(eng, b, 1)
                leave_low(eng, b, 2)
                evacuate_turned(eng, b, Wr, 0, "q", 1)
                evacuate_turned(eng, b, Wr, 1, "k", 1)
                leave_low(eng, b, 3)
                evacuate_turned(eng, b, Wr, 1, "q", 1)

                def top(h):
                    eng.wait_ge(*SMr.until_filled(b, h))
                    v = SM[h % 2][:, :].rearrange("p (t k) -> p t k", t=BT)
                    eng.tensor_reduce(nm[:, h, 0, :], v[:, :, 0:MAIN], AX.X, ALU.max, negate=True)
                    eng.tensor_reduce(nm[:, h, 1, :], v[:, :, MAIN:S], AX.X, ALU.max,
                                      negate=True).then_inc(SMe[h % 2], 1)
                    if h % GH == GH - 1:
                        g = h // GH
                        for i in (h - 1, h):
                            eng.wait_ge(*SMr.until_freed(b, i))
                        if g:
                            eng.wait_ge(*Wr.until_freed(b, late(MAX_TR[g - 1], last)))
                        src = nm[:, g * GH:(g + 1) * GH, :, :].rearrange("p a m t -> p t m a")
                        dst = nms[:, :, :].rearrange("p t (m j a) -> p t m j a", m=2, j=2)
                        for t in range(BT):
                            i = eng.tensor_copy(dst[:, t, :, 0, :].bitcast(F32R), src[:, t])
                        i.then_inc(vseq, c.inc())
                        eng.wait_ge(vseq, c.now)
                        for t in range(BT):
                            i = eng.tensor_tensor(dst[:, t, :, 1, :], src[:, t], dst[:, t, :, 0, :], ALU.subtract)
                        i.then_inc(nms_ready, 1)

                def normalise(q):
                    j = late(O_TR[q], last)
                    o = W[j % 2][:, 0:QH * BT * VC].rearrange("p (x e) -> p x e", e=VC)
                    eng.wait_ge(*Wr.until_filled(b, j))
                    eng.wait_ge(vseq, c.now)
                    if q:
                        eng.wait_ge(*Wr.until_freed(b, late(O_TR[q - 1], last)))
                    eng.reciprocal(rden[:, :, :], o[:, :, 2 * HD:VC]).then_inc(vseq, c.inc())
                    eng.wait_ge(vseq, c.now)
                    eng.tensor_tensor(nrm[:, :, :, :], o[:, :, 0:2 * HD].rearrange("p x (m e) -> p x m e", m=2),
                                      rden[:, :, :].unsqueeze(3).to_broadcast([P, QH * BT, 2, HD]),
                                      ALU.mult).then_inc(We[j % 2], 1)
                    eng.wait_ge(*Wr.until_freed(b, j))
                    dst = att[:, :, q * QH * HD:(q + 1) * QH * HD].rearrange("p t (h e) -> p h t e", h=QH)
                    nv = nrm[:, :, :, :].rearrange("p (h t) m e -> p h t m e", h=QH)
                    i = eng.tensor_tensor(dst, nv[:, :, :, 0, :], nv[:, :, :, 1, :], ALU.add)
                    if q == NQ - 1:
                        i.then_inc(att_ready, 1)
                    else:
                        i.then_inc(vseq, c.inc())

                for h in range(LEAD):
                    top(h)
                for h in range(H):
                    if h + LEAD < H:
                        top(h + LEAD)
                    if h % 2 == 1 and h >= 3:
                        normalise((h - 3) // 2)
                    if not last:
                        if h == C_HEAD:
                            low_context(b + 1)
                        for n in (0, 1):
                            if h == K_HEAD[n]:
                                deviations(c, Wr, b, NEXT_K[n], n)
                normalise(NQ - 1)
                for t in range(BT):
                    eng.wait_ge(aT_hi, b * BT + t + 1)
                    eng.tensor_tensor(aT[1][:, :, t * P:(t + 1) * P],
                                      W[late(A_TR[t], last) % 2][:, :].rearrange("p (k n) -> p k n", k=KD),
                                      r32(aT[0][:, :, t * P:(t + 1) * P]),
                                      ALU.subtract).then_inc(We[late(A_TR[t], last) % 2], 1)
                if not last:
                    over_spread(c, (0, 1))
                for t in range(BT):
                    j = late(OUT[t], last)
                    xx = X[:, bass.ds(2 * b + t, 1), :].rearrange("p o d -> p (o d)")
                    eng.wait_ge(*Wr.until_filled(b, j))
                    eng.wait_ge(vseq, c.now)
                    eng.tensor_tensor(y[:, :], W[j % 2][:, :], bo[:, :], ALU.add).then_inc(We[j % 2], 1)
                    eng.wait_ge(*Wr.until_freed(b, j))
                    eng.scalar_tensor_tensor(out=xx, in0=y[:, :], scalar=gate, in1=xx,
                                             op0=ALU.mult, op1=ALU.add).then_inc(vseq, c.inc())
                assert c.n == PER - KEYS * last

            every_batch(eng, step)

        @block.scalar
        def _(eng):
            def high_context(Wr, it, j):
                eng.wait_ge(*Wr.until_filled(it, j))
                for dst, _, src in context_parts():
                    i = eng.activation(dst(0), src, ACT.Copy)
                i.then_inc(xT_hi, 1)

            def rounded(b, n):
                t, w = NORMED[n]
                a = "qk".index(w)
                heads = cen[:, n, :].rearrange("p (h e) -> p h e", e=HD)
                if n == 2:
                    eng.wait_ge(normed_q0, b + 1)
                else:
                    eng.wait_ge(normed, b * 3 + min(n, 2) + 1)
                for at in (0, HD if a == 0 else LO_HI):
                    eng.activation(aug[:, a, :, at:at + HD].bitcast(F32R), heads, ACT.Copy).then_inc(aug_hi[a], 1)

            high_context(first_ring, 0, FIRST_C)
            rounded(0, 0)

            def step(b, last):
                Wr, SMr, STr, Or = rings(b)
                for t in range(BT):
                    eng.wait_ge(*Wr.until_filled(b, X_TR[t]))
                    eng.activation(xT[0][:, :, t * P:(t + 1) * P],
                                   W[X_TR[t] % 2][:, :].rearrange("p (k n) -> p k n", k=KD),
                                   ACT.Copy).then_inc(xT_hi, 1)
                evacuate_turned(eng, b, Wr, 0, "k", 0)
                eng.wait_ge(*Wr.until_filled(b, AUG_TR[0, "k", 3]))
                rounded(b, 1)
                rounded(b, 2)
                evacuate_turned(eng, b, Wr, 0, "q", 0)
                eng.wait_ge(*Wr.until_filled(b, AUG_TR[0, "q", 3]))
                rounded(b, 3)
                evacuate_turned(eng, b, Wr, 1, "k", 0)
                evacuate_turned(eng, b, Wr, 1, "q", 0)

                def maxima(g):
                    j = late(MAX_TR[g], last)
                    eng.wait_ge(*Wr.until_filled(b, j))
                    eng.activation(nmT[:, g, :], W[j % 2][0:NROW * GH, 0:S], ACT.Copy).then_inc(We[j % 2], 1)

                def turned_outputs(q):
                    eng.wait_ge(weighted_done, b * H + (q + 1) * QH)
                    if q >= 2:
                        eng.wait_ge(*Wr.until_filled(b, late(O_TR[q - 2], last)))
                    eng.activation(oT[:, q % 2, :], O[q % 2][0:VC, :], ACT.Copy).then_inc(Oe[q % 2], 1)

                maxima(0)
                for h in range(H):
                    eng.wait_ge(*STr.until_filled(b, h))
                    if h >= 2:
                        eng.wait_ge(weighted_done, b * H + h - 1)
                    eng.activation(PT[:, h % 2, :, :].rearrange("p t s -> p (t s)"), ST[h % 2][:, :], ACT.Exp,
                                   scale=SCALE).then_inc(exp_done, 1)
                    if h == 5:
                        maxima(1)
                    if h % 2 == 0 and h >= 2:
                        turned_outputs((h - 2) // 2)
                    if not last and h == C_HEAD + 1:
                        high_context(Wr, b, NEXT_C)
                turned_outputs(NQ - 1)
                for t in range(BT):
                    eng.wait_ge(*Wr.until_filled(b, late(A_TR[t], last)))
                    eng.activation(aT[0][:, :, t * P:(t + 1) * P],
                                   W[late(A_TR[t], last) % 2][:, :].rearrange("p (k n) -> p k n", k=KD),
                                   ACT.Copy).then_inc(aT_hi, 1)
                if not last:
                    rounded(b + 1, 0)

            every_batch(eng, step)

        @block.tensor
        def _(eng):
            for s_ in We + SMe + Oe:
                eng.sem_inc(s_, 1)

            def turn(Wr, it, j, srcs):
                eng.wait_ge(*Wr.until_free(it, j))
                at = 0
                for s in srcs:
                    k = s.shape[0]
                    m = eng.transpose(W[j % 2][0:s.shape[1], at:at + k], s, core.ident[0:k, 0:k])
                    at += k
                m.then_inc(Wf[j % 2], 1)

            def product(Wr, it, j, terms):
                eng.wait_ge(*Wr.until_free(it, j))
                total, n = 3 * sum(k for _, _, k in terms), 0
                for lhs, rhs, k in terms:
                    for x_, w_ in ((0, 0), (0, 1), (1, 0)):
                        for i in range(k):
                            m = eng.matmul(W[j % 2][:, :], lhs(x_, i), rhs(w_, i), start=(n == 0),
                                           stop=(n == total - 1))
                            n += 1
                m.then_inc(Wf[j % 2], 1)

            tok = lambda a, t: (lambda x_, i: a[x_][:, i, t * P:(t + 1) * P])
            cols = lambda w, c0: (lambda w_, i: w[w_][:, i, c0:c0 + D])
            heads = lambda s: (lambda w_, i: wkv[w_][:, i, :].rearrange("p (h s e) -> p s h e", s=2, e=HD)[:, s])

            def turn_context(Wr, it, j, b):
                eng.wait_ge(ctx_loaded, (b + 1) * 32)
                turn(Wr, it, j, [ctxb[:, t, k * P:(k + 1) * P] for t in range(BT) for k in range(KC)])

            def project_keys(Wr, it, j, t):
                terms = [(tok(cT, t), heads(0), KC)]
                if t:
                    terms.append((tok(cD, 0), cols(wdc, 0), KC))
                product(Wr, it, j, terms)

            turn_context(first_ring, 0, FIRST_C, 0)
            eng.wait_ge(*first_ring.until_freed(0, FIRST_C))
            for t in range(BT):
                project_keys(first_ring, 0, FIRST_K[t], t)

            def step(b, last):
                Wr, SMr, STr, Or = rings(b)
                for t in range(BT):
                    eng.wait_ge(xn_ready, b * BT + t + 1)
                    turn(Wr, b, X_TR[t], [xn[:, t, k * P:(k + 1) * P] for k in range(KD)])
                eng.wait_ge(*Wr.until_freed(b, X_TR[1]))
                product(Wr, b, PROJ[0, "q"], [(tok(xT, 0), cols(wq, 0), KD)])
                product(Wr, b, PROJ[0, "v"], [(tok(cT, 0), heads(1), KC)])
                product(Wr, b, PROJ[1, "q"], [(tok(xT, 1), cols(wq, 0), KD)])
                product(Wr, b, PROJ[1, "v"], [(tok(cT, 1), heads(1), KC)])
                product(Wr, b, PROJ[1, "d"], [(tok(cD, 0), cols(wdc, D), KC)])
                for t in range(BT):
                    for a, w in ((1, "k"), (0, "q")):
                        eng.wait_ge(aug_lo[a], b * BT + t + 1)
                        for i in range(4):
                            turn(Wr, b, AUG_TR[t, w, i], [aug[:, a, h, :] for h in range(4 * i, 4 * i + 4)])
                for i in (2, 3):
                    eng.wait_ge(*Wr.until_freed(b, AUG_TR[1, "q", i]))

                def scores_for_max(h):
                    eng.wait_ge(*SMr.until_free(b, h))
                    for t in range(BT):
                        m = eng.matmul(SM[h % 2][:, t * S:(t + 1) * S], qT[0:MAXROW, h, t * P:(t + 1) * P],
                                       kT[0:MAXROW, h, :], start=True, stop=True)
                    m.then_inc(SMf[h % 2], 1)

                def turn_maxima(g):
                    eng.wait_ge(nms_ready, b * NG + g + 1)
                    turn(Wr, b, late(MAX_TR[g], last), [nms[:, t, :] for t in range(BT)])

                def scores(h):
                    if h % GH == 0:
                        eng.wait_ge(max_rows[h // GH], (b + 1) * 16 * NROW)
                    if h >= 2:
                        eng.wait_ge(exp_done, b * H + h - 1)
                    for t in range(BT):
                        m = eng.matmul(ST[h % 2][:, t * S:(t + 1) * S], kT[0:MAXROW + NROW, h, t * P:(t + 1) * P],
                                       qT[0:MAXROW + NROW, h, :], start=True, stop=True)
                    m.then_inc(STf[h % 2], 1)

                def weighted(h):
                    q = h // QH
                    if h % QH == 0:
                        eng.wait_ge(*Or.until_free(b, q))
                    eng.wait_ge(exp_done, b * H + h + 1)
                    for k in range(BT):
                        m = eng.matmul(O[q % 2][0:VC, (h % QH) * S:(h % QH + 1) * S], V[:, k, h, :], PT[:, h % 2, k, :],
                                       start=(k == 0), stop=(k == BT - 1))
                    m.then_inc(weighted_done, 1)

                def turn_outputs(q):
                    eng.wait_ge(*Or.until_freed(b, q))
                    turn_small(late(O_TR[q], last), [oT[:, q % 2, i * P:(i + 1) * P] for i in range(QH * BT)])

                def turn_small(j, srcs):
                    eng.wait_ge(*Wr.until_free(b, j))
                    for i, s in enumerate(srcs):
                        m = eng.transpose(W[j % 2][:, i * VC:(i + 1) * VC], s, core.ident[0:VC, 0:VC])
                    m.then_inc(Wf[j % 2], 1)

                for h in range(LEAD):
                    scores_for_max(h)
                    if h == GH + 1:
                        turn_maxima(0)
                for h in range(H):
                    scores(h)
                    if h + LEAD < H:
                        scores_for_max(h + LEAD)
                    if h:
                        weighted(h - 1)
                    if h == 5:
                        turn_maxima(1)
                    if h % 2 == 1 and h >= 3:
                        turn_outputs((h - 3) // 2)
                    if not last:
                        if h == C_HEAD:
                            turn_context(Wr, b, NEXT_C, b + 1)
                        for t in range(BT):
                            if h == K_HEAD[t]:
                                if t == 0:
                                    eng.wait_ge(*Wr.until_freed(b, NEXT_C))
                                project_keys(Wr, b, NEXT_K[t], t)
                weighted(H - 1)
                turn_outputs(NQ - 1)
                eng.wait_ge(att_ready, b + 1)
                for t in range(BT):
                    turn(Wr, b, late(A_TR[t], last), [att[:, t, k * P:(k + 1) * P] for k in range(KD)])
                for t in range(BT):
                    eng.wait_ge(*Wr.until_freed(b, late(A_TR[t], last)))
                for t in range(BT):
                    product(Wr, b, late(OUT[t], last), [(tok(aT, t), cols(wo, 0), KD)])

            every_batch(eng, step)


def send_tables(eng, core, table, scattered):
    C = core.place_sums.shape[1]
    for c in range(C):
        eng.indirect_dma_start(out=table, out_offset=bass.IndirectOffsetOnAxis(ap=core.place_rows[:, c:c + 1], axis=0),
                               in_=core.place_sums[:, c, :], in_offset=None).then_inc(scattered, 16)
    eng.wait_ge(scattered, 16 * C)


def scatter_tables(nc, core, x, atoms, eaw, importance, mask_idx, table):
    E, A = eaw.shape
    NS = mask_idx.shape[0]
    C = NS // P
    H = D
    NP = 3
    HALF = C // 2
    with ExitStack() as ctx:
        sb = lambda n, shape, dt=F32: ctx.enter_context(nc.sbuf_tensor("st_" + n, shape, dt))
        sem = semaphores(nc, ctx, "st_")
        zeros = sb("zeros", [P, 4096])
        row_i, row_f = sb("row_i", [P, NS], I32), sb("row_f", [P, C, P])
        idx_i, idx_f = sb("idx_i", [P, C], I32), sb("idx_f", [P, C])
        at_col, at_row, addr, dump = (sb("at_col", [P, C], I32), sb("at_row", [P, C], I32), sb("addr", [P, C]),
                                      sb("dump", [P, C]))
        total, addr_u = core.place_sums, core.place_rows
        dump_i = sb("dump_i", [P, C], I32)
        eq = sb("eq", [P, 2, C, P], BF16)
        before, eqm = sb("before", [P, P], BF16), sb("eqm", [P, 2, P], BF16)
        ea, at_ = sb("ea", [E, A]), sb("atoms", [A, NS])
        imp = sb("imp", [E, NS])
        m1, s1 = sb("m1", [E, 1]), sb("s1", [E, 1])
        eaT = sb("eaT", [A, E])
        sig = sb("sig", [P, C * E])
        w, rest = sb("w", [P, C * E]), sb("rest", [P, C * E])
        parts = sb("parts", [P, C, NP * E + 1], BF16)
        flag = sb("flag", [P, C])
        tb = ctx.enter_context(nc.psum_tensor("st_tb", [A, E], F32))
        delta = ctx.enter_context(nc.psum_tensor("st_delta", [P, C * E], F32))
        sigT = ctx.enter_context(nc.psum_tensor("st_sigT", [P, C * E], F32))
        acc = [ctx.enter_context(nc.psum_tensor(f"st_acc{i}", [P, HALF * (NP * E + 1)], F32)) for i in range(2)]
        loaded, x_in, idx_in, imp_in, atoms_in, zeroed = [
            sem(n) for n in ("loaded", "x_in", "idx_in", "imp_in", "atoms_in", "zeroed")]
        consts, vseq, aseq, eq_ready, eq_used, parts_ready, pe_small, summed, acc_zero = [
            sem(n) for n in ("consts", "vseq", "aseq", "eq_ready", "eq_used", "parts_ready", "pe_small", "summed",
                             "acc_zero")]
        block = ctx.enter_context(nc.Block())
        ZD = H * H * E // (P * 4096)

        @block.sync
        def _(eng):
            eng.dma_start(ea[:, :], eaw).then_inc(loaded, 16)
            eng.dma_start(idx_i[:, :], mask_idx.rearrange("(p c) -> p c", p=P)).then_inc(idx_in, 16)
            eng.dma_start(row_i[:, :], mask_idx.partition_broadcast(P)).then_inc(idx_in, 16)
            eng.dma_start(imp[:, :], importance).then_inc(imp_in, 16)
            eng.dma_start(at_[:, :], atoms).then_inc(atoms_in, 16)
            xf = x.rearrange("b (t p) d -> p (b t) d", p=P)
            for q in range(4):
                eng.dma_start(core.X[:, 4 * q:4 * q + 4, :], xf[:, 4 * q:4 * q + 4, :]).then_inc(x_in, 16)
            eng.wait_ge(consts, 1)
            flat = table[0:H * H, :].rearrange("(p q r) e -> p q (r e)", p=P, q=ZD)
            for q in range(ZD):
                eng.dma_start(flat[:, q, :], zeros[:, :]).then_inc(zeroed, 16)
            eng.wait_ge(zeroed, 16 * ZD)
            eng.wait_ge(x_in, 4 * 16)

        @block.gpsimd
        def _(eng):
            eng.memset(zeros[:, :], 0.0).then_inc(consts, 1)
            eng.memset(before[:, :], 1.0).then_inc(consts, 1)
            eng.wait_ge(consts, 2)
            eng.affine_select(out=before[:, :], in_=before[:, :], compare_op=ALU.is_gt, fill=0.0, base=0,
                              pattern=[[1, P]], channel_multiplier=-1).then_inc(consts, 1)
            eng.iota(dump_i[:, :], pattern=[[1, C]], base=H * H, channel_multiplier=C).then_inc(consts, 1)

        @block.scalar
        def _(eng):
            eng.wait_ge(vseq, 1)
            eng.activation(ea[:, :], ea[:, :], ACT.Exp, bias=m1[:, 0:1], accum_out=s1[:, 0:1]).then_inc(aseq, 1)
            eng.wait_ge(imp_in, 16)
            eng.activation(imp[:, :], imp[:, :], ACT.Sigmoid).then_inc(aseq, 1)
            eng.wait_ge(pe_small, 1)
            eng.activation(eaT[:, :], tb[:, :], ACT.Copy).then_inc(aseq, 1)
            eng.wait_ge(pe_small, 2)
            eng.activation(sig[:, :], sigT[:, :], ACT.Copy).then_inc(aseq, 1)

        @block.vector
        def _(eng):
            c = Count()
            eng.wait_ge(loaded, 16)
            eng.tensor_reduce(m1[:, :], ea[:, :], AX.X, ALU.max, negate=True).then_inc(vseq, c.inc())
            eng.wait_ge(aseq, 1)
            eng.reciprocal(m1[:, :], s1[:, :]).then_inc(vseq, c.inc())
            eng.wait_ge(vseq, c.now)
            eng.tensor_scalar(ea[:, :], ea[:, :], m1[:, 0:1], None, ALU.mult).then_inc(vseq, c.inc())
            for i in range(2):
                eng.memset(acc[i][:, :], 0.0).then_inc(acc_zero, 1)
            eng.wait_ge(idx_in, 32)
            eng.tensor_copy(idx_f[:, :], idx_i[:, :]).then_inc(vseq, c.inc())
            eng.tensor_copy(row_f[:, :, :], row_i[:, :].rearrange("p (q c) -> p c q", c=C)).then_inc(vseq, c.inc())
            eng.tensor_scalar(at_col[:, :], idx_i[:, :], H - 1, 9, ALU.bitwise_and,
                              ALU.logical_shift_left).then_inc(vseq, c.inc())
            eng.tensor_scalar(at_row[:, :], idx_i[:, :], 9, None, ALU.logical_shift_right).then_inc(vseq, c.inc())
            eng.wait_ge(vseq, c.now)
            eng.tensor_tensor(addr[:, :], at_col[:, :], at_row[:, :], ALU.add).then_inc(vseq, c.inc())
            eng.wait_ge(consts, 4)
            eng.tensor_copy(dump[:, :], dump_i[:, :]).then_inc(vseq, c.inc())
            eng.wait_ge(vseq, c.now)
            eng.tensor_tensor(dump[:, :], dump[:, :], addr[:, :], ALU.subtract).then_inc(vseq, c.inc())
            eng.wait_ge(aseq, 4)
            eng.wait_ge(pe_small, 3)
            eng.tensor_tensor(w[:, :], delta[:, :], sig[:, :], ALU.mult).then_inc(vseq, c.inc())
            eng.memset(parts[:, :, NP * E:NP * E + 1], 1.0).then_inc(vseq, c.inc())
            cur = w
            for i in range(NP):
                pv = parts[:, :, i * E:(i + 1) * E]
                cv = cur[:, :].rearrange("p (c e) -> p c e", e=E)
                eng.wait_ge(vseq, c.now)
                eng.tensor_copy(pv, cv).then_inc(vseq, c.inc())
                if i < NP - 1:
                    eng.wait_ge(vseq, c.now)
                    eng.tensor_tensor(rest[:, :].rearrange("p (c e) -> p c e", e=E), cv, pv,
                                      ALU.subtract).then_inc(vseq, c.inc())
                    cur = rest
            eng.wait_ge(vseq, c.now)
            for a in range(C):
                if a >= 2:
                    eng.wait_ge(eq_used, a - 1)
                eng.tensor_scalar(eq[:, a % 2].rearrange("p c q -> p (c q)"),
                                  row_f[:, :, :].rearrange("p c q -> p (c q)"), idx_f[:, a:a + 1], None,
                                  ALU.is_equal).then_inc(vseq, c.inc())
                eng.wait_ge(vseq, c.now)
                eng.tensor_tensor(eqm[:, a % 2, :], eq[:, a % 2, a, :], before[:, :], ALU.mult).then_inc(eq_ready, 1)
            eng.wait_ge(summed, 1)
            for i in range(2):
                av = acc[i][:, :].rearrange("p (c m) -> p c m", m=NP * E + 1)
                tv = total[:, i * HALF:(i + 1) * HALF, :]
                eng.tensor_copy(tv, av[:, :, 0:E]).then_inc(vseq, c.inc())
                for q in (1, 2):
                    eng.wait_ge(vseq, c.now)
                    eng.tensor_tensor(tv, tv, av[:, :, q * E:(q + 1) * E], ALU.add).then_inc(vseq, c.inc())
                eng.tensor_scalar(flag[:, i * HALF:(i + 1) * HALF], av[:, :, NP * E], 0.5, None,
                                  ALU.is_gt).then_inc(vseq, c.inc())
            eng.wait_ge(vseq, c.now)
            eng.tensor_tensor(dump[:, :], dump[:, :], flag[:, :], ALU.mult).then_inc(vseq, c.inc())
            eng.wait_ge(vseq, c.now)
            eng.tensor_tensor(addr_u[:, :], addr[:, :], dump[:, :], ALU.add)

        @block.tensor
        def _(eng):
            eng.wait_ge(vseq, 3)
            eng.transpose(tb[:, :], ea[:, :], core.ident[0:E, 0:E]).then_inc(pe_small, 1)
            eng.wait_ge(aseq, 2)
            for c in range(C):
                m = eng.transpose(sigT[:, c * E:(c + 1) * E], imp[:, c::C], core.ident[0:E, 0:E])
            m.then_inc(pe_small, 1)
            eng.wait_ge(atoms_in, 16)
            eng.wait_ge(aseq, 3)
            for c in range(C):
                m = eng.matmul(delta[:, c * E:(c + 1) * E], at_[:, c::C], eaT[:, :], start=True, stop=True)
            m.then_inc(pe_small, 1)
            eng.wait_ge(acc_zero, 2)
            N = NP * E + 1
            for a in range(C):
                eng.wait_ge(eq_ready, a + 1)
                for b in range(C):
                    n = N if a < b else N - 1
                    o = acc[b // HALF][:, (b % HALF) * N:(b % HALF) * N + n]
                    m = eng.matmul(o, eq[:, a % 2, b, :], parts[:, a, 0:n], start=False, stop=(a == C - 1),
                                   skip_group_check=True)
                b = a
                m = eng.matmul(acc[b // HALF][:, (b % HALF) * N + N - 1:(b % HALF) * N + N], eqm[:, a % 2, :],
                               parts[:, a, N - 1:N], start=False, stop=(a == C - 1), skip_group_check=True)
                m.then_inc(eq_used if a < C - 1 else summed, 1)


def masked_router(nc, core, lg, E, gt):
    with ExitStack() as ctx:
        sb = lambda n, shape, dt=F32: ctx.enter_context(nc.sbuf_tensor("dr_" + n, shape, dt))
        sem = semaphores(nc, ctx, "dr_")
        p, rank, ex = sb("p", [P, NT, E]), sb("rank", [P, NT, E]), sb("ex", [P, NT, E])
        m1, s1 = sb("m1", [P, NT]), sb("s1", [P, NT])
        tri, g1, eq = sb("tri", [P, E, E]), sb("g1", [P, NT, E, E], BF16), sb("eq", [P, NT, E, E], BF16)
        shifted, exped, vseq, consts = [sem(n) for n in ("shifted", "exped", "vseq", "consts")]
        block = ctx.enter_context(nc.Block())
        bc = lambda a: a.unsqueeze(2).to_broadcast([P, NT, E])

        @block.gpsimd
        def _(eng):
            eng.memset(tri[:, :, :], 1.0).then_inc(consts, 1)
            eng.wait_ge(consts, 1)
            eng.affine_select(out=tri[:, :, :], in_=tri[:, :, :], compare_op=ALU.is_gt, fill=0.0, base=0,
                              pattern=[[1, E], [-1, E]], channel_multiplier=0).then_inc(consts, 1)

        @block.scalar
        def _(eng):
            eng.wait_ge(shifted, 1)
            eng.activation(ex[:, :, :], ex[:, :, :], ACT.Exp).then_inc(exped, 1)

        @block.vector
        def _(eng):
            c = Count()
            eng.tensor_scalar(p[:, :, :], lg, 50.0, -50.0,
                              ALU.min, ALU.max).then_inc(vseq, c.inc())
            eng.wait_ge(vseq, c.now)
            eng.tensor_reduce(m1[:, :], p[:, :, :], AX.X, ALU.max).then_inc(vseq, c.inc())
            eng.wait_ge(vseq, c.now)
            eng.tensor_tensor(ex[:, :, :], p[:, :, :], bc(m1[:, :]), ALU.subtract).then_inc(shifted, 1)
            eng.wait_ge(consts, 2)
            chosen(eng, vseq, c, p[:, :, :], E, tri[:, :, :], g1[:, :, :, :], eq[:, :, :, :], rank[:, :, :])
            eng.wait_ge(exped, 1)
            eng.wait_ge(vseq, c.now)
            eng.scalar_tensor_tensor(out=p[:, :, :], in0=rank[:, :, :], scalar=1.5, in1=ex[:, :, :],
                                     op0=ALU.is_lt, op1=ALU.mult).then_inc(vseq, c.inc())
            eng.wait_ge(vseq, c.now)
            eng.tensor_reduce(s1[:, :], p[:, :, :], AX.X, ALU.add).then_inc(vseq, c.inc())
            eng.wait_ge(vseq, c.now)
            eng.reciprocal(m1[:, :], s1[:, :]).then_inc(vseq, c.inc())
            eng.wait_ge(vseq, c.now)
            eng.tensor_scalar(m1[:, :], m1[:, :], core.gates[:, 3:4], None, ALU.mult).then_inc(vseq, c.inc())
            eng.wait_ge(vseq, c.now)
            eng.tensor_tensor(gt[:, :, :], p[:, :, :], bc(m1[:, :]), ALU.mult)


def masked_ffn(nc, core, gate_w, W, table, out):
    E = gate_w.shape[0]
    with ExitStack() as ctx:
        sb = lambda n, shape, dt=F32: ctx.enter_context(nc.sbuf_tensor("d_" + n, shape, dt))
        sem = semaphores(nc, ctx, "d_")
        xT = [sb(f"xT{i}", [P, KD, T], F32R) for i in range(2)]
        gt = sb("gt", [P, NT, E])
        M = sb("M", [P, KD, D, E])
        WT = sb("WT", [P, KD, D])
        M_in = [sem(f"M_in{k}") for k in range(KD)]
        w_in, w_turned = sem("w_in"), sem("w_turned")
        c3 = ExitStack()
        Wraw = c3.enter_context(nc.sbuf_tensor("d_Wraw", [P, KD, D], F32))

        def load_matrices(eng):
            eng.dma_start(Wraw[:, :, :], W.rearrange("(r p) c -> p r c", p=P)).then_inc(w_in, 16)
            for k in range(KD):
                eng.dma_start(M[:, k].rearrange("p r e -> p (r e)"),
                              table[k * P * D:(k + 1) * P * D, :].rearrange("(p r) e -> p (r e)", p=P))\
                   .then_inc(M_in[k], 16)

        with nc.sbuf_tensor("d_logits", [P, NT, E], F32) as logits:
            turned_tokens(nc, core, "dt_", xT, gate_w, E, logits[:, :, :], load_matrices)
            masked_router(nc, core, logits[:, :, :], E, gt)
        with c3:
            wb = [c3.enter_context(nc.psum_tensor(f"d_wb{i}", [P, D], F32)) for i in range(KD)]
            block = c3.enter_context(nc.Block())

            @block.tensor
            def _(eng):
                eng.wait_ge(w_in, 16)
                for k in range(KD):
                    for r in range(KD):
                        m = eng.transpose(wb[k][:, r * P:(r + 1) * P], Wraw[:, r, k * P:(k + 1) * P], core.ident[:, :])
                    m.then_inc(w_turned, 1)

            @block.scalar
            def _(eng):
                for k in range(KD):
                    eng.wait_ge(w_turned, k + 1)
                    eng.activation(WT[:, k, :], wb[k][:, :], ACT.Copy)

        mh = [sb(f"mh{i}", [P, KD, D], F32R) for i in range(2)]
        ml = [sb(f"ml{i}", [P, KD, D], F32R) for i in range(2)]
        gb = sb("gb", [P, 2, NT])
        NBANK = 8
        Y = [ctx.enter_context(nc.psum_tensor(f"d_Y{i}", [P, D], F32)) for i in range(NBANK)]
        stored = sem("stored")
        summed, m_hi, m_lo, y_done, y_free, g_ready = [
            sem(n) for n in ("summed", "m_hi", "m_lo", "y_done", "y_free", "g_ready")]
        block = ctx.enter_context(nc.Block())
        of = out.rearrange("b (t p) d -> p (b t) d", p=P)

        @block.sync
        def _(eng):
            for q in range(4):
                eng.wait_ge(y_free, NBANK + NT * (E - 1) + 4 * (q + 1))
                eng.dma_start(of[:, 4 * q:4 * q + 4, :], core.X[:, 4 * q:4 * q + 4, :]).then_inc(stored, 16)
            eng.wait_ge(stored, 64)

        @block.vector
        def _(eng):
            eng.sem_inc(y_free, NBANK)

            def prepare(e, s, first):
                mv = M[:, :, :, bass.ds(e, 1)].rearrange("p k r o -> p k (r o)")
                if not first:
                    eng.wait_ge(m_lo, e)
                eng.tensor_tensor(mv, mv, WT[:, :, :], ALU.add).then_inc(summed, 1)
                if not first:
                    eng.wait_ge(y_free, NBANK + NT * (e - 1))
                eng.tensor_copy(gb[:, s, :], gt[:, :, bass.ds(e, 1)].rearrange("p t o -> p (t o)")).then_inc(g_ready, 1)
                eng.wait_ge(m_hi, e + 1)
                eng.tensor_tensor(ml[s][:, :, :], mv, r32(mh[s][:, :, :]), ALU.subtract).then_inc(m_lo, 1)

            def add(e, s, t):
                eng.wait_ge(y_done, NT * e + t + 1)
                eng.scalar_tensor_tensor(out=core.X[:, t, :], in0=Y[t % NBANK][:, :], scalar=gb[:, s, t:t + 1],
                                         in1=core.X[:, t, :], op0=ALU.mult, op1=ALU.add).then_inc(y_free, 1)

            def expert(e, s, last=False):
                eng.wait_ge(g_ready, e + 1)
                for t in range(NT):
                    add(e, s, t)
                    if t == 3 and not last:
                        prepare(e + 1, 1 - s, False)

            for k in range(KD):
                eng.wait_ge(M_in[k], 16)
            prepare(0, 0, True)
            with eng.Fori(0, E // 2 - 1) as it:
                for s in range(2):
                    expert(2 * it + s, s)
            expert(E - 2, 0)
            expert(E - 1, 1, last=True)

        @block.scalar
        def _(eng):
            def high(e, s):
                eng.wait_ge(summed, e + 1)
                mv = M[:, :, :, bass.ds(e, 1)].rearrange("p k r o -> p k (r o)")
                if not isinstance(e, int) or e >= 2:
                    eng.wait_ge(y_done, NT * (e - 1))
                eng.activation(mh[s][:, :, :], mv, ACT.Copy).then_inc(m_hi, 1)

            high(0, 0)
            high(1, 1)
            with eng.Fori(1, E // 2) as it:
                for s in range(2):
                    high(2 * it + s, s)

        @block.tensor
        def _(eng):
            def expert(e, s):
                eng.wait_ge(m_lo, e + 1)
                for t in range(NT):
                    eng.wait_ge(y_free, NT * e + t + 1)
                    i = 0
                    for x_, w_ in ((0, mh[s]), (0, ml[s]), (1, mh[s])):
                        for k in range(KD):
                            m = eng.matmul(Y[t % NBANK][:, :], xT[x_][:, k, t * P:(t + 1) * P], w_[:, k, :],
                                           start=(i == 0), stop=(i == 3 * KD - 1))
                            i += 1
                    m.then_inc(y_done, 1)

            with eng.Fori(0, E // 2) as it:
                for s in range(2):
                    expert(2 * it + s, s)


def program(nc, x, ctx_1024, fside_BxSx2_0, g_xattn, g_ffn, *args):
    attn0, ffn0, attn1, ffn1, out = args[0:4], args[4:11], args[11:27], args[27:33], args[33]
    gate_w, W, atoms, atom_weights, importance, mask_idx = ffn1
    core = Core()
    table = nc.dram_tensor("table", [D * D + mask_idx.shape[0], atom_weights.shape[0]], F32, kind="Internal").ap()
    with ExitStack() as ctx:
        core.X = ctx.enter_context(nc.sbuf_tensor("X", [P, NT, D], F32))
        core.ident = ctx.enter_context(nc.sbuf_tensor("ident", [P, P], F32))
        core.gates = ctx.enter_context(nc.sbuf_tensor("gates", [P, 4], F32))
        setup(nc, core, g_xattn, g_ffn)
        with ExitStack() as c2:
            places = mask_idx.shape[0] // P
            core.place_sums = c2.enter_context(nc.sbuf_tensor("place_sums", [P, places, atom_weights.shape[0]], F32))
            core.place_rows = c2.enter_context(nc.sbuf_tensor("place_rows", [P, places], U32))
            scattered = semaphores(nc, c2, "")("scattered")
            scatter_tables(nc, core, x, atoms, atom_weights, importance, mask_idx, table)
            rope_attention(nc, core, ctx_1024, fside_BxSx2_0, *attn0, core.gates[:, 0:1],
                           lambda eng: send_tables(eng, core, table, scattered))
        expert_ffn(nc, core, *ffn0, core.gates[:, 2:3])
        normed_attention(nc, core, ctx_1024, *attn1, core.gates[:, 1:2])
        masked_ffn(nc, core, gate_w, W, table, out)


_INS = ["x", "ctx_1024", "fside_BxSx2_0", "g_xattn", "g_ffn"] \
    + ["L0_xattn_" + n for n in ("Wq", "Wkv", "Wout", "bout")] \
    + ["L0_ffn_" + n for n in ("w_gate", "wg", "wu", "wd", "sg", "su", "sd")] \
    + ["L1_xattn_" + n for n in ("Wq", "bq", "Wk", "bk", "Wv", "bv", "Wkv_dca", "bkv_dca", "qn_w", "qn_b", "kn_w", "kn_b",
                                 "kn_dca_w", "kn_dca_b", "Wo", "bo")] \
    + ["L1_ffn_" + n for n in ("gate_w", "W", "atoms", "expert_atom_weights", "importance", "mask_idx")]


def kernel(**inputs):
    import concourse.bacc as _bacc
    from concourse.bass_utils import run_bass_kernel_spmd as _run

    nc = _bacc.Bacc("TRN2", target_bir_lowering=False, num_devices=1)
    arrays, args = {}, []
    for name in _INS:
        a = np.ascontiguousarray(inputs[name])
        arrays[f"in_{name}"] = a
        args.append(nc.dram_tensor(f"in_{name}", a.shape, mybir.dt.from_np(a.dtype), kind="ExternalInput").ap())
    out = nc.dram_tensor("out", (B, S, D), F32, kind="ExternalOutput").ap()
    program(nc, *args, out)
    r = _run(nc, [arrays], core_ids=[0])
    return r.results[0]["out"]
```
